# Optimizing a Trainium2 kernel written in Bass

```python
import numpy as np
import jax
import jax.numpy as jnp

def _softmax(x, axis=-1):
    return jax.nn.softmax(x, axis=axis)

def _gelu(x):
    return jax.nn.gelu(x, approximate=True)

def _silu(x):
    return jax.nn.silu(x)

def _sigmoid(x):
    return jax.nn.sigmoid(x)

def _layernorm(x, axis=-1, eps=1e-05):
    m = jnp.mean(x, axis=axis, keepdims=True)
    v = jnp.var(x, axis=axis, keepdims=True)
    return (x - m) / jnp.sqrt(v + eps)

def _scatter_add(tgt, idx, src, axis=0):
    return tgt.at[idx].add(src)

def _segment_sum(src, seg, n):
    return jax.ops.segment_sum(src, seg, n)
kernel_name = 'mk_hybrid_d2_jaxref_r8_0fa824'

def setup_inputs(seed: int=0):
    np.random.seed(seed)
    _w = jnp.asarray

    def _L0_attn_a_setup():
        import jax, jax.numpy as jnp
        import numpy as np
        EMBED_DIM = 128
        HEADS = 16
        HEAD_DIM = EMBED_DIM // HEADS
        key = jax.random.key(seed)
        ks = jax.random.split(key, 9)
        B, T, C = (4, 512, EMBED_DIM)
        s = 1.0 / np.sqrt(C)
        inp = {'x': jax.random.normal(ks[0], (B, T, C), dtype=jnp.float32), 'Wq': jax.random.normal(ks[1], (C, C), dtype=jnp.float32) * s, 'bq': jnp.zeros((C,), dtype=jnp.float32), 'Wk': jax.random.normal(ks[2], (C, C), dtype=jnp.float32) * s, 'bk': jnp.zeros((C,), dtype=jnp.float32), 'Wv': jax.random.normal(ks[3], (C, C), dtype=jnp.float32) * s, 'bv': jnp.zeros((C,), dtype=jnp.float32), 'Wc': jax.random.normal(ks[4], (C, C), dtype=jnp.float32) * s, 'bc': jnp.zeros((C,), dtype=jnp.float32)}
        return inp
    _L0_attn_a_in = _L0_attn_a_setup()

    def _L0_attn_b_setup():
        import jax, jax.numpy as jnp
        import numpy as np
        HIDDEN = 128
        HEADS = 16
        HEAD_DIM = HIDDEN // HEADS
        SCALE = HEAD_DIM ** (-0.5)
        key = jax.random.key(seed)
        ks = jax.random.split(key, 9)
        init = 1.0 / np.sqrt(HIDDEN)
        hidden_states = jax.random.normal(ks[0], (8, 128, HIDDEN), dtype=jnp.float32)

        def lin(k):
            kw, kb = jax.random.split(k)
            W = jax.random.uniform(kw, (HIDDEN, HIDDEN), jnp.float32, -init, init)
            b = jax.random.uniform(kb, (HIDDEN,), jnp.float32, -init, init)
            return (W, b)
        Wq, bq = lin(ks[1])
        Wk, bk = lin(ks[2])
        Wv, bv = lin(ks[3])
        Wo, bo = lin(ks[4])
        return {'hidden_states': hidden_states, 'Wq': Wq, 'bq': bq, 'Wk': Wk, 'bk': bk, 'Wv': Wv, 'bv': bv, 'Wo': Wo, 'bo': bo}
    _L0_attn_b_in = _L0_attn_b_setup()

    def _L0_ffn_setup():
        import math
        import jax, jax.numpy as jnp
        import numpy as np
        D_MODEL = 128
        D_HIDDEN = 256
        N_EXPERTS = 8
        TOP_K = 2
        CAPACITY_FACTOR = 1.25

        def _moe_forward(x, w_router, w_gate, w_down):
            B, T, D = x.shape
            N = B * T
            xf = x.reshape(N, D)
            logits = xf.astype(jnp.float32) @ w_router.T
            gates = jax.nn.softmax(logits, axis=-1)
            topk_gates, topk_idx = jax.lax.top_k(gates, TOP_K)
            expert_mask = jax.nn.one_hot(topk_idx, N_EXPERTS, dtype=jnp.int32).sum(axis=1)
            capacity = math.ceil(N / N_EXPERTS * CAPACITY_FACTOR)
            position_in_expert = jnp.cumsum(expert_mask, axis=0) - 1
            expert_mask = expert_mask * (position_in_expert < capacity)
            keep = jnp.take_along_axis(expert_mask, topk_idx, axis=1) > 0
            topk_gates = topk_gates * keep
            topk_gates = topk_gates / (topk_gates.sum(axis=-1, keepdims=True) + 1e-06)
            hidden = jax.nn.silu(xf @ w_gate.T)
            combine = (topk_gates[:, :, None] * jax.nn.one_hot(topk_idx, N_EXPERTS, dtype=topk_gates.dtype)).sum(axis=1)
            y = jnp.zeros((N, D), dtype=x.dtype)
            for e in range(N_EXPERTS):
                y = y + combine[:, e:e + 1] * (hidden @ w_down[e].T)
            return y.reshape(B, T, D)
        key = jax.random.key(seed)
        k0, k1, k2, k3 = jax.random.split(key, 4)
        B, T = (2, 256)
        x = jax.random.normal(k0, (B, T, D_MODEL), dtype=jnp.float32)
        w_router = jax.random.normal(k1, (N_EXPERTS, D_MODEL), dtype=jnp.float32) * 0.02
        w_gate = jax.random.normal(k2, (D_HIDDEN, D_MODEL), dtype=jnp.float32) * 0.02
        w_down = jax.random.normal(k3, (N_EXPERTS, D_MODEL, D_HIDDEN), dtype=jnp.float32) * 0.02
        return {'x': x, 'w_router': w_router, 'w_gate': w_gate, 'w_down': w_down}
    _L0_ffn_in = _L0_ffn_setup()

    def _L1_attn_a_setup():
        import jax, jax.numpy as jnp
        import numpy as np
        N_EMBD = 128
        N_HEAD = 16
        LATENT = 64
        HEAD_DIM = N_EMBD // N_HEAD
        B, T = (2, 256)
        SCALE = 1.0 / np.sqrt(LATENT)
        key = jax.random.key(seed)
        ks = jax.random.split(key, 10)
        s = lambda fan_in: 1.0 / np.sqrt(fan_in)
        return {'x': jax.random.normal(ks[0], (B, T, N_EMBD), dtype=jnp.float32), 'Wq': jax.random.normal(ks[1], (N_EMBD, N_EMBD), dtype=jnp.float32) * s(N_EMBD), 'bq': jnp.zeros((N_EMBD,), dtype=jnp.float32), 'Wk': jax.random.normal(ks[2], (N_EMBD, N_HEAD * LATENT), dtype=jnp.float32) * s(N_EMBD), 'bk': jnp.zeros((N_HEAD * LATENT,), dtype=jnp.float32), 'Wv': jax.random.normal(ks[3], (N_EMBD, N_HEAD * LATENT), dtype=jnp.float32) * s(N_EMBD), 'bv': jnp.zeros((N_HEAD * LATENT,), dtype=jnp.float32), 'Wo': jax.random.normal(ks[4], (N_HEAD * LATENT, N_EMBD), dtype=jnp.float32) * s(N_HEAD * LATENT), 'bo': jnp.zeros((N_EMBD,), dtype=jnp.float32), 'Wc': jax.random.normal(ks[5], (HEAD_DIM, LATENT), dtype=jnp.float32) * s(HEAD_DIM)}
    _L1_attn_a_in = _L1_attn_a_setup()

    def _L1_attn_b_setup():
        import math
        import jax, jax.numpy as jnp
        import numpy as np
        N_HEADS = 16
        D_EMBED = 128
        key = jax.random.key(seed)
        ks = jax.random.split(key, 5)
        b, l, d = (2, 256, D_EMBED)
        return {'x': jax.random.normal(ks[0], (b, l, d), dtype=jnp.float32), 'w_in': jax.random.normal(ks[1], (3 * d, d), dtype=jnp.float32) * 0.02, 'b_in': jax.random.normal(ks[2], (3 * d,), dtype=jnp.float32) * 0.02, 'w_out': jax.random.normal(ks[3], (d, d), dtype=jnp.float32) * 0.02, 'b_out': jax.random.normal(ks[4], (d,), dtype=jnp.float32) * 0.02}
    _L1_attn_b_in = _L1_attn_b_setup()

    def _L1_ffn_setup():
        import jax, jax.numpy as jnp
        import numpy as np
        B, S, D, F, E = (4, 256, 128, 512, 8)
        LN_EPS = 1e-05
        key = jax.random.key(seed)
        ks = jax.random.split(key, 6)
        sc = 0.02
        return {'x': jax.random.normal(ks[0], (B, S, D), dtype=jnp.float32), 'Wr': jax.random.normal(ks[1], (D, E), dtype=jnp.float32) * sc, 'br': jnp.zeros((E,), jnp.float32), 'ln_g': jnp.ones((D,), jnp.float32), 'ln_b': jnp.zeros((D,), jnp.float32), 'W1': jax.random.normal(ks[2], (E, D, F), dtype=jnp.float32) * sc, 'b1': jnp.zeros((E, F), jnp.float32), 'W2': jax.random.normal(ks[3], (E, F, D), dtype=jnp.float32) * sc, 'b2': jnp.zeros((E, D), jnp.float32)}
    _L1_ffn_in = _L1_ffn_setup()
    _d = {'L0_attn_a_x': _L0_attn_a_in['x'], 'L0_attn_a_Wq': _L0_attn_a_in['Wq'], 'L0_attn_a_bq': _L0_attn_a_in['bq'], 'L0_attn_a_Wk': _L0_attn_a_in['Wk'], 'L0_attn_a_bk': _L0_attn_a_in['bk'], 'L0_attn_a_Wv': _L0_attn_a_in['Wv'], 'L0_attn_a_bv': _L0_attn_a_in['bv'], 'L0_attn_a_Wc': _L0_attn_a_in['Wc'], 'L0_attn_a_bc': _L0_attn_a_in['bc'], 'L0_attn_b_Wq': _L0_attn_b_in['Wq'], 'L0_attn_b_bq': _L0_attn_b_in['bq'], 'L0_attn_b_Wk': _L0_attn_b_in['Wk'], 'L0_attn_b_bk': _L0_attn_b_in['bk'], 'L0_attn_b_Wv': _L0_attn_b_in['Wv'], 'L0_attn_b_bv': _L0_attn_b_in['bv'], 'L0_attn_b_Wo': _L0_attn_b_in['Wo'], 'L0_attn_b_bo': _L0_attn_b_in['bo'], 'L0_ffn_w_router': _L0_ffn_in['w_router'], 'L0_ffn_w_gate': _L0_ffn_in['w_gate'], 'L0_ffn_w_down': _L0_ffn_in['w_down'], 'L1_attn_a_Wq': _L1_attn_a_in['Wq'], 'L1_attn_a_bq': _L1_attn_a_in['bq'], 'L1_attn_a_Wk': _L1_attn_a_in['Wk'], 'L1_attn_a_bk': _L1_attn_a_in['bk'], 'L1_attn_a_Wv': _L1_attn_a_in['Wv'], 'L1_attn_a_bv': _L1_attn_a_in['bv'], 'L1_attn_a_Wo': _L1_attn_a_in['Wo'], 'L1_attn_a_bo': _L1_attn_a_in['bo'], 'L1_attn_a_Wc': _L1_attn_a_in['Wc'], 'L1_attn_b_w_in': _L1_attn_b_in['w_in'], 'L1_attn_b_b_in': _L1_attn_b_in['b_in'], 'L1_attn_b_w_out': _L1_attn_b_in['w_out'], 'L1_attn_b_b_out': _L1_attn_b_in['b_out'], 'L1_ffn_Wr': _L1_ffn_in['Wr'], 'L1_ffn_br': _L1_ffn_in['br'], 'L1_ffn_ln_g': _L1_ffn_in['ln_g'], 'L1_ffn_ln_b': _L1_ffn_in['ln_b'], 'L1_ffn_W1': _L1_ffn_in['W1'], 'L1_ffn_b1': _L1_ffn_in['b1'], 'L1_ffn_W2': _L1_ffn_in['W2'], 'L1_ffn_b2': _L1_ffn_in['b2']}
    _x0 = _d['L0_attn_a_x']
    _d['L0_attn_a_x'] = jax.random.normal(jax.random.fold_in(jax.random.key(seed), 1), (4, 1024, 128), dtype=_x0.dtype)
    del _x0
    return _d

def reference(L0_attn_a_x, L0_attn_a_Wq, L0_attn_a_bq, L0_attn_a_Wk, L0_attn_a_bk, L0_attn_a_Wv, L0_attn_a_bv, L0_attn_a_Wc, L0_attn_a_bc, L0_attn_b_Wq, L0_attn_b_bq, L0_attn_b_Wk, L0_attn_b_bk, L0_attn_b_Wv, L0_attn_b_bv, L0_attn_b_Wo, L0_attn_b_bo, L0_ffn_w_router, L0_ffn_w_gate, L0_ffn_w_down, L1_attn_a_Wq, L1_attn_a_bq, L1_attn_a_Wk, L1_attn_a_bk, L1_attn_a_Wv, L1_attn_a_bv, L1_attn_a_Wo, L1_attn_a_bo, L1_attn_a_Wc, L1_attn_b_w_in, L1_attn_b_b_in, L1_attn_b_w_out, L1_attn_b_b_out, L1_ffn_Wr, L1_ffn_br, L1_ffn_ln_g, L1_ffn_ln_b, L1_ffn_W1, L1_ffn_b1, L1_ffn_W2, L1_ffn_b2):

    def _L0_attn_a_ref(x, Wq, bq, Wk, bk, Wv, bv, Wc, bc):
        import jax, jax.numpy as jnp
        import numpy as np
        EMBED_DIM = 128
        HEADS = 16
        HEAD_DIM = EMBED_DIM // HEADS
        B, T, C = x.shape
        H, D = (HEADS, HEAD_DIM)
        q = (x @ Wq.T + bq).reshape(B, T, H, D).transpose(0, 2, 1, 3)
        k = (x @ Wk.T + bk).reshape(B, T, H, D).transpose(0, 2, 1, 3)
        v = (x @ Wv.T + bv).reshape(B, T, H, D).transpose(0, 2, 1, 3)
        q = jax.nn.elu(q) + 1.0
        k = jax.nn.elu(k) + 1.0
        kv = jnp.einsum('bhtd,bhte->bhde', k, v)
        k_sum = k.sum(axis=2)
        z = 1.0 / (jnp.einsum('bhtd,bhd->bht', q, k_sum)[..., None] + 1e-06)
        y = jnp.einsum('bhtd,bhde->bhte', q, kv) * z
        y = y.transpose(0, 2, 1, 3).reshape(B, T, C)
        return y @ Wc.T + bc

    def _L0_attn_b_ref(hidden_states, Wq, bq, Wk, bk, Wv, bv, Wo, bo):
        import jax, jax.numpy as jnp
        import numpy as np
        HIDDEN = 128
        HEADS = 16
        HEAD_DIM = HIDDEN // HEADS
        SCALE = HEAD_DIM ** (-0.5)
        b, s, d = hidden_states.shape
        q = (hidden_states @ Wq.T + bq).reshape(b, s, HEADS, HEAD_DIM)
        k = (hidden_states @ Wk.T + bk).reshape(b, s, HEADS, HEAD_DIM)
        v = (hidden_states @ Wv.T + bv).reshape(b, s, HEADS, HEAD_DIM)
        q = q * SCALE
        scores = jnp.einsum('bqhd,bkhd->bhqk', q, k)
        probs = jax.nn.softmax(scores.astype(jnp.float32), axis=-1).astype(scores.dtype)
        out = jnp.einsum('bhqk,bkhd->bqhd', probs, v).reshape(b, s, d)
        return out @ Wo.T + bo

    def _L0_ffn_ref(x, w_router, w_gate, w_down):
        import math
        import jax, jax.numpy as jnp
        import numpy as np
        D_MODEL = 128
        D_HIDDEN = 256
        N_EXPERTS = 8
        TOP_K = 2
        CAPACITY_FACTOR = 1.25

        def _moe_forward(x, w_router, w_gate, w_down):
            B, T, D = x.shape
            N = B * T
            xf = x.reshape(N, D)
            logits = xf.astype(jnp.float32) @ w_router.T
            gates = jax.nn.softmax(logits, axis=-1)
            topk_gates, topk_idx = jax.lax.top_k(gates, TOP_K)
            expert_mask = jax.nn.one_hot(topk_idx, N_EXPERTS, dtype=jnp.int32).sum(axis=1)
            capacity = math.ceil(N / N_EXPERTS * CAPACITY_FACTOR)
            position_in_expert = jnp.cumsum(expert_mask, axis=0) - 1
            expert_mask = expert_mask * (position_in_expert < capacity)
            keep = jnp.take_along_axis(expert_mask, topk_idx, axis=1) > 0
            topk_gates = topk_gates * keep
            topk_gates = topk_gates / (topk_gates.sum(axis=-1, keepdims=True) + 1e-06)
            hidden = jax.nn.silu(xf @ w_gate.T)
            combine = (topk_gates[:, :, None] * jax.nn.one_hot(topk_idx, N_EXPERTS, dtype=topk_gates.dtype)).sum(axis=1)
            y = jnp.zeros((N, D), dtype=x.dtype)
            for e in range(N_EXPERTS):
                y = y + combine[:, e:e + 1] * (hidden @ w_down[e].T)
            return y.reshape(B, T, D)
        return _moe_forward(x, w_router, w_gate, w_down)

    def _L1_attn_a_ref(x, Wq, bq, Wk, bk, Wv, bv, Wo, bo, Wc):
        import jax, jax.numpy as jnp
        import numpy as np
        N_EMBD = 128
        N_HEAD = 16
        LATENT = 64
        HEAD_DIM = N_EMBD // N_HEAD
        B, T = (2, 256)
        SCALE = 1.0 / np.sqrt(LATENT)
        Bv, Tv, C = x.shape
        q = (x @ Wq + bq).reshape(Bv, Tv, N_HEAD, HEAD_DIM)
        k = (x @ Wk + bk).reshape(Bv, Tv, N_HEAD, LATENT)
        v = (x @ Wv + bv).reshape(Bv, Tv, N_HEAD, LATENT)
        qc = jnp.einsum('bthd,dl->bthl', q, Wc)
        att = jnp.einsum('bthl,bshl->bhts', qc, k) * SCALE
        causal = jnp.tril(jnp.ones((Tv, Tv), dtype=bool))
        att = jnp.where(causal[None, None], att, -jnp.inf)
        att = jax.nn.softmax(att, axis=-1)
        y = jnp.einsum('bhts,bshl->bthl', att, v).reshape(Bv, Tv, N_HEAD * LATENT)
        return y @ Wo + bo

    def _L1_attn_b_ref(x, w_in, b_in, w_out, b_out):
        import math
        import jax, jax.numpy as jnp
        import numpy as np
        N_HEADS = 16
        D_EMBED = 128
        b, l, d = x.shape
        h = N_HEADS
        scale = 1.0 / math.sqrt(d // h)
        x_proj = (x @ w_in.T + b_in).reshape(b, l, h, -1)
        q, k, v = jnp.split(x_proj, 3, axis=-1)
        att = jnp.einsum('blhd,bmhd->blmh', q, k) * scale
        att = jax.nn.softmax(att, axis=2)
        opt = jnp.einsum('blmh,blhd->blhd', att, v).reshape(b, l, d)
        return opt @ w_out.T + b_out

    def _L1_ffn_ref(x, Wr, br, ln_g, ln_b, W1, b1, W2, b2):
        import jax, jax.numpy as jnp
        import numpy as np
        B, S, D, F, E = (4, 256, 128, 512, 8)
        LN_EPS = 1e-05
        tokens_shape = x.shape[:-1]
        xt = x.reshape(-1, x.shape[-1])
        router_logits = xt @ Wr + br
        router_probs = jax.nn.softmax(router_logits, axis=-1)
        gates = jnp.max(router_probs, axis=-1, keepdims=True)
        idx = jnp.argmax(router_probs, axis=-1)
        onehot = jax.nn.one_hot(idx, E, dtype=xt.dtype)
        mu = jnp.mean(xt, axis=-1, keepdims=True)
        var = jnp.mean(jnp.square(xt - mu), axis=-1, keepdims=True)
        xn = (xt - mu) * jax.lax.rsqrt(var + LN_EPS) * ln_g + ln_b
        h = jnp.einsum('te,td,edf->tf', onehot, xn, W1) + b1[idx]
        h = jax.nn.relu(h)
        y = jnp.einsum('te,tf,efd->td', onehot, h, W2) + b2[idx]
        y = y * gates
        return y.reshape(tokens_shape + (y.shape[-1],))
    x = L0_attn_a_x
    x = x + _L0_attn_a_ref(_layernorm(x, axis=-1), L0_attn_a_Wq, L0_attn_a_bq, L0_attn_a_Wk, L0_attn_a_bk, L0_attn_a_Wv, L0_attn_a_bv, L0_attn_a_Wc, L0_attn_a_bc)
    x = x + _L0_ffn_ref(_layernorm(x, axis=-1), L0_ffn_w_router, L0_ffn_w_gate, L0_ffn_w_down)
    x = x + _L0_attn_b_ref(_layernorm(x, axis=-1), L0_attn_b_Wq, L0_attn_b_bq, L0_attn_b_Wk, L0_attn_b_bk, L0_attn_b_Wv, L0_attn_b_bv, L0_attn_b_Wo, L0_attn_b_bo)
    x = x + _L0_ffn_ref(_layernorm(x, axis=-1), L0_ffn_w_router, L0_ffn_w_gate, L0_ffn_w_down)
    x = x + _L1_attn_a_ref(_layernorm(x, axis=-1), L1_attn_a_Wq, L1_attn_a_bq, L1_attn_a_Wk, L1_attn_a_bk, L1_attn_a_Wv, L1_attn_a_bv, L1_attn_a_Wo, L1_attn_a_bo, L1_attn_a_Wc)
    x = x + _L1_ffn_ref(_layernorm(x, axis=-1), L1_ffn_Wr, L1_ffn_br, L1_ffn_ln_g, L1_ffn_ln_b, L1_ffn_W1, L1_ffn_b1, L1_ffn_W2, L1_ffn_b2)
    x = x + _L1_attn_b_ref(_layernorm(x, axis=-1), L1_attn_b_w_in, L1_attn_b_b_in, L1_attn_b_w_out, L1_attn_b_b_out)
    x = x + _L1_ffn_ref(_layernorm(x, axis=-1), L1_ffn_Wr, L1_ffn_br, L1_ffn_ln_g, L1_ffn_ln_b, L1_ffn_W1, L1_ffn_b1, L1_ffn_W2, L1_ffn_b2)
    return x

_drawn_inputs = setup_inputs


def setup_inputs(seed=0):
    import zlib

    import numpy as np

    out = dict(_drawn_inputs(seed))
    spreads = {'L0_attn_a_bq': (0.0, 2.0),
     'L0_attn_a_bk': (0.0, 2.0),
     'L0_attn_a_bv': (0.0, 0.1),
     'L0_attn_a_bc': (0.0, 0.1),
     'L1_attn_a_bq': (0.0, 0.606),
     'L1_attn_a_bk': (0.0, 2.0),
     'L1_attn_a_bv': (0.0, 0.1),
     'L1_attn_a_bo': (0.0, 0.1),
     'L1_ffn_br': (0.0, 0.268),
     'L1_ffn_ln_g': (1.0, 0.6),
     'L1_ffn_ln_b': (0.0, 0.8),
     'L1_ffn_b1': (0.0, 0.765),
     'L1_ffn_b2': (0.0, 0.1)}
    factors = {'L0_attn_a_Wq': 3.708,
     'L0_attn_b_Wq': 5.138,
     'L0_attn_b_bq': 8.0,
     'L0_attn_b_Wk': 5.208,
     'L0_attn_b_bk': 64.0,
     'L1_attn_b_b_in': 8.0,
     'L1_attn_b_b_out': 2.896,
     'L1_ffn_W1': 2.726}
    for name, (base, spread) in spreads.items():
        noise = np.random.default_rng([zlib.crc32(name.encode()), seed]).standard_normal(out[name].shape)
        drawn = base * np.exp(spread * noise) if base else spread * noise
        out[name] = jnp.asarray(drawn.astype(out[name].dtype))
    for name, factor in factors.items():
        out[name] = (out[name] * factor).astype(out[name].dtype)
    return out
```

```python
import concourse.bass as bass
from concourse import mybir
from contextlib import ExitStack

F32 = mybir.dt.float32
BF16 = mybir.dt.bfloat16
I32 = mybir.dt.int32
ALU = mybir.AluOpType
ACT = mybir.ActivationFunctionType
AX = mybir.AxisListType

P = 128
BATCH, SEQ, D = 4, 1024, 128
TOK = BATCH * SEQ
TILES = TOK // P
GROUP = 512
GROUPS = TOK // GROUP
GT = GROUP // P
PAIRS = GROUPS // 2
H, HD = 16, 8
E = 8
EPS = 1e-5


class Chain:

    def __init__(self, eng, sem, turn=0, per_turn=0, before=0):
        self.eng, self.sem, self.turn, self.per_turn, self.before, self.n = eng, sem, turn, per_turn, before, 0

    def run(self, op):
        self.n += 1
        op.then_inc(self.sem, 1)
        self.eng.wait_ge(self.sem, self.turn * self.per_turn + self.before + self.n)

    def end(self):
        assert self.per_turn == 0 or self.n == self.per_turn, self.n


def cols(start, n):
    return bass.ds(start, n)


LEAD = 8


class Steps:

    def __init__(self, sem):
        self.sem = sem

    def open(self, eng):
        eng.sem_inc(self.sem, LEAD)

    def after(self, n):
        return n + (LEAD + 1)

    def wait(self, eng, n):
        eng.wait_ge(self.sem, self.after(n))


class Shared:
    pass


def scope(nc):
    ctx = ExitStack()
    phase = nc.next_id()

    def sb(name, shape, dt=F32):
        return ctx.enter_context(nc.sbuf_tensor(f"{name}_{phase}", shape, dt))

    sems = []

    def close():
        if sems:
            nc.clear_and_free_semaphores(sems)
            nc.all_engine_barrier()

    ctx.callback(close)

    def sem(name):
        sems.append(nc.alloc_semaphore(f"{name}_{phase}"))
        return sems[-1]

    def steps(name):
        return Steps(sem(name))

    return ctx, sb, sem, steps


def load_phase(nc, S, loads):
    ctx, sb, sem, steps = scope(nc)
    with ctx:
        loaded, made, cleared = sem("loaded"), sem("made"), sem("cleared")
        with nc.Block() as block:
            @block.sync
            def _(sp):
                for dst, src in loads:
                    sp.dma_start(dst, src).then_inc(loaded, 16)
                sp.wait_ge(loaded, 16 * len(loads))
                sp.wait_ge(made, 5)
                sp.dma_start(S.x_slots[:, :].rearrange("(t p) d -> p t d", p=P),
                             S.zeros[:].rearrange("p (o d) -> p o d", o=1).broadcast_to([P, SLOT_TILES, D])
                             ).then_inc(cleared, 16)
                sp.wait_ge(cleared, 16)

            @block.gpsimd
            def _(pool):
                c = Chain(pool, made)
                for m in (S.ident, S.ident_b):
                    c.run(nc.gpsimd.memset(m[:], 0.0))
                    c.run(nc.gpsimd.affine_select(out=m[:], in_=m[:], compare_op=ALU.not_equal, fill=1.0, base=0,
                                                  pattern=[[-1, P]], channel_multiplier=1))
                c.run(nc.gpsimd.memset(S.zeros[:], 0.0))
                c.run(nc.gpsimd.memset(S.head_mask[:], 1.0))
                v = S.head_mask[:].rearrange("p (h d) -> p h d", h=H)
                c.run(nc.gpsimd.affine_select(out=v, in_=v, compare_op=ALU.is_ge, fill=0.0, base=0,
                                              pattern=[[-HD, H], [0, HD]], channel_multiplier=1))
                c.run(nc.gpsimd.affine_select(out=v, in_=v, compare_op=ALU.is_ge, fill=0.0, base=HD - 1,
                                              pattern=[[HD, H], [0, HD]], channel_multiplier=-1))
                c.run(nc.gpsimd.memset(S.prefix[:], 1.0))
                c.run(nc.gpsimd.affine_select(out=S.prefix[:], in_=S.prefix[:], compare_op=ALU.is_ge, fill=0.0,
                                              base=0, pattern=[[1, P]], channel_multiplier=-1))
                c.run(nc.gpsimd.memset(S.ones_b[:], 1.0))
                for m, sign in ((S.mask_qk, -1), (S.mask_kq, 1)):
                    c.run(nc.gpsimd.memset(m[:], 0.0))
                    c.run(nc.gpsimd.affine_select(out=m[:], in_=m[:], compare_op=ALU.is_ge, fill=MASKED, base=0,
                                                  pattern=[[sign, P]], channel_multiplier=-sign))
                c.run(nc.gpsimd.iota(S.first_rank[:], pattern=[[0, GT], [-1, E]], base=E, channel_multiplier=0,
                                     allow_small_or_imprecise_dtypes=True))
                c.run(nc.gpsimd.iota(S.tile_start[:], pattern=[[P, S.tile_start.shape[1]]], base=0,
                                     channel_multiplier=0, allow_small_or_imprecise_dtypes=True))


MASKED = -3.0e38


def stats_tail(nc, dve, c, st, tmp, mean, rstd, var_ready, std_ready):
    stv = st[:].rearrange("p (t s) -> p s t", s=6)
    c.run(nc.vector.tensor_tensor(tmp[:, 1], stv[:, 1], stv[:, 4], ALU.subtract))
    nc.vector.tensor_tensor(tmp[:, 2], stv[:, 2], stv[:, 5], ALU.add)
    c.run(nc.vector.tensor_tensor(tmp[:, 0], stv[:, 1], stv[:, 4], ALU.add))
    nc.vector.tensor_scalar(mean[:], tmp[:, 0], 0.5, None, ALU.mult)
    c.run(nc.vector.tensor_tensor(tmp[:, 3], tmp[:, 1], tmp[:, 1], ALU.mult))
    nc.vector.scalar_tensor_tensor(tmp[:, 2], tmp[:, 3], float(D // 4), tmp[:, 2], ALU.mult,
                                   ALU.add).then_inc(var_ready, 1)
    dve.wait_ge(std_ready, 1)
    c.run(nc.vector.reciprocal(rstd[:], tmp[:, 1]))


def norm_stats(nc, S):
    ctx, sb, sem, steps = scope(nc)
    with ctx:
        st = sb("bn", [P, TILES * 6])
        tmp = sb("bn_tmp", [P, 4, TILES])
        bn, chain, var_ready, std_ready = sem("bn"), sem("chain"), sem("var_ready"), sem("std_ready")
        with nc.Block() as block:
            @block.vector
            def _(dve):
                with dve.Fori(0, GROUPS) as g:
                    for k in range(GT):
                        op = nc.vector.bn_stats(st[:, cols((g * GT + k) * 6, 6)], S.x[:, cols((g * GT + k) * P, P)])
                    op.then_inc(bn, 1)
                dve.wait_ge(bn, GROUPS)
                stats_tail(nc, dve, Chain(dve, chain), st, tmp, S.mean, S.rstd, var_ready, std_ready)

            @block.scalar
            def _(act):
                act.wait_ge(var_ready, 1)
                nc.scalar.activation(tmp[:, 1], tmp[:, 2], ACT.Sqrt, bias=S.eps[:], scale=1.0 / D).then_inc(std_ready, 1)


def normalize_tile(nc, S, out, t):
    return nc.vector.tensor_scalar(out, S.x[:, cols(t * P, P)], S.mean[:, cols(t, 1)], S.rstd[:, cols(t, 1)],
                                   ALU.subtract, ALU.mult)


def linear_attention(nc, S):
    ctx, sb, sem, steps = scope(nc)
    ps = S.ps
    VA = 2 * P + 1
    SW = P + H
    with ctx:
        xn = sb("xn", [P, 2, GROUP])
        xT = sb("xT", [P, 2, GROUP])
        qT = sb("qT", [P, 2, GROUP])
        qneg = sb("qneg", [P, 2, GROUP])
        kv = sb("kv", [P, 2, GT, VA])
        kneg = sb("kneg", [P, 2, GT, P])
        ksum = sb("ksum", [P, 1])
        state = sb("state", [P, SW])
        den = sb("den", [P, GT * H])
        y = sb("y", [P, 2, GROUP])
        yT = sb("yT", [P, 2, GROUP])
        chain = sem("chain")
        (normed, transposed, xT_ready, q_mm, q_neg, q_exp, q_ready, kv_mm, kv_biased, k_exp, k_ready, s_mm, s_ready,
         n_mm, y_ready, yT_mm, yT_ready, o_mm, x_ready, x_biased) = [steps(n) for n in (
             "normed transposed xT_ready q_mm q_neg q_exp q_ready kv_mm kv_biased k_exp k_ready s_mm s_ready "
             "n_mm y_ready yT_mm yT_ready o_mm x_ready x_biased").split()]
        T, Q, KV, ST, NUM, YT = 0, 1, (2, 3), 4, (5, 6), 7
        with nc.Block() as block:
            @block.tensor
            def _(pe):
                for s in (transposed, q_mm, kv_mm, s_mm, n_mm, yT_mm, o_mm):
                    s.open(pe)
                with pe.Fori(0, BATCH) as b:
                    for s in (0, 1):
                        g = b * 2 + s
                        normed.wait(pe, g)
                        xT_ready.wait(pe, g - 1)
                        for k in range(GT):
                            op = nc.tensor.transpose(ps[:, T, k * P:(k + 1) * P], xn[:, s, k * P:(k + 1) * P], S.ident[:])
                        op.then_inc(transposed.sem, 1)
                        xT_ready.wait(pe, g)
                        q_ready.wait(pe, g - 1)
                        nc.tensor.matmul(ps[:, Q, :], S.a0_wq[:], xT[:, s, :], start=True, stop=True).then_inc(q_mm.sem, 1)
                        for half in (0, 1):
                            kv_biased.wait(pe, g * 2 + half - 2)
                            for k in (0, 1):
                                op = nc.tensor.matmul(ps[:, KV[half], k * 2 * P:(k + 1) * 2 * P],
                                                      xT[:, s, (2 * half + k) * P:(2 * half + k + 1) * P],
                                                      S.a0_wkv[:], start=True, stop=True)
                            op.then_inc(kv_mm.sem, 1)
                    x_ready.wait(pe, b * 2 - 1)
                    for s in (0, 1):
                        k_ready.wait(pe, b * 2 + s)
                        for k in range(GT):
                            op = nc.tensor.matmul(ps[:, ST, 0:P + 1], kv[:, s, k, 0:P], kv[:, s, k, P:VA],
                                                  start=(s == 0 and k == 0), stop=(s == 1 and k == GT - 1))
                    op.then_inc(s_mm.sem, 1)
                    s_ready.wait(pe, b)
                    for s in (0, 1):
                        g = b * 2 + s
                        q_ready.wait(pe, g)
                        for half in (0, 1):
                            y_ready.wait(pe, g * 2 + half - 2)
                            for k in (0, 1):
                                op = nc.tensor.matmul(ps[:, NUM[half], k * SW:(k + 1) * SW],
                                                      qT[:, s, (2 * half + k) * P:(2 * half + k + 1) * P],
                                                      state[:], start=True, stop=True)
                            op.then_inc(n_mm.sem, 1)
                    for s in (0, 1):
                        g = b * 2 + s
                        y_ready.wait(pe, g * 2 + 1)
                        yT_ready.wait(pe, g - 1)
                        for k in range(GT):
                            op = nc.tensor.transpose(ps[:, YT, k * P:(k + 1) * P], y[:, s, k * P:(k + 1) * P], S.ident[:])
                        op.then_inc(yT_mm.sem, 1)
                        yT_ready.wait(pe, g)
                        x_ready.wait(pe, g - 1)
                        for k in range(GT):
                            op = nc.tensor.matmul(ps[:, ST, k * P:(k + 1) * P], yT[:, s, k * P:(k + 1) * P],
                                                  S.a0_wc[:], start=True, stop=True)
                        op.then_inc(o_mm.sem, 1)

            @block.scalar
            def _(act):
                for s in (xT_ready, q_exp, k_exp, yT_ready):
                    s.open(act)
                nc.scalar.activation(S.act_warm[:], S.eps[:], ACT.Exp)
                with act.Fori(0, BATCH) as b:
                    for s in (0, 1):
                        g = b * 2 + s
                        transposed.wait(act, g)
                        nc.scalar.activation(xT[:, s, :], ps[:, T, :], ACT.Copy).then_inc(xT_ready.sem, 1)
                        q_neg.wait(act, g)
                        nc.scalar.activation(qneg[:, s, :], qneg[:, s, :], ACT.Exp).then_inc(q_exp.sem, 1)
                        kv_biased.wait(act, g * 2 + 1)
                        nc.scalar.activation(kneg[:, s, :, :], kneg[:, s, :, :], ACT.Exp).then_inc(k_exp.sem, 1)
                    for s in (0, 1):
                        g = b * 2 + s
                        yT_mm.wait(act, g)
                        nc.scalar.activation(yT[:, s, :], ps[:, YT, :], ACT.Copy).then_inc(yT_ready.sem, 1)

            @block.gpsimd
            def _(pool):
                x_biased.open(pool)
                with pool.Fori(0, GROUPS) as g:
                    normed.wait(pool, g)
                    nc.gpsimd.tensor_tensor(S.x[:, cols(g * GROUP, GROUP)], S.x[:, cols(g * GROUP, GROUP)],
                                            S.a0_bc[:], ALU.add).then_inc(x_biased.sem, 1)

            @block.vector
            def _(dve):
                for s in (normed, q_neg, q_ready, kv_biased, k_ready, s_ready, y_ready, x_ready):
                    s.open(dve)
                c0 = Chain(dve, chain)
                c0.run(nc.vector.memset(kv[:], 1.0))
                with dve.Fori(0, BATCH) as b:
                    c = Chain(dve, chain, b, 14, 1)
                    for s in (0, 1):
                        g = b * 2 + s
                        transposed.wait(dve, g - 2)
                        for k in range(GT):
                            op = normalize_tile(nc, S, xn[:, s, k * P:(k + 1) * P], g * GT + k)
                        op.then_inc(normed.sem, 1)
                    for s in (0, 1):
                        g = b * 2 + s
                        q_mm.wait(dve, g)
                        nc.vector.tensor_scalar(qneg[:, s, :], ps[:, Q, :], S.a0_bq[:], 0.0, ALU.add,
                                                ALU.min).then_inc(q_neg.sem, 1)
                        for half in (0, 1):
                            kv_mm.wait(dve, g * 2 + half)
                            z = kv[:, s, 2 * half:2 * half + 2, :]
                            c.run(nc.vector.tensor_tensor(z[:, :, 0:2 * P],
                                                          ps[:, KV[half], :].rearrange("p (t c) -> p t c", t=2),
                                                          S.a0_bkv[:].rearrange("p (t c) -> p t c", t=2), ALU.add))
                            nc.vector.tensor_scalar(kneg[:, s, 2 * half:2 * half + 2, :], z[:, :, 0:P], 0.0, None,
                                                    ALU.min).then_inc(kv_biased.sem, 1)
                        q_exp.wait(dve, g)
                        nc.vector.scalar_tensor_tensor(qT[:, s, :], ps[:, Q, :], S.a0_bq1[:], qneg[:, s, :], ALU.add,
                                                       ALU.max).then_inc(q_ready.sem, 1)
                        k_exp.wait(dve, g)
                        nc.vector.scalar_tensor_tensor(kv[:, s, :, 0:P], kv[:, s, :, 0:P], 1.0, kneg[:, s, :, :],
                                                       ALU.add, ALU.max).then_inc(k_ready.sem, 1)
                    s_mm.wait(dve, b)
                    c.run(nc.vector.tensor_copy(ksum[:], ps[:, ST, P:P + 1]))
                    c.run(nc.vector.tensor_tensor(state[:, 0:P], ps[:, ST, 0:P], S.head_mask[:], ALU.mult))
                    nc.vector.tensor_scalar(state[:, P:SW], S.head_mask[:].rearrange("p (h d) -> p h d", h=H)[:, :, 0],
                                            ksum[:], None, ALU.mult).then_inc(s_ready.sem, 1)
                    for s in (0, 1):
                        g = b * 2 + s
                        for half in (0, 1):
                            n_mm.wait(dve, g * 2 + half)
                            num = ps[:, NUM[half], 0:2 * SW].rearrange("p (t c) -> p t c", t=2)
                            r = den[:, half * 2 * H:(half + 1) * 2 * H]
                            c.run(nc.vector.tensor_scalar(r.rearrange("p (t h) -> p t h", t=2), num[:, :, P:SW], 1e-6,
                                                          None, ALU.add))
                            c.run(nc.vector.reciprocal(r, r))
                            for k in (0, 1):
                                o = y[:, s, (2 * half + k) * P:(2 * half + k + 1) * P].rearrange("p (h d) -> p h d", h=H)
                                op = nc.vector.tensor_tensor(
                                    o, num[:, k, 0:P].rearrange("p (h d) -> p h d", h=H),
                                    r[:, k * H:(k + 1) * H].rearrange("p (h o) -> p h o", o=1).broadcast_to([P, H, HD]),
                                    ALU.mult)
                            op.then_inc(y_ready.sem, 1)
                    for s in (0, 1):
                        g = b * 2 + s
                        o_mm.wait(dve, g)
                        x_biased.wait(dve, g)
                        nc.vector.tensor_tensor(S.x[:, cols(g * GROUP, GROUP)], S.x[:, cols(g * GROUP, GROUP)],
                                                ps[:, ST, :], ALU.add).then_inc(x_ready.sem, 1)
                    c.end()


def store_phase(nc, S, out):
    ctx, sb, sem, steps = scope(nc)
    with ctx:
        stored = sem("stored")
        with nc.Block() as block:
            @block.sync
            def _(sp):
                sp.dma_start(out.rearrange("b (t p) d -> p (b t) d", p=P),
                             S.x[:].rearrange("p (t d) -> p t d", d=D)).then_inc(stored, 16)
                sp.wait_ge(stored, 16)


def bcast(v, n):
    return v.rearrange("p (a o) -> p a o", o=1).broadcast_to([P, v.shape[-1], n])


def by_tile(v):
    return v.rearrange("p (t e) -> p t e", e=E)


def softmax_start(nc, dve, c, logits, mx, shifted):
    c.run(nc.vector.tensor_reduce(mx, logits, AX.X, ALU.max))
    return nc.vector.tensor_tensor(by_tile(shifted), logits, bcast(mx, E), ALU.subtract)


def softmax_end(nc, c, exped, total, gates):
    c.run(nc.vector.tensor_reduce(total, by_tile(exped), AX.X, ALU.add))
    c.run(nc.vector.reciprocal(total, total))
    c.run(nc.vector.tensor_tensor(by_tile(gates), by_tile(exped), bcast(total, E), ALU.mult))


def pick_largest(nc, S, c, values, mx, work, onehot, largest=None):
    largest = mx if largest is None else largest
    c.run(nc.vector.tensor_reduce(largest, by_tile(values), AX.X, ALU.max))
    c.run(nc.vector.tensor_tensor(by_tile(work), by_tile(values), bcast(largest, E), ALU.is_equal))
    c.run(nc.vector.tensor_tensor(work, work, S.first_rank[:], ALU.mult))
    c.run(nc.vector.tensor_reduce(mx, by_tile(work), AX.X, ALU.max))
    c.run(nc.vector.tensor_tensor(by_tile(onehot), by_tile(work), bcast(mx, E), ALU.is_equal))


def count_matmuls(nc, S, bank, mask):
    W = GT * E
    nc.tensor.matmul(bank[:, 0:W], S.prefix[:], mask, start=True, stop=True, skip_group_check=True)
    for m in range(GT):
        one = mask[:, m * E:(m + 1) * E]
        for n in range(m + 1, GT):
            nc.tensor.matmul(bank[:, n * E:(n + 1) * E], S.ones_b[:], one, start=False, stop=True,
                             skip_group_check=True)
        op = nc.tensor.matmul(bank[:, W:W + E], S.ones_b[:], one, start=False, stop=True, skip_group_check=True)
    return op


def routed_pair_ffn(nc, S):
    CAP = float(-(-TOK * 5 // (E * 4)))
    FC = 2
    ctx, sb, sem, steps = scope(nc)
    ps = S.ps
    T, L, C, HB = 0, 1, 2, 3
    W = GT * E
    with ctx:
        xn = sb("xn", [P, 2, GROUP])
        xT = sb("xT", [P, 2, GROUP])
        hT = sb("hT", [P, 2, FC, GROUP])
        mx, total = sb("mx", [P, GT]), sb("total", [P, GT])
        exped, gates, work, rest = sb("exped", [P, W]), sb("gates", [P, W]), sb("work", [P, W]), sb("rest", [P, W])
        best, second, mask = sb("best", [P, W]), sb("second", [P, W]), sb("mask", [P, W], BF16)
        carry, cum = sb("carry", [P, E]), sb("cum", [P, W])
        comb = sb("comb", [P, 2, W])
        chain = sem("chain")
        (normed, transposed, xT_ready, l_mm, shifted, exp_done, h_mm, h_ready, masked, counted, counts_read, y_mm,
         y_added) = [steps(n) for n in ("normed transposed xT_ready l_mm shifted exp_done h_mm h_ready masked counted "
                                        "counts_read y_mm y_added").split()]
        FRONT, BACK = 22, GT * (E - 1)

        def pairs(eng, front, back):
            front(0, 0, True)
            with eng.Fori(0, (GROUPS - 2) // 2) as j:
                for s in (0, 1):
                    front(j * 2 + (s + 1), 1 - s)
                    back(j * 2 + s, s)
            front(GROUPS - 1, 1)
            back(GROUPS - 2, 0)
            back(GROUPS - 1, 1, True)

        with nc.Block() as block:
            @block.tensor
            def _(pe):
                for s in (transposed, l_mm, h_mm, counted, y_mm):
                    s.open(pe)

                def front(g, s, first=False):
                    normed.wait(pe, g)
                    xT_ready.wait(pe, g - 1)
                    for k in range(GT):
                        op = nc.tensor.transpose(ps[:, T, k * P:(k + 1) * P], xn[:, s, k * P:(k + 1) * P], S.ident[:])
                    op.then_inc(transposed.sem, 1)
                    xT_ready.wait(pe, g)
                    shifted.wait(pe, g - 1)
                    for k in range(GT):
                        op = nc.tensor.matmul(ps[:, L, k * E:(k + 1) * E], xT[:, s, k * P:(k + 1) * P], S.f0_wr[:],
                                              start=True, stop=True)
                    op.then_inc(l_mm.sem, 1)
                    for f in range(FC):
                        h_ready.wait(pe, g * FC + f - 1)
                        nc.tensor.matmul(ps[:, HB, :], S.f0_wg[:, f * P:(f + 1) * P], xT[:, s, :],
                                         start=True, stop=True).then_inc(h_mm.sem, 1)
                    if first:
                        counts(g)

                def counts(g):
                    masked.wait(pe, g)
                    counts_read.wait(pe, g - 1)
                    count_matmuls(nc, S, ps[:, C, :], mask[:]).then_inc(counted.sem, 1)

                def back(g, s, last=False):
                    h_ready.wait(pe, g * FC + FC - 1)
                    for k in range(GT):
                        if k == 2 and not last:
                            counts(g + 1)
                        y_added.wait(pe, g * GT + k - 2)
                        for half in (0, 1):
                            for f in range(FC):
                                op = nc.tensor.matmul(ps[:, 4 + 2 * (k % 2) + half, :], hT[:, s, f, k * P:(k + 1) * P],
                                                      S.f0_wd[:, f, half * GROUP:(half + 1) * GROUP],
                                                      start=(f == 0), stop=(f == FC - 1))
                        op.then_inc(y_mm.sem, 1)

                pairs(pe, front, back)

            @block.scalar
            def _(act):
                for s in (xT_ready, exp_done, h_ready):
                    s.open(act)

                def front(g, s, first=False):
                    transposed.wait(act, g)
                    nc.scalar.activation(xT[:, s, :], ps[:, T, :], ACT.Copy).then_inc(xT_ready.sem, 1)
                    shifted.wait(act, g)
                    nc.scalar.activation(exped[:], exped[:], ACT.Exp).then_inc(exp_done.sem, 1)
                    y_mm.wait(act, g * GT - GT - 1)
                    for f in range(FC):
                        h_mm.wait(act, g * FC + f)
                        nc.scalar.activation(hT[:, s, f, :], ps[:, HB, :], ACT.Silu).then_inc(h_ready.sem, 1)

                pairs(act, front, lambda *_: None)

            @block.vector
            def _(dve):
                for s in (normed, shifted, masked, counts_read, y_added):
                    s.open(dve)

                def front(g, s, first=False):
                    c = Chain(dve, chain, 0, 0, 1) if first else Chain(dve, chain, g - 1, FRONT + BACK, FRONT + 1)
                    transposed.wait(dve, g - 2)
                    for k in range(GT):
                        op = normalize_tile(nc, S, xn[:, s, k * P:(k + 1) * P], g * GT + k)
                    op.then_inc(normed.sem, 1)
                    l_mm.wait(dve, g)
                    softmax_start(nc, dve, c, by_tile(ps[:, L, 0:W]), mx[:], exped[:]).then_inc(shifted.sem, 1)
                    exp_done.wait(dve, g)
                    softmax_end(nc, c, exped[:], total[:], gates[:])
                    pick_largest(nc, S, c, gates[:], mx[:], work[:], best[:])
                    c.run(nc.vector.scalar_tensor_tensor(rest[:], best[:], -2.0, gates[:], ALU.mult, ALU.add))
                    pick_largest(nc, S, c, rest[:], mx[:], work[:], second[:])
                    nc.vector.tensor_tensor(mask[:], best[:], second[:], ALU.add).then_inc(masked.sem, 1)
                    counted.wait(dve, g)
                    c.run(nc.vector.tensor_tensor(by_tile(cum[:]), by_tile(ps[:, C, 0:W]),
                                                  carry[:].rearrange("p (o e) -> p o e", o=1).broadcast_to([P, GT, E]),
                                                  ALU.add))
                    nc.vector.tensor_tensor(carry[:], carry[:], ps[:, C, W:W + E], ALU.add).then_inc(counts_read.sem, 1)
                    counts_read.wait(dve, g)
                    c.run(nc.vector.scalar_tensor_tensor(cum[:], cum[:], CAP, mask[:], ALU.is_le, ALU.mult))
                    c.run(nc.vector.tensor_tensor(work[:], cum[:], gates[:], ALU.mult))
                    c.run(nc.vector.tensor_reduce(total[:], by_tile(work[:]), AX.X, ALU.add))
                    c.run(nc.vector.tensor_scalar(total[:], total[:], 1e-6, None, ALU.add))
                    c.run(nc.vector.reciprocal(total[:], total[:]))
                    c.run(nc.vector.tensor_tensor(by_tile(comb[:, s, :]), by_tile(work[:]), bcast(total[:], E), ALU.mult))
                    assert c.n == FRONT, c.n

                def back(g, s, last=False):
                    c = Chain(dve, chain, g, FRONT + BACK, (1 if last else 2) * FRONT + 1)
                    for k in range(GT):
                        y_mm.wait(dve, g * GT + k)
                        xt = S.x[:, cols((g * GT + k) * P, P)]
                        for e in range(E):
                            op = nc.vector.scalar_tensor_tensor(
                                xt, ps[:, 4 + 2 * (k % 2) + e // 4, (e % 4) * P:(e % 4 + 1) * P],
                                comb[:, s, k * E + e:k * E + e + 1], xt, ALU.mult, ALU.add)
                            if e < E - 1:
                                c.run(op)
                        op.then_inc(y_added.sem, 1)
                    assert c.n == BACK

                c0 = Chain(dve, chain)
                c0.run(nc.vector.memset(carry[:], 0.0))
                pairs(dve, front, back)


PARTS = 3
STACK = PARTS * PARTS * HD
SHIFT = 2
HEADS = BATCH * H


def project_qkv(nc, S, wq, bq, scale, wk, bk, wv, bv, vd, keep_v=False):
    ctx, sb, sem, steps = scope(nc)
    ps = S.ps
    VC = H * vd
    VB = max(1, VC // GROUP)
    KTS = SEQ // P
    T, QK, V = 0, (1, 2), 3
    with ctx:
        xn = sb("xn", [P, 2, GROUP])
        xT = sb("xT", [P, 2, GROUP])
        z = sb("z", [P, 2, GROUP])
        parts = sb("parts", [P, 2, 2, PARTS, GROUP], BF16)
        v_out = sb("v_out", [P, 8 if keep_v else VC * KTS])
        (normed, transposed, xT_ready, qk_mm, z_ready, hi_ready, rest_ready, mid_ready, lo_ready, v_mm, v_ready) = [
            steps(n) for n in ("normed transposed xT_ready qk_mm z_ready hi_ready rest_ready mid_ready lo_ready v_mm "
                               "v_ready").split()]
        parts_out = [sem("parts_out0"), sem("parts_out1")]
        v_stored = sem("v_stored")
        chain = sem("chain")
        v_view = v_out[:].rearrange("p (c t) -> p t c", t=KTS)
        VSTEPS = GT * VB if VC > GROUP else 1
        with nc.Block() as block:
            @block.tensor
            def _(pe):
                for s in (transposed, qk_mm, v_mm):
                    s.open(pe)
                with pe.Fori(0, BATCH) as b:
                    for s in (0, 1):
                        g = b * 2 + s
                        normed.wait(pe, g)
                        xT_ready.wait(pe, g - 1)
                        for k in range(GT):
                            op = nc.tensor.transpose(ps[:, T, k * P:(k + 1) * P], xn[:, s, k * P:(k + 1) * P], S.ident[:])
                        op.then_inc(transposed.sem, 1)
                        xT_ready.wait(pe, g)
                        for n, w in enumerate((wq, wk)):
                            z_ready.wait(pe, g * 2 + n - 2)
                            nc.tensor.matmul(ps[:, QK[n], :], w[:], xT[:, s, :], start=True, stop=True).then_inc(qk_mm.sem, 1)
                        if VC <= GROUP:
                            v_ready.wait(pe, g - 1)
                            for k in range(GT):
                                op = nc.tensor.matmul(ps[:, V, k * VC:(k + 1) * VC], xT[:, s, k * P:(k + 1) * P], wv[:],
                                                      start=True, stop=True)
                            op.then_inc(v_mm.sem, 1)
                        else:
                            for k in range(GT):
                                for w in range(VB):
                                    n = k * VB + w
                                    v_ready.wait(pe, g * VSTEPS + n - 4)
                                    nc.tensor.matmul(ps[:, V + n % 4, :], xT[:, s, k * P:(k + 1) * P],
                                                     wv[:, w * GROUP:(w + 1) * GROUP], start=True,
                                                     stop=True).then_inc(v_mm.sem, 1)

            @block.scalar
            def _(act):
                for s in (xT_ready, hi_ready, mid_ready):
                    s.open(act)
                with act.Fori(0, BATCH) as b:
                    for s in (0, 1):
                        g = b * 2 + s
                        transposed.wait(act, g)
                        nc.scalar.activation(xT[:, s, :], ps[:, T, :], ACT.Copy).then_inc(xT_ready.sem, 1)
                        for n in (0, 1):
                            z_ready.wait(act, g * 2 + n)
                            nc.scalar.activation(parts[:, s, n, 0, :], z[:, n, :], ACT.Copy).then_inc(hi_ready.sem, 1)
                            rest_ready.wait(act, g * 2 + n)
                            nc.scalar.activation(parts[:, s, n, 1, :], z[:, n, :], ACT.Copy).then_inc(mid_ready.sem, 1)

            @block.vector
            def _(dve):
                for s in (normed, z_ready, rest_ready, lo_ready, v_ready):
                    s.open(dve)

                def group(b, s, first):
                    g = b * 2 + s
                    transposed.wait(dve, g - 2)
                    for k in range(GT):
                        op = normalize_tile(nc, S, xn[:, s, k * P:(k + 1) * P], g * GT + k)
                    op.then_inc(normed.sem, 1)
                    if not first:
                        dve.wait_ge(parts_out[s], b * 32)
                    for n in (0, 1):
                        qk_mm.wait(dve, g * 2 + n)
                        if n == 0:
                            nc.vector.tensor_scalar(z[:, n, :], ps[:, QK[n], :], bq[:], scale, ALU.add,
                                                    ALU.mult).then_inc(z_ready.sem, 1)
                        else:
                            nc.vector.tensor_scalar(z[:, n, :], ps[:, QK[n], :], bk[:], None,
                                                    ALU.add).then_inc(z_ready.sem, 1)
                    if s == 0 and not first and not keep_v:
                        dve.wait_ge(v_stored, b * 16)
                    if keep_v:
                        v_mm.wait(dve, g)
                        nc.vector.tensor_tensor(S.v_tok[:, cols(g * GROUP, GROUP)], ps[:, V, :], bv[:],
                                                ALU.add).then_inc(v_ready.sem, 1)
                    elif VC <= GROUP:
                        v_mm.wait(dve, g)
                        nc.vector.tensor_tensor(v_view[:, s * GT:(s + 1) * GT, :],
                                                ps[:, V, :].rearrange("p (t c) -> p t c", t=GT),
                                                bv[:].rearrange("p (t c) -> p t c", t=GT), ALU.add).then_inc(v_ready.sem, 1)
                    else:
                        for k in range(GT):
                            for w in range(VB):
                                n = k * VB + w
                                v_mm.wait(dve, g * VSTEPS + n)
                                nc.vector.tensor_tensor(v_view[:, s * GT + k, w * GROUP:(w + 1) * GROUP],
                                                        ps[:, V + n % 4, :], bv[:, w * GROUP:(w + 1) * GROUP],
                                                        ALU.add).then_inc(v_ready.sem, 1)
                    for n in (0, 1):
                        hi_ready.wait(dve, g * 2 + n)
                        nc.vector.tensor_tensor(z[:, n, :], z[:, n, :], parts[:, s, n, 0, :],
                                                ALU.subtract).then_inc(rest_ready.sem, 1)
                    for n in (0, 1):
                        mid_ready.wait(dve, g * 2 + n)
                        nc.vector.tensor_tensor(parts[:, s, n, 2, :], z[:, n, :], parts[:, s, n, 1, :],
                                                ALU.subtract).then_inc(lo_ready.sem, 1)

                for s in (0, 1):
                    group(0, s, True)
                with dve.Fori(1, BATCH) as b:
                    for s in (0, 1):
                        group(b, s, False)

            @block.sync
            def _(sp):
                with sp.Fori(0, BATCH) as b:
                    for s in (0, 1):
                        for n, dst in enumerate((S.q_parts, S.k_parts)):
                            lo_ready.wait(sp, b * 4 + s * 2 + n)
                            sp.dma_start(dst[bass.ds(b, 1), :, :, :, s * GROUP:(s + 1) * GROUP]
                                         .rearrange("b a h d t -> (b h d) a t"), parts[:, s, n]).then_inc(parts_out[s], 16)
                    if not keep_v:
                        v_ready.wait(sp, b * 2 * VSTEPS + 2 * VSTEPS - 1)
                        sp.dma_start(S.v_heads[bass.ds(b * H, H), :, 0:vd * KTS].rearrange("h p c -> p h c"),
                                     v_out[:].rearrange("p (h c) -> p h c", h=H)).then_inc(v_stored, 16)
                for q in parts_out:
                    sp.wait_ge(q, 32 * BATCH)
                if not keep_v:
                    sp.wait_ge(v_stored, 16 * BATCH)


class Head:

    def __init__(self, turn, c):
        self.turn, self.c = turn, c

    def __sub__(self, n):
        return Head(self.turn, self.c - n)

    def times(self, k, plus=0):
        return self.turn * (4 * k) + (self.c * k + plus)

    def rounds(self, ring):
        return self.turn * (4 // ring) + self.c // ring

    def slot(self, ring):
        return self.c % ring


def load_stacks(sp, S, i, q_stack, k_stack, loaded):
    b, h = i.times(1) // H, i.times(1) % H
    for r in range(PARTS):
        rows = slice(r * PARTS * HD, (r + 1) * PARTS * HD)
        q = S.q_parts[bass.ds(b, 1), r, bass.ds(h, 1), :, :].rearrange("b h d t -> (b h) d t")
        sp.dma_start(q_stack[rows, :], q.broadcast_to([PARTS, HD, SEQ])).then_inc(loaded, 16)
        k = S.k_parts[bass.ds(b, 1), :, bass.ds(h, 1), :, :].rearrange("b a h d t -> (b a) (h d) t")
        sp.dma_start(k_stack[rows, :], k).then_inc(loaded, 16)


def attend(nc, S, causal, vd):
    ctx, sb, sem, steps = scope(nc)
    ps = S.ps
    KTS = SEQ // P
    VW = vd + 1 if causal else 32
    CH = SEQ // GROUP
    S1, S2, OB, MB = 0, 4, 6, 7
    MP = 96 if causal else 0
    if causal:
        MB = OB
        tiles = [(kt, c) for kt in range(KTS) for c in range(CH) if kt * P < (c + 1) * GROUP]
        groups = [tiles[0:4], tiles[4:8], tiles[8:10], tiles[10:12]]
    else:
        tiles = [(kt, c) for kt in range(KTS) for c in range(CH)]
        groups = [tiles[n:n + 4] for n in range(0, 16, 4)]
    NT = len(tiles)
    RING = 6 if causal else 8
    LOADS = 16 * (2 * PARTS + 1)
    OROWS = VW if causal else P

    with ctx:
        qs = [sb(f"q_stack{n}", [P, SEQ], BF16) for n in range(4)]
        ks = [sb(f"k_stack{n}", [P, SEQ], BF16) for n in range(4)]
        vs = [sb(f"v{n}", [P, VW, KTS]) for n in range(4)]
        prob = sb("prob", [P, RING, GROUP])
        neg_max = sb("neg_max", [P, 2, KTS])
        shift = sb("shift", [P, 2, SHIFT * KTS], BF16)
        shift_rows = sb("shift_rows", [P, 2, P], BF16)
        o_out = sb("o_out", [P, 2, SEQ if causal else GROUP])
        (s1_mm, maxed, split, m_mm, m_read, s2_mm, exped, pv_mm, o_read) = [steps(n) for n in (
            "s1_mm maxed split m_mm m_read s2_mm exped pv_mm o_read").split()]
        loaded = [sem(f"loaded{n}") for n in range(4)]
        shifted = [sem(f"shifted{n}") for n in range(2)]
        stored = [sem(f"stored{n}") for n in range(2)]
        cleared, chain = sem("cleared"), sem("chain")

        def offset(kt, c):
            return max(kt * P - c * GROUP, 0) if causal else 0

        def run(eng, step):
            last = HEADS + 2
            for c in range(4):
                step(Head(0, c), c)
            with eng.Fori(1, HEADS // 4 - 1) as turn:
                for c in range(4):
                    step(Head(turn, c), None)
            for c in range(HEADS - 4, last + 1):
                step(Head(0, c), c)

        def there(n, h):
            return n is None or 0 <= n - h < HEADS

        with nc.Block() as block:
            @block.tensor
            def _(pe):
                for s in (s1_mm, m_mm, s2_mm, pv_mm):
                    s.open(pe)

                def first_pass(i, qt):
                    bank = S1 + 2 * (qt % 2)
                    maxed.wait(pe, i.times(KTS, qt - 2))
                    q, k = qs[i.slot(4)], ks[i.slot(4)]
                    for c in range(CH):
                        n = min(GROUP, (qt + 1) * P - c * GROUP) if causal else GROUP
                        if n > 0:
                            op = nc.tensor.matmul(ps[:, bank + c, 0:n], q[0:STACK, qt * P:(qt + 1) * P],
                                                  k[0:STACK, c * GROUP:c * GROUP + n], start=True,
                                                  stop=not causal or qt * P >= (c + 1) * GROUP)
                    if causal:
                        c, at = divmod(qt * P, GROUP)
                        op = nc.tensor.matmul(ps[:, bank + c, at:at + P], S.ident_b[:], S.mask_qk[:],
                                              start=False, stop=True)
                    op.then_inc(s1_mm.sem, 1)

                def second_scores(j, n, kt, c):
                    exped.wait(pe, j.times(NT, n - 2))
                    o = offset(kt, c)
                    diagonal = causal and kt * P >= c * GROUP
                    out = ps[:, S2 + n % 2, o:GROUP]
                    op = nc.tensor.matmul(out, ks[j.slot(4)][:, kt * P:(kt + 1) * P],
                                          qs[j.slot(4)][:, c * GROUP + o:(c + 1) * GROUP], start=True, stop=not diagonal)
                    if diagonal:
                        op = nc.tensor.matmul(ps[:, S2 + n % 2, o:o + P], S.ident_b[:], S.mask_kq[:],
                                              start=False, stop=True)
                    op.then_inc(s2_mm.sem, 1)

                def weigh(j, g):
                    if g == 0:
                        o_read.wait(pe, j.times(1, -1))
                    at = sum(len(x) for x in groups[:g])
                    exped.wait(pe, j.times(NT, at + len(groups[g]) - 1))
                    for n, (kt, c) in enumerate(groups[g], at):
                        o = offset(kt, c)
                        if causal:
                            out = ps[0:VW, OB + c, o:GROUP]
                            start, stop = kt == 0, kt == (c + 1) * GROUP // P - 1
                        else:
                            quad = (c * 2 + kt % 2) * 32
                            out = ps[quad:quad + VW, OB, :]
                            start, stop = kt < 2, kt >= KTS - 2
                        nc.tensor.matmul(out, vs[j.slot(4)][:, :, kt], prob[:, n % RING, o:GROUP], start=start,
                                         stop=stop).then_inc(pv_mm.sem, 1)

                def step(i, n):
                    one, two = there(n, 0), there(n, 2)
                    if one:
                        pe.wait_ge(loaded[i.slot(4)], (i.rounds(4) + 1) * LOADS)
                    if two:
                        pe.wait_ge(shifted[i.slot(2)], ((i - 2).rounds(2) + 1) * 16)
                    j = i - 2
                    for g in range(4):
                        at = sum(len(x) for x in groups[:g])
                        mine = list(enumerate(groups[g], at))
                        half = len(mine) // 2
                        if two:
                            for m, (kt, c) in mine[:half]:
                                second_scores(j, m, kt, c)
                        if one:
                            first_pass(i, 2 * g)
                        if two:
                            for m, (kt, c) in mine[half:]:
                                second_scores(j, m, kt, c)
                        if g > 0 and two:
                            weigh(j, g - 1)
                        if g == 0 and there(n, 3):
                            weigh(i - 3, 3)
                        if one:
                            first_pass(i, 2 * g + 1)
                        if g == 1 and there(n, 1):
                            h = i - 1
                            split.wait(pe, h.times(1))
                            m_read.wait(pe, h.times(1, -1))
                            nc.tensor.transpose(ps[MP:MP + SHIFT * KTS, MB, 0:P // 2].bitcast(BF16),
                                                shift[:, h.slot(2), :], S.ident_b[:]).then_inc(m_mm.sem, 1)

                pe.wait_ge(cleared, 1)
                run(pe, step)

            @block.scalar
            def _(act):
                for s in (exped, m_read):
                    s.open(act)

                def step(i, n):
                    j = i - 2
                    for g in range(4):
                        if there(n, 2):
                            at = sum(len(x) for x in groups[:g])
                            for m, (kt, c) in enumerate(groups[g], at):
                                s2_mm.wait(act, j.times(NT, m))
                                pv_mm.wait(act, j.times(NT, m - RING))
                                o = offset(kt, c)
                                nc.scalar.activation(prob[:, m % RING, o:GROUP], ps[:, S2 + m % 2, o:GROUP],
                                                     ACT.Exp).then_inc(exped.sem, 1)
                        if g == 1 and there(n, 1):
                            h = i - 1
                            m_mm.wait(act, h.times(1))
                            if n is None or n - 3 >= 0:
                                act.wait_ge(shifted[h.slot(2)], h.rounds(2) * 16)
                            nc.scalar.activation(shift_rows[MP:MP + SHIFT * KTS, h.slot(2), :],
                                                 ps[MP:MP + SHIFT * KTS, MB, 0:P // 2].bitcast(BF16),
                                                 ACT.Copy).then_inc(m_read.sem, 1)

                nc.scalar.activation(S.act_warm[:], S.eps[:], ACT.Exp)
                run(act, step)

            @block.vector
            def _(dve):
                for s in (maxed, o_read):
                    s.open(dve)

                def step(i, n):
                    for qt in range(KTS):
                        if there(n, 0):
                            if qt == 0:
                                split.wait(dve, i.times(1, -2))
                            s1_mm.wait(dve, i.times(KTS, qt))
                            bank = S1 + 2 * (qt % 2)
                            keys = (qt + 1) * P if causal else SEQ
                            nc.vector.tensor_reduce(neg_max[:, i.slot(2), qt:qt + 1],
                                                    ps[:, bank:bank + 2, :].rearrange("p b n -> p (b n)")[:, 0:keys],
                                                    AX.X, ALU.max, negate=True).then_inc(maxed.sem, 1)
                        if qt == 1 and there(n, 3):
                            h = i - 3
                            pv_mm.wait(dve, h.times(NT, NT - 1))
                            if n is None or n - 3 >= 2:
                                dve.wait_ge(stored[h.slot(2)], h.rounds(2) * 16)
                            src = ps[0:OROWS, OB:OB + 2, :] if causal else ps[:, OB, :]
                            dst = o_out[0:OROWS, h.slot(2), :]
                            if causal:
                                dst = dst.rearrange("p (c n) -> p c n", c=CH)
                            nc.vector.tensor_copy(dst, src).then_inc(o_read.sem, 1)

                run(dve, step)

            @block.gpsimd
            def _(pool):
                split.open(pool)
                for n in range(4):
                    nc.gpsimd.memset(qs[n][:], 0.0)
                    nc.gpsimd.memset(ks[n][:], 1.0)
                    nc.gpsimd.memset(vs[n][:, vd + 1:VW, :], 0.0) if VW > vd + 1 else None
                    op = nc.gpsimd.memset(vs[n][:, vd:vd + 1, :], 1.0)
                op.then_inc(cleared, 1)

                def heads(i):
                    maxed.wait(pool, i.times(KTS, KTS - 1))
                    m_mm.wait(pool, i.times(1, -2))
                    hi = shift[:, i.slot(2), 0:KTS]
                    nc.gpsimd.tensor_tensor(hi, neg_max[:, i.slot(2), :], S.zeros[:, 0:KTS],
                                            ALU.add).then_inc(chain, 1)
                    pool.wait_ge(chain, i.times(1, 1))
                    nc.gpsimd.tensor_tensor(shift[:, i.slot(2), KTS:2 * KTS], neg_max[:, i.slot(2), :], hi,
                                            ALU.subtract).then_inc(split.sem, 1)

                with pool.Fori(0, HEADS // 4) as turn:
                    for c in range(4):
                        heads(Head(turn, c))

            @block.sync
            def _(sp):
                sp.wait_ge(cleared, 1)

                def load(i, n):
                    if n is None or n >= 4:
                        pv_mm.wait(sp, i.times(NT, -3 * NT - 1))
                    at, slot = i.times(1), i.slot(4)
                    load_stacks(sp, S, i, qs[slot], ks[slot], loaded[slot])
                    sp.dma_start(vs[slot][:, 0:vd, :],
                                 S.v_heads[bass.ds(at, 1), :, 0:vd * KTS].rearrange("a p (d t) -> (a p) d t", t=KTS)
                                 ).then_inc(loaded[slot], 16)

                def step(i, n):
                    if n is None or n + 1 < HEADS:
                        load(i - (-1), None if n is None else n + 1)
                    if there(n, 3):
                        h = i - 3
                        o_read.wait(sp, h.times(1))
                        at = h.times(1)
                        if causal:
                            sp.dma_start(S.o_wide[bass.ds(at, 1), :, :].rearrange("a r n -> (a r) n"),
                                         o_out[0:OROWS, h.slot(2), :]).then_inc(stored[h.slot(2)], 16)
                        else:
                            sp.dma_start(S.o_quads[bass.ds(at, 1), :, :].rearrange("a r n -> (a r) n"),
                                         o_out[:, h.slot(2), :]).then_inc(stored[h.slot(2)], 16)
                    if there(n, 1):
                        h = i - 1
                        m_read.wait(sp, h.times(1))
                        sp.dma_start(qs[h.slot(4)][STACK:STACK + SHIFT, :].rearrange("r (q t) -> r q t", t=P),
                                     shift_rows[MP:MP + SHIFT * KTS, h.slot(2), :]).then_inc(shifted[h.slot(2)], 16)

                load(Head(0, 0), 0)
                run(sp, step)
                for s in stored:
                    sp.wait_ge(s, 16 * HEADS // 2)


def reciprocal_sums(nc, S, rows, out):
    ctx, sb, sem, steps = scope(nc)
    with ctx:
        part = sb("sums", [P, len(rows), GROUP])
        loaded, chain, ready, stored = sem("loaded"), sem("chain"), sem("ready"), sem("stored")
        with nc.Block() as block:
            @block.sync
            def _(sp):
                n = 0
                for k, some in enumerate(rows):
                    for at, src in some:
                        sp.dma_start(part[at, k, :], src).then_inc(loaded, 16)
                        n += 1
                sp.wait_ge(ready, 1)
                sp.dma_start(out, part[:, 0, :]).then_inc(stored, 16)
                sp.wait_ge(stored, 16)

            @block.vector
            def _(dve):
                dve.wait_ge(loaded, 16 * sum(len(x) for x in rows))
                c = Chain(dve, chain)
                if len(rows) == 2:
                    c.run(nc.vector.tensor_tensor(part[:, 0, :], part[:, 0, :], part[:, 1, :], ALU.add))
                nc.vector.reciprocal(part[:, 0, :], part[:, 0, :]).then_inc(ready, 1)


def attention_output(nc, S, wo, bo):
    quads = S.o_quads[:, :, :].rearrange("a (c q r) n -> a c q r n", c=2, q=2)
    reciprocal_sums(nc, S, [[(slice(0, P), quads[:, :, q, HD, :].rearrange("a c n -> (a c) n"))] for q in (0, 1)],
                    S.r_sums[:, :, :].rearrange("a c n -> (a c) n"))
    ctx, sb, sem, steps = scope(nc)
    ps = S.ps
    with ctx:
        num = sb("num", [P, 2, 2, GROUP])
        r = sb("r", [P, 2, GROUP])
        oT = sb("oT", [P, 2, GROUP])
        loaded = [sem("loaded0"), sem("loaded1")]
        added, x_biased, o_ready, y_mm, x_ready = [steps(n) for n in "added x_biased o_ready y_mm x_ready".split()]
        with nc.Block() as block:
            @block.sync
            def _(sp):
                with sp.Fori(0, BATCH) as b:
                    for c in (0, 1):
                        o_ready.wait(sp, b * 2 + c - 2)
                        for q in (0, 1):
                            src = quads[bass.ds(b * H, H), c, q, 0:HD, :]
                            sp.dma_start(num[:, c, q, :], src.rearrange("h r n -> h r n")).then_inc(loaded[c], 16)
                        sp.dma_start(r[:, c, :],
                                     S.r_sums[bass.ds(b * H, H), c:c + 1, :].broadcast_to([H, HD, GROUP])
                                     ).then_inc(loaded[c], 16)

            @block.gpsimd
            def _(pool):
                added.open(pool)
                x_biased.open(pool)
                with pool.Fori(0, BATCH) as b:
                    for c in (0, 1):
                        x = S.x[:, cols((b * 2 + c) * GROUP, GROUP)]
                        nc.gpsimd.tensor_tensor(x, x, bo[:], ALU.add).then_inc(x_biased.sem, 1)
                        pool.wait_ge(loaded[c], b * 48 + 48)
                        nc.gpsimd.tensor_tensor(num[:, c, 0, :], num[:, c, 0, :], num[:, c, 1, :],
                                                ALU.add).then_inc(added.sem, 1)

            @block.vector
            def _(dve):
                o_ready.open(dve)
                x_ready.open(dve)
                with dve.Fori(0, BATCH) as b:
                    for c in (0, 1):
                        g = b * 2 + c
                        added.wait(dve, g)
                        dve.wait_ge(loaded[c], b * 48 + 48)
                        y_mm.wait(dve, g - 2)
                        nc.vector.tensor_tensor(oT[:, c, :], num[:, c, 0, :], r[:, c, :], ALU.mult).then_inc(o_ready.sem, 1)
                    for c in (0, 1):
                        g = b * 2 + c
                        y_mm.wait(dve, g)
                        x_biased.wait(dve, g)
                        x = S.x[:, cols(g * GROUP, GROUP)]
                        nc.vector.tensor_tensor(x, x, ps[:, c, :], ALU.add).then_inc(x_ready.sem, 1)

            @block.tensor
            def _(pe):
                y_mm.open(pe)
                with pe.Fori(0, BATCH) as b:
                    for c in (0, 1):
                        g = b * 2 + c
                        o_ready.wait(pe, g)
                        x_ready.wait(pe, g - 2)
                        for k in range(GT):
                            op = nc.tensor.matmul(ps[:, c, k * P:(k + 1) * P], oT[:, c, k * P:(k + 1) * P], wo[:],
                                                  start=True, stop=True)
                        op.then_inc(y_mm.sem, 1)


def wide_attention_output(nc, S, wo, bo):
    VD = LATENT
    FC = H * VD // P
    reciprocal_sums(nc, S, [[(slice(c * HEADS, (c + 1) * HEADS), S.o_wide[:, VD, c * GROUP:(c + 1) * GROUP])
                             for c in (0, 1)]], S.r_wide[:, :, :].rearrange("c a n -> (c a) n"))
    ctx, sb, sem, steps = scope(nc)
    ps = S.ps
    with ctx:
        num = sb("num", [P, 2, FC, GROUP])
        r = sb("r", [H, 2, GROUP])
        oT = sb("oT", [P, 2, FC, GROUP])
        pick = sb("pick", [H, FC * P])
        made = sem("made")
        loaded = [sem("loaded0"), sem("loaded1")]
        r_mm, o_ready, x_biased, y_mm, x_ready = [steps(n) for n in "r_mm o_ready x_biased y_mm x_ready".split()]
        with nc.Block() as block:
            @block.sync
            def _(sp):
                with sp.Fori(0, BATCH) as b:
                    for c in (0, 1):
                        o_ready.wait(sp, (b * 2 + c) * FC - FC - 1)
                        for h in (0, 1):
                            src = S.o_wide[bass.ds(b * H, H), 0:VD, c * GROUP:(c + 1) * GROUP]
                            src = src.rearrange("(f h) l n -> h l f n", h=2)[h]
                            sp.dma_start(num[h * VD:(h + 1) * VD, c, :, :], src).then_inc(loaded[c], 16)
                        sp.dma_start(r[:, c, :], S.r_wide[c, bass.ds(b * H, H), :]).then_inc(loaded[c], 16)

            @block.gpsimd
            def _(pool):
                x_biased.open(pool)
                v = pick[:].rearrange("p (f h l) -> p f h l", f=FC, h=2)
                nc.gpsimd.memset(pick[:], 1.0).then_inc(made, 1)
                pool.wait_ge(made, 1)
                nc.gpsimd.affine_select(out=v, in_=v, compare_op=ALU.is_equal, fill=0.0, base=0,
                                        pattern=[[-2, FC], [-1, 2], [0, VD]], channel_multiplier=1).then_inc(made, 1)
                with pool.Fori(0, GROUPS) as g:
                    x = S.x[:, cols(g * GROUP, GROUP)]
                    nc.gpsimd.tensor_tensor(x, x, bo[:], ALU.add).then_inc(x_biased.sem, 1)

            @block.vector
            def _(dve):
                o_ready.open(dve)
                x_ready.open(dve)
                with dve.Fori(0, BATCH) as b:
                    for c in (0, 1):
                        g = b * 2 + c
                        y_mm.wait(dve, g - 2)
                        for f in range(FC):
                            r_mm.wait(dve, g * FC + f)
                            nc.vector.tensor_tensor(oT[:, c, f, :], num[:, c, f, :], ps[:, f % 4, :],
                                                    ALU.mult).then_inc(o_ready.sem, 1)
                        y_mm.wait(dve, g)
                        x_biased.wait(dve, g)
                        x = S.x[:, cols(g * GROUP, GROUP)]
                        nc.vector.tensor_tensor(x, x, ps[:, 4:8, 0:P], ALU.add).then_inc(x_ready.sem, 1)

            @block.tensor
            def _(pe):
                r_mm.open(pe)
                y_mm.open(pe)
                pe.wait_ge(made, 2)
                with pe.Fori(0, BATCH) as b:
                    for c in (0, 1):
                        g = b * 2 + c
                        pe.wait_ge(loaded[c], b * 48 + 48)
                        for f in range(FC):
                            o_ready.wait(pe, g * FC + f - 4)
                            nc.tensor.matmul(ps[:, f % 4, :], pick[:, f * P:(f + 1) * P], r[:, c, :], start=True,
                                             stop=True).then_inc(r_mm.sem, 1)
                        o_ready.wait(pe, g * FC + FC - 1)
                        x_ready.wait(pe, g - 1)
                        for k in range(GT):
                            for f in range(FC):
                                op = nc.tensor.matmul(ps[:, 4 + k, 0:P], oT[:, c, f, k * P:(k + 1) * P], wo[:, f, :],
                                                      start=(f == 0), stop=(f == FC - 1))
                        op.then_inc(y_mm.sem, 1)


LATENT = 64


def full_attention(nc, S):
    project_qkv(nc, S, S.b0_wq, S.b0_bq, HD ** -0.5, S.b0_wk, S.b0_bk, S.b0_wv, S.b0_bv, HD)
    attend(nc, S, False, HD)
    attention_output(nc, S, S.b0_wo, S.b0_bo)


def fold_latent_key(nc, S):
    ctx, sb, sem, steps = scope(nc)
    ps = S.ps
    L = LATENT
    with ctx:
        outer = sb("outer", [L, H * HD])
        ones = sb("ones", [L, 1])
        made, folded = sem("made"), sem("folded")
        with nc.Block() as block:
            @block.vector
            def _(dve):
                nc.vector.memset(ones[:], 1.0)
                nc.vector.tensor_tensor(outer[:].rearrange("p (h d) -> p h d", h=H),
                                        S.a1_bkl[:].rearrange("p (h o) -> p h o", o=1).broadcast_to([L, H, HD]),
                                        S.a1_wc[:].rearrange("p (o d) -> p o d", o=1).broadcast_to([L, H, HD]),
                                        ALU.mult).then_inc(made, 1)
                dve.wait_ge(folded, 1)
                nc.vector.tensor_copy(S.a1_wk2[:], ps[:, 0, 0:P])
                nc.vector.tensor_copy(S.a1_bk2[:], ps[:, 1, 0:1])

            @block.tensor
            def _(pe):
                for h in range(H):
                    nc.tensor.matmul(ps[:, 0, h * HD:(h + 1) * HD], S.a1_wkl[:, h * P:(h + 1) * P], S.a1_wc[:],
                                     start=True, stop=True)
                pe.wait_ge(made, 1)
                nc.tensor.matmul(ps[:, 1, 0:1], outer[:], ones[:], start=True, stop=True).then_inc(folded, 1)


def causal_attention(nc, S):
    fold_latent_key(nc, S)
    project_qkv(nc, S, S.a1_wq, S.a1_bq, LATENT ** -0.5, S.a1_wk2, S.a1_bk2, S.a1_wv, S.a1_bv, LATENT)
    attend(nc, S, True, LATENT)
    wide_attention_output(nc, S, S.a1_wo, S.a1_bo)


def row_attention(nc, S):
    ctx, sb, sem, steps = scope(nc)
    with ctx:
        S.v_tok = sb("v_tok", [P, TOK])
        S.weight = sb("weight", [P, TILES * H])
        project_qkv(nc, S, S.b1_wq, S.b1_bq, HD ** -0.5, S.b1_wk, S.b1_bk, S.b1_wv, S.b1_bv, HD, keep_v=True)
        attention_row_sums(nc, S)
        weighted_values_output(nc, S, S.b1_wo, S.b1_bo)


def attention_row_sums(nc, S):
    ctx, sb, sem, steps = scope(nc)
    ps = S.ps
    KTS = SEQ // P
    LOADS = 16 * 2 * PARTS
    with ctx:
        qs = [sb(f"q_stack{n}", [P, SEQ], BF16) for n in range(4)]
        ks = [sb(f"k_stack{n}", [P, SEQ], BF16) for n in range(4)]
        neg_max = sb("neg_max", [P, 2, KTS])
        sums = sb("sums", [P, 2, KTS])
        inverse = sb("inverse", [P, 2, KTS])
        s_mm, maxed, summed, inverted, weighed = [steps(n) for n in "s_mm maxed summed inverted weighed".split()]
        loaded = [sem(f"loaded{n}") for n in range(4)]
        cleared = sem("cleared")
        weight = S.weight[:].rearrange("p (t h) -> p t h", h=H)

        def heads(eng, step):
            with eng.Fori(0, HEADS // 4) as turn:
                for c in range(4):
                    step(Head(turn, c))

        with nc.Block() as block:
            @block.tensor
            def _(pe):
                s_mm.open(pe)
                pe.wait_ge(cleared, 1)

                def step(i):
                    pe.wait_ge(loaded[i.slot(4)], (i.rounds(4) + 1) * LOADS)
                    for qt in range(KTS):
                        summed.wait(pe, i.times(KTS, qt - 4))
                        for c in (0, 1):
                            op = nc.tensor.matmul(ps[:, 2 * (qt % 4) + c, :], qs[i.slot(4)][:, qt * P:(qt + 1) * P],
                                                  ks[i.slot(4)][:, c * GROUP:(c + 1) * GROUP], start=True, stop=True)
                        op.then_inc(s_mm.sem, 1)

                heads(pe, step)

            @block.vector
            def _(dve):
                maxed.open(dve)
                inverted.open(dve)

                def invert(h):
                    weighed.wait(dve, h.times(1, -2))
                    nc.vector.reciprocal(inverse[:, h.slot(2), :], sums[:, h.slot(2), :]).then_inc(inverted.sem, 1)

                def step(i):
                    for qt in range(KTS):
                        s_mm.wait(dve, i.times(KTS, qt))
                        nc.vector.tensor_reduce(neg_max[:, i.slot(2), qt:qt + 1],
                                                ps[:, 2 * (qt % 4):2 * (qt % 4) + 2, :], AX.XY, ALU.max,
                                                negate=True).then_inc(maxed.sem, 1)
                    summed.wait(dve, i.times(KTS, KTS - 1))
                    invert(i)

                heads(dve, step)

            @block.scalar
            def _(act):
                summed.open(act)
                nc.scalar.activation(S.act_warm[:], S.eps[:], ACT.Exp)

                def step(i):
                    weighed.wait(act, i.times(1, -2))
                    for qt in range(KTS):
                        maxed.wait(act, i.times(KTS, qt))
                        s = ps[:, 2 * (qt % 4):2 * (qt % 4) + 2, :]
                        nc.scalar.activation(s, s, ACT.Exp, bias=neg_max[:, i.slot(2), qt:qt + 1],
                                             accum_out=sums[:, i.slot(2), qt:qt + 1]).then_inc(summed.sem, 1)

                heads(act, step)

            @block.gpsimd
            def _(pool):
                weighed.open(pool)
                for n in range(4):
                    nc.gpsimd.memset(qs[n][:], 0.0)
                    op = nc.gpsimd.memset(ks[n][:], 0.0)
                op.then_inc(cleared, 1)

                def step(i):
                    at = i.times(1)
                    inverted.wait(pool, at)
                    nc.gpsimd.tensor_tensor(weight[:, bass.ds(at // H * KTS, KTS), bass.ds(at % H, 1)]
                                            .rearrange("p t h -> p (t h)"), sums[:, i.slot(2), :],
                                            inverse[:, i.slot(2), :], ALU.mult).then_inc(weighed.sem, 1)

                heads(pool, step)

            @block.sync
            def _(sp):
                sp.wait_ge(cleared, 1)

                def step(i):
                    s_mm.wait(sp, i.times(KTS, -3 * KTS - 1))
                    load_stacks(sp, S, i, qs[i.slot(4)], ks[i.slot(4)], loaded[i.slot(4)])

                for c in range(4):
                    load_stacks(sp, S, Head(0, c), qs[c], ks[c], loaded[c])
                with sp.Fori(1, HEADS // 4) as turn:
                    for c in range(4):
                        step(Head(turn, c))


def weighted_values_output(nc, S, wo, bo):
    ctx, sb, sem, steps = scope(nc)
    ps = S.ps
    with ctx:
        y = sb("y", [P, 2, GROUP])
        yT = sb("yT", [P, 2, GROUP])
        y_ready, transposed, yT_ready, o_mm, x_biased, x_ready = [steps(n) for n in (
            "y_ready transposed yT_ready o_mm x_biased x_ready").split()]
        with nc.Block() as block:
            @block.tensor
            def _(pe):
                transposed.open(pe)
                o_mm.open(pe)
                with pe.Fori(0, BATCH) as b:
                    for s in (0, 1):
                        g = b * 2 + s
                        y_ready.wait(pe, g)
                        yT_ready.wait(pe, g - 2)
                        for k in range(GT):
                            op = nc.tensor.transpose(ps[:, s, k * P:(k + 1) * P], y[:, s, k * P:(k + 1) * P], S.ident[:])
                        op.then_inc(transposed.sem, 1)
                    for s in (0, 1):
                        g = b * 2 + s
                        yT_ready.wait(pe, g)
                        x_ready.wait(pe, g - 2)
                        for k in range(GT):
                            op = nc.tensor.matmul(ps[:, 2 + s, k * P:(k + 1) * P], yT[:, s, k * P:(k + 1) * P], wo[:],
                                                  start=True, stop=True)
                        op.then_inc(o_mm.sem, 1)

            @block.scalar
            def _(act):
                yT_ready.open(act)
                with act.Fori(0, BATCH) as b:
                    for s in (0, 1):
                        g = b * 2 + s
                        transposed.wait(act, g)
                        o_mm.wait(act, g - 2)
                        nc.scalar.activation(yT[:, s, :], ps[:, s, :], ACT.Copy).then_inc(yT_ready.sem, 1)

            @block.gpsimd
            def _(pool):
                x_biased.open(pool)
                with pool.Fori(0, GROUPS) as g:
                    x = S.x[:, cols(g * GROUP, GROUP)]
                    nc.gpsimd.tensor_tensor(x, x, bo[:], ALU.add).then_inc(x_biased.sem, 1)

            @block.vector
            def _(dve):
                y_ready.open(dve)
                x_ready.open(dve)
                with dve.Fori(0, BATCH) as b:
                    for s in (0, 1):
                        g = b * 2 + s
                        transposed.wait(dve, g - 2)
                        w = S.weight[:, cols(g * GT * H, GT * H)]
                        nc.vector.tensor_tensor(y[:, s, :].rearrange("p (h d) -> p h d", d=HD),
                                                S.v_tok[:, cols(g * GROUP, GROUP)].rearrange("p (h d) -> p h d", d=HD),
                                                bcast(w, HD), ALU.mult).then_inc(y_ready.sem, 1)
                    for s in (0, 1):
                        g = b * 2 + s
                        o_mm.wait(dve, g)
                        x_biased.wait(dve, g)
                        x = S.x[:, cols(g * GROUP, GROUP)]
                        nc.vector.tensor_tensor(x, x, ps[:, 2 + s, :], ALU.add).then_inc(x_ready.sem, 1)


def double_norm(nc, S):
    ctx, sb, sem, steps = scope(nc)
    with ctx:
        st = sb("bn", [P, TILES * 6])
        tmp = sb("bn_tmp", [P, 4, TILES])
        mean, rstd = sb("mean2", [P, TILES]), sb("rstd2", [P, TILES])
        once, bn, chain, var_ready, std_ready = sem("once"), sem("bn"), sem("chain"), sem("var_ready"), sem("std_ready")
        with nc.Block() as block:
            @block.vector
            def _(dve):
                with dve.Fori(0, GROUPS) as g:
                    for k in range(GT):
                        op = normalize_tile(nc, S, S.normed2[:, cols((g * GT + k) * P, P)], g * GT + k)
                    op.then_inc(once, 1)
                    dve.wait_ge(once, g + 1)
                    for k in range(GT):
                        op = nc.vector.bn_stats(st[:, cols((g * GT + k) * 6, 6)],
                                                S.normed2[:, cols((g * GT + k) * P, P)])
                    op.then_inc(bn, 1)
                dve.wait_ge(bn, GROUPS)
                c = Chain(dve, chain)
                stats_tail(nc, dve, c, st, tmp, mean, rstd, var_ready, std_ready)
                with dve.Fori(0, TILES) as t:
                    v = S.normed2[:, cols(t * P, P)]
                    nc.vector.tensor_scalar(v, v, mean[:, cols(t, 1)], rstd[:, cols(t, 1)], ALU.subtract, ALU.mult)

            @block.scalar
            def _(act):
                act.wait_ge(var_ready, 1)
                nc.scalar.activation(tmp[:, 1], tmp[:, 2], ACT.Sqrt, bias=S.eps[:], scale=1.0 / D).then_inc(std_ready, 1)


def route_best(nc, S):
    ctx, sb, sem, steps = scope(nc)
    ps = S.ps
    T, L, C = 0, 1, 2
    W = GT * E
    with ctx:
        xn = sb("xn", [P, 2, GROUP])
        xT = sb("xT", [P, 2, GROUP])
        mx, total = sb("mx", [P, GT]), sb("total", [P, GT])
        logits, exped, gates, work = sb("logits", [P, W]), sb("exped", [P, W]), sb("gates", [P, W]), sb("work", [P, W])
        best, mask = sb("best", [P, TILES * E]), sb("mask", [P, W], BF16)
        count, cum = sb("count", [P, E]), sb("cum", [P, W])
        rank = sb("rank", [P, TILES])
        filled = sb("filled", [P, E, TILES])
        tiles_of, base = sb("tiles_of", [P, E]), sb("base", [P, E])
        ones = sb("ones", [P, E])
        at = sb("at", [P, TILES * E])
        slot_f, expert_f = sb("slot_f", [P, TILES]), sb("expert_f", [P, SLOT_TILES])
        reached = sb("reached", [P, SLOT_TILES, E - 1])
        chain = sem("chain")
        normed, transposed, xT_ready, l_mm, shifted, exp_done, masked, counted, counts_read = [steps(n) for n in (
            "normed transposed xT_ready l_mm shifted exp_done masked counted counts_read").split()]
        LINKS = 13
        with nc.Block() as block:
            @block.tensor
            def _(pe):
                for s in (transposed, l_mm, counted):
                    s.open(pe)
                with pe.Fori(0, BATCH) as b:
                    for s in (0, 1):
                        g = b * 2 + s
                        normed.wait(pe, g)
                        xT_ready.wait(pe, g - 1)
                        for k in range(GT):
                            op = nc.tensor.transpose(ps[:, T, k * P:(k + 1) * P], xn[:, s, k * P:(k + 1) * P], S.ident[:])
                        op.then_inc(transposed.sem, 1)
                    for s in (0, 1):
                        g = b * 2 + s
                        xT_ready.wait(pe, g)
                        shifted.wait(pe, g - 1)
                        for k in range(GT):
                            op = nc.tensor.matmul(ps[:, L, k * E:(k + 1) * E], xT[:, s, k * P:(k + 1) * P], S.f1_wr[:],
                                                  start=True, stop=True)
                        op.then_inc(l_mm.sem, 1)
                    for s in (0, 1):
                        g = b * 2 + s
                        masked.wait(pe, g)
                        counts_read.wait(pe, g - 1)
                        count_matmuls(nc, S, ps[:, C, :], mask[:]).then_inc(counted.sem, 1)

            @block.scalar
            def _(act):
                xT_ready.open(act)
                exp_done.open(act)
                nc.scalar.activation(S.act_warm[:], S.eps[:], ACT.Exp)
                with act.Fori(0, BATCH) as b:
                    for s in (0, 1):
                        transposed.wait(act, b * 2 + s)
                        nc.scalar.activation(xT[:, s, :], ps[:, T, :], ACT.Copy).then_inc(xT_ready.sem, 1)
                    for s in (0, 1):
                        shifted.wait(act, b * 2 + s)
                        nc.scalar.activation(exped[:], exped[:], ACT.Exp).then_inc(exp_done.sem, 1)

            @block.vector
            def _(dve):
                for s in (normed, shifted, masked, counts_read):
                    s.open(dve)
                c0 = Chain(dve, chain)
                nc.vector.memset(ones[:], 1.0)
                c0.run(nc.vector.memset(count[:], 0.0))
                with dve.Fori(0, BATCH) as b:
                    for s in (0, 1):
                        g = b * 2 + s
                        transposed.wait(dve, g - 2)
                        for k in range(GT):
                            op = normalize_tile(nc, S, xn[:, s, k * P:(k + 1) * P], g * GT + k)
                        op.then_inc(normed.sem, 1)
                    for s in (0, 1):
                        g = b * 2 + s
                        c = Chain(dve, chain, g, LINKS, 1)
                        l_mm.wait(dve, g)
                        c.run(nc.vector.tensor_tensor(logits[:], ps[:, L, 0:W], S.f1_br[:], ALU.add))
                        softmax_start(nc, dve, c, by_tile(logits[:]), mx[:], exped[:]).then_inc(shifted.sem, 1)
                        exp_done.wait(dve, g)
                        softmax_end(nc, c, exped[:], total[:], gates[:])
                        pick_largest(nc, S, c, gates[:], mx[:], work[:], mask[:], S.gate[:, cols(g * GT, GT)])
                        nc.vector.tensor_copy(best[:, cols(g * W, W)], mask[:]).then_inc(masked.sem, 1)
                        counted.wait(dve, g)
                        c.run(nc.vector.tensor_tensor(by_tile(cum[:]), by_tile(ps[:, C, 0:W]),
                                                      count[:].rearrange("p (o e) -> p o e", o=1).broadcast_to([P, GT, E]),
                                                      ALU.add))
                        nc.vector.tensor_tensor(count[:], count[:], ps[:, C, W:W + E], ALU.add).then_inc(counts_read.sem, 1)
                        counts_read.wait(dve, g)
                        c.run(nc.vector.tensor_tensor(work[:], cum[:], mask[:], ALU.mult))
                        c.run(nc.vector.tensor_reduce(rank[:, cols(g * GT, GT)], by_tile(work[:]), AX.X, ALU.add))
                        assert c.n == LINKS, c.n
                c = Chain(dve, chain, 0, 0, 1 + LINKS * GROUPS)
                c.run(nc.vector.tensor_tensor(filled[:], bcast(count[:], TILES),
                                              S.tile_start[:, 0:TILES].rearrange("p (o k) -> p o k", o=1)
                                              .broadcast_to([P, E, TILES]), ALU.is_gt))
                c.run(nc.vector.tensor_reduce(tiles_of[:], filled[:], AX.X, ALU.add))
                c.run(nc.vector.tensor_tensor_scan(base[:], ones[:], tiles_of[:], 0.0, ALU.mult, ALU.add))
                c.run(nc.vector.tensor_tensor(base[:], base[:], tiles_of[:], ALU.subtract))
                c.run(nc.vector.tensor_scalar(base[:], base[:], float(P), None, ALU.mult))
                c.run(nc.vector.tensor_tensor(at[:].rearrange("p (t e) -> p t e", e=E),
                                              best[:].rearrange("p (t e) -> p t e", e=E),
                                              base[:].rearrange("p (o e) -> p o e", o=1).broadcast_to([P, TILES, E]),
                                              ALU.mult))
                c.run(nc.vector.tensor_reduce(slot_f[:], at[:].rearrange("p (t e) -> p t e", e=E), AX.X, ALU.add))
                c.run(nc.vector.scalar_tensor_tensor(slot_f[:], slot_f[:], -1.0, rank[:], ALU.add, ALU.add))
                nc.vector.tensor_copy(S.slot[:], slot_f[:])
                c.run(nc.vector.tensor_tensor(reached[:], bcast(S.tile_start[:], E - 1),
                                              base[:, 1:E].rearrange("p (o e) -> p o e", o=1)
                                              .broadcast_to([P, SLOT_TILES, E - 1]), ALU.is_ge))
                c.run(nc.vector.tensor_reduce(expert_f[:], reached[:], AX.X, ALU.add))
                nc.vector.tensor_copy(S.tile_expert[:], expert_f[:])


def expert_tiles(nc, S):
    ctx, sb, sem, steps = scope(nc)
    ps = S.ps
    F = 4 * P
    FC = F // P
    XB, HB, TB, YB = (0, 1), (2, 3), (4, 5), (6, 7)
    with ctx:
        xs = sb("xs", [P, 2, P])
        xsT = sb("xsT", [P, 2, P])
        h = sb("h", [P, 2, F])
        hT = sb("hT", [P, 2, F])
        y = sb("y", [P, 2, P])
        back = sb("back", [P, TOK])
        scattered, gathered = sem("scattered"), sem("gathered")
        loaded = [sem("loaded0"), sem("loaded1")]
        stored = [sem("stored0"), sem("stored1")]
        x_mm, xT_ready, h_mm, h_ready, hT_mm, hT_ready, y_mm, y_ready = [steps(n) for n in (
            "x_mm xT_ready h_mm h_ready hT_mm hT_ready y_mm y_ready").split()]
        with nc.Block() as block:
            @block.gpsimd
            def _(pool):
                for t in range(TILES):
                    nc.gpsimd.indirect_dma_start(
                        S.x_slots[:, :], bass.IndirectOffsetOnAxis(ap=S.slot[:, t:t + 1], axis=0),
                        S.normed2[:, t * P:(t + 1) * P], None).then_inc(scattered, 16)
                pool.wait_ge(scattered, 16 * TILES)

            @block.sync
            def _(sp):
                sp.wait_ge(scattered, 16 * TILES)

                def load(j, s):
                    sp.dma_start(xs[:, s, :], S.x_slots[bass.ds(j * P, P), :]).then_inc(loaded[s], 16)

                def store(j, s):
                    y_ready.wait(sp, j)
                    sp.dma_start(S.y_slots[bass.ds(j * P, P), :], y[:, s, :]).then_inc(stored[s], 16)

                for s in (0, 1):
                    load(s, s)
                with sp.Fori(1, SLOT_TILES // 2) as m:
                    for s in (0, 1):
                        x_mm.wait(sp, m * 2 + (s - 2))
                        load(m * 2 + s, s)
                    for s in (0, 1):
                        store(m * 2 + (s - 2), s)
                for s in (0, 1):
                    store(SLOT_TILES - 2 + s, s)
                for s in (0, 1):
                    sp.wait_ge(stored[s], 16 * SLOT_TILES // 2)

            @block.tensor
            def _(pe):
                for s in (x_mm, h_mm, hT_mm, y_mm):
                    s.open(pe)

                def turn(m):
                    e = [pe.value_load(S.tile_expert[0:1, bass.ds(m * 2 + s, 1)], min_val=0, max_val=E - 1)
                         for s in (0, 1)]
                    for s in (0, 1):
                        j = m * 2 + s
                        pe.wait_ge(loaded[s], m * 16 + 16)
                        xT_ready.wait(pe, j - 2)
                        nc.tensor.transpose(ps[:, XB[s], 0:P], xs[:, s, :], S.ident[:]).then_inc(x_mm.sem, 1)
                    for s in (0, 1):
                        j = m * 2 + s
                        xT_ready.wait(pe, j)
                        h_ready.wait(pe, j - 2)
                        nc.tensor.matmul(ps[:, HB[s], :], xsT[:, s, :], S.f1_w1[:, cols(e[s] * F, F)], start=True,
                                         stop=True).then_inc(h_mm.sem, 1)
                    for s in (0, 1):
                        j = m * 2 + s
                        h_ready.wait(pe, j)
                        hT_ready.wait(pe, j - 2)
                        for f in range(FC):
                            op = nc.tensor.transpose(ps[:, TB[s], f * P:(f + 1) * P], h[:, s, f * P:(f + 1) * P],
                                                     S.ident[:])
                        op.then_inc(hT_mm.sem, 1)
                    for s in (0, 1):
                        j = m * 2 + s
                        hT_ready.wait(pe, j)
                        y_ready.wait(pe, j - 2)
                        for f in range(FC):
                            op = nc.tensor.matmul(ps[:, YB[s], 0:P], hT[:, s, f * P:(f + 1) * P],
                                                  S.f1_w2[:, cols(e[s] * F + f * P, P)], start=(f == 0),
                                                  stop=(f == FC - 1))
                        op.then_inc(y_mm.sem, 1)

                with pe.Fori(0, SLOT_TILES // 2) as m:
                    turn(m)

            @block.scalar
            def _(act):
                xT_ready.open(act)
                hT_ready.open(act)
                with act.Fori(0, SLOT_TILES // 2) as m:
                    for s in (0, 1):
                        j = m * 2 + s
                        x_mm.wait(act, j)
                        h_mm.wait(act, j - 2)
                        nc.scalar.activation(xsT[:, s, :], ps[:, XB[s], 0:P], ACT.Identity, bias=S.f1_lnb[:],
                                             scale=S.f1_lng[:]).then_inc(xT_ready.sem, 1)
                    for s in (0, 1):
                        j = m * 2 + s
                        hT_mm.wait(act, j)
                        y_mm.wait(act, j - 2)
                        nc.scalar.activation(hT[:, s, :], ps[:, TB[s], :], ACT.Relu).then_inc(hT_ready.sem, 1)

            @block.vector
            def _(dve):
                h_ready.open(dve)
                y_ready.open(dve)

                def turn(m, first):
                    e = [dve.value_load(S.tile_expert[0:1, bass.ds(m * 2 + s, 1)], min_val=0, max_val=E - 1)
                         for s in (0, 1)]
                    for s in (0, 1):
                        j = m * 2 + s
                        h_mm.wait(dve, j)
                        hT_mm.wait(dve, j - 2)
                        nc.vector.tensor_tensor(h[:, s, :], ps[:, HB[s], :], S.f1_b1[:, cols(e[s] * F, F)],
                                                ALU.add).then_inc(h_ready.sem, 1)
                    for s in (0, 1):
                        j = m * 2 + s
                        y_mm.wait(dve, j)
                        if not first:
                            dve.wait_ge(stored[s], m * 16)
                        nc.vector.tensor_tensor(y[:, s, :], ps[:, YB[s], 0:P], S.f1_b2[:, cols(e[s] * P, P)],
                                                ALU.add).then_inc(y_ready.sem, 1)

                turn(0, True)
                with dve.Fori(1, SLOT_TILES // 2) as m:
                    turn(m, False)
        with nc.Block() as block:
            @block.gpsimd
            def _(pool):
                for t in range(TILES):
                    nc.gpsimd.indirect_dma_start(
                        back[:, t * P:(t + 1) * P], None, S.y_slots[:, :],
                        bass.IndirectOffsetOnAxis(ap=S.slot[:, t:t + 1], axis=0)).then_inc(gathered, 16)
                pool.wait_ge(gathered, 16 * TILES)

            @block.vector
            def _(dve):
                dve.wait_ge(gathered, 16 * TILES)
                with dve.Fori(0, TILES) as t:
                    x = S.x[:, cols(t * P, P)]
                    nc.vector.scalar_tensor_tensor(x, back[:, cols(t * P, P)], S.gate[:, cols(t, 1)], x, ALU.mult,
                                                   ALU.add)


def best_expert_ffn(nc, S):
    ctx, sb, sem, steps = scope(nc)
    with ctx:
        S.normed2 = sb("normed2", [P, TOK])
        S.gate = sb("gate", [P, TILES])
        S.slot = sb("slot", [P, TILES], I32)
        S.tile_expert = sb("tile_expert", [P, SLOT_TILES], I32)
        double_norm(nc, S)
        route_best(nc, S)
        expert_tiles(nc, S)


def program(nc, a, out, start=0, upto=8):
    S = Shared()
    with ExitStack() as ctx:
        loads = []

        def sb(name, shape, dt=F32):
            return ctx.enter_context(nc.sbuf_tensor(name, shape, dt))

        def weight(name, shape, src=None):
            t = sb("w_" + name, shape)
            loads.append((t[:], a[name] if src is None else src))
            return t

        def column(name):
            return weight(name + "_col", [P, 1], a[name].rearrange("(p o) -> p o", o=1))

        def row(name, times=1):
            n = a[name].shape[0]
            t = sb("w_" + name + "_row", [P, times * n])
            for i in range(times):
                loads.append((t[:, i * n:(i + 1) * n], a[name].partition_broadcast(P)))
            return t

        S.ps = ctx.enter_context(nc.psum_tensor("ps", [P, 8, 512], F32))
        S.x = sb("x_res", [P, TOK])
        loads.append((S.x[:].rearrange("p (t d) -> p t d", d=D), a["x"].rearrange("(t p) d -> p t d", p=P)))
        S.mean, S.rstd = sb("mean", [P, TILES]), sb("rstd", [P, TILES])
        S.eps, S.act_warm = sb("eps", [P, 1]), sb("act_warm", [P, 1])
        S.ident, S.ident_b = sb("ident", [P, P]), sb("ident_b", [P, P], BF16)
        S.head_mask = sb("head_mask", [P, P])
        S.prefix, S.ones_b = sb("prefix", [P, P], BF16), sb("ones_b", [P, P], BF16)
        S.mask_qk, S.mask_kq = sb("mask_qk", [P, P], BF16), sb("mask_kq", [P, P], BF16)
        S.first_rank = sb("first_rank", [P, GT * E])
        S.tile_start = sb("tile_start", [P, SLOT_TILES])

        S.a0_wq, S.a0_wkv, S.a0_wc = weight("a0_wqT", [P, D]), weight("a0_wkvT", [P, 2 * D]), weight("a0_wcT", [P, D])
        S.a0_bq, S.a0_bkv, S.a0_bc = column("a0_bq"), row("a0_bkv", 2), row("a0_bc", GT)
        S.a0_bq1 = sb("a0_bq1", [P, 1])

        S.f0_wr, S.f0_wg = weight("f0_wrT", [P, E]), weight("f0_wgT", [P, 2 * P])
        S.f0_wd = sb("f0_wd", [P, 2, E * D])
        loads.append((S.f0_wd[:], a["f0_wdT"].rearrange("(f p) n -> p f n", p=P)))

        S.b0_wq, S.b0_wk, S.b0_wv = weight("b0_wqT", [P, D]), weight("b0_wkT", [P, D]), weight("b0_wvT", [P, D])
        S.b0_bq, S.b0_bk, S.b0_bv = column("b0_bq"), column("b0_bk"), row("b0_bv", GT)
        S.b0_wo, S.b0_bo = weight("b0_woT", [P, D]), row("b0_bo", GT)

        S.a1_wq, S.a1_bq, S.a1_wkl = weight("a1_wq", [P, D]), column("a1_bq"), weight("a1_wkl", [LATENT, H * D])
        S.a1_bkl, S.a1_wc = weight("a1_bkl", [LATENT, H]), weight("a1_wcT", [LATENT, HD])
        S.a1_wk2, S.a1_bk2 = sb("a1_wk2", [P, P]), sb("a1_bk2", [P, 1])
        S.a1_wv, S.a1_bv = weight("a1_wv", [P, H * LATENT]), row("a1_bv")
        S.a1_wo = sb("a1_wo", [P, H * LATENT // P, D])
        loads.append((S.a1_wo[:], a["a1_wo"].rearrange("(f p) n -> p f n", p=P)))
        S.a1_bo = row("a1_bo", GT)
        S.b1_wq, S.b1_wk, S.b1_wv = weight("b1_wqT", [P, D]), weight("b1_wkT", [P, D]), weight("b1_wvT", [P, D])
        S.b1_bq, S.b1_bk, S.b1_bv = column("b1_bq"), column("b1_bk"), row("b1_bv", GT)
        S.b1_wo, S.b1_bo = weight("b1_woT", [P, D]), row("b1_bo", GT)
        S.f1_wr, S.f1_br = weight("f1_wr", [P, E]), row("f1_br", GT)
        S.f1_lng, S.f1_lnb = column("f1_lng"), column("f1_lnb")
        S.f1_w1, S.f1_b1 = weight("f1_w1", [P, E * 4 * P]), row("f1_b1")
        S.f1_w2, S.f1_b2 = weight("f1_w2", [P, E * 4 * P]), row("f1_b2")
        S.zeros = sb("zeros", [P, D])

        S.x_slots = nc.dram_tensor("x_slots", [SLOT_TILES * P, D], F32)
        S.y_slots = nc.dram_tensor("y_slots", [SLOT_TILES * P, D], F32)
        S.q_parts = nc.dram_tensor("q_parts", [BATCH, PARTS, H, HD, SEQ], BF16)
        S.k_parts = nc.dram_tensor("k_parts", [BATCH, PARTS, H, HD, SEQ], BF16)
        S.v_heads = nc.dram_tensor("v_heads", [HEADS, P, LATENT * SEQ // P], F32)
        S.o_quads = nc.dram_tensor("o_quads", [HEADS, P, GROUP], F32)
        S.o_wide = nc.dram_tensor("o_wide", [HEADS, LATENT + 1, SEQ], F32)
        S.r_wide = nc.dram_tensor("r_wide", [2, HEADS, GROUP], F32)
        S.r_sums = nc.dram_tensor("r_sums", [HEADS, 2, GROUP], F32)

        load_phase(nc, S, loads)
        with nc.Block() as block:
            @block.vector
            def _(dve):
                nc.vector.tensor_scalar(S.a0_bq1[:], S.a0_bq[:], 1.0, None, ALU.add)
                nc.vector.memset(S.eps[:], EPS)
        layers = (linear_attention, routed_pair_ffn, full_attention, routed_pair_ffn,
                  causal_attention, best_expert_ffn, row_attention, best_expert_ffn)
        for layer in layers[start:upto]:
            norm_stats(nc, S)
            layer(nc, S)
        store_phase(nc, S, out)


SLOT_TILES = 40


def arrays_of(i):
    import numpy as np

    def T(w):
        return np.ascontiguousarray(w.T)

    g = {k: np.asarray(v) for k, v in i.items()}
    w_in = g["L1_attn_b_w_in"].reshape(H, PARTS, HD, D)
    b_in = g["L1_attn_b_b_in"].reshape(H, PARTS, HD)
    return {
        **{f"b1_w{c}T": T(w_in[:, n].reshape(D, D)) for n, c in enumerate("qkv")},
        **{f"b1_b{c}": b_in[:, n].reshape(D) for n, c in enumerate("qkv")},
        "b1_woT": T(g["L1_attn_b_w_out"]),
        "b1_bo": g["L1_attn_b_b_out"],
        "a1_wq": g["L1_attn_a_Wq"],
        "a1_bq": g["L1_attn_a_bq"],
        "a1_wkl": g["L1_attn_a_Wk"].reshape(D, H, LATENT).transpose(2, 1, 0).reshape(LATENT, H * D),
        "a1_bkl": T(g["L1_attn_a_bk"].reshape(H, LATENT)),
        "a1_wcT": T(g["L1_attn_a_Wc"]),
        "a1_wv": g["L1_attn_a_Wv"],
        "a1_bv": g["L1_attn_a_bv"],
        "a1_wo": g["L1_attn_a_Wo"],
        "a1_bo": g["L1_attn_a_bo"],
        "f1_wr": g["L1_ffn_Wr"],
        "f1_br": g["L1_ffn_br"],
        "f1_lng": g["L1_ffn_ln_g"],
        "f1_lnb": g["L1_ffn_ln_b"],
        "f1_w1": g["L1_ffn_W1"].transpose(1, 0, 2).reshape(D, E * 4 * P),
        "f1_b1": g["L1_ffn_b1"].reshape(E * 4 * P),
        "f1_w2": g["L1_ffn_W2"].reshape(E, 4, P, D).transpose(2, 0, 1, 3).reshape(P, E * 4 * D),
        "f1_b2": g["L1_ffn_b2"].reshape(E * D),
        "x": g["L0_attn_a_x"].reshape(TOK, D),
        "a0_wqT": T(g["L0_attn_a_Wq"]),
        "a0_wkvT": np.concatenate([T(g["L0_attn_a_Wk"]), T(g["L0_attn_a_Wv"])], axis=1),
        "a0_bkv": np.concatenate([g["L0_attn_a_bk"], g["L0_attn_a_bv"]]),
        "a0_bq": g["L0_attn_a_bq"],
        "a0_wcT": T(g["L0_attn_a_Wc"]),
        "a0_bc": g["L0_attn_a_bc"],
        **{f"b0_w{c}T": T(g[f"L0_attn_b_W{c}"]) for c in "qkvo"},
        **{f"b0_b{c}": g[f"L0_attn_b_b{c}"] for c in "qkvo"},
        "f0_wrT": T(g["L0_ffn_w_router"]),
        "f0_wgT": T(g["L0_ffn_w_gate"]),
        "f0_wdT": np.ascontiguousarray(g["L0_ffn_w_down"].transpose(2, 0, 1)).reshape(2 * P, E * D),
    }


def kernel(**inputs):
    import numpy as np
    import concourse.bacc as bacc
    from concourse.bass_utils import run_bass_kernel_spmd

    nc = bacc.Bacc("TRN2", target_bir_lowering=False, num_devices=1)
    arrays = {f"in_{k}": v for k, v in arrays_of(inputs).items()}
    a = {k[3:]: nc.dram_tensor(k, v.shape, mybir.dt.from_np(v.dtype), kind="ExternalInput").ap()
         for k, v in arrays.items()}
    out = nc.dram_tensor("out", (BATCH, SEQ, D), F32, kind="ExternalOutput").ap()
    program(nc, a, out)
    r = run_bass_kernel_spmd(nc, [arrays], core_ids=[0])
    return r.results[0]["out"]
```

```python
import concourse.bass as bass
from concourse import mybir
from contextlib import ExitStack

F32 = mybir.dt.float32
BF16 = mybir.dt.bfloat16
I32 = mybir.dt.int32
ALU = mybir.AluOpType
ACT = mybir.ActivationFunctionType
AX = mybir.AxisListType

P = 128
BATCH, SEQ, D = 4, 1024, 128
TOK = BATCH * SEQ
TILES = TOK // P
GROUP = 512
GROUPS = TOK // GROUP
GT = GROUP // P
PAIRS = GROUPS // 2
H, HD = 16, 8
E = 8
EPS = 1e-5


class Chain:

    def __init__(self, eng, sem, turn=0, per_turn=0, before=0):
        self.eng, self.sem, self.turn, self.per_turn, self.before, self.n = eng, sem, turn, per_turn, before, 0

    def run(self, op):
        self.n += 1
        op.then_inc(self.sem, 1)
        self.eng.wait_ge(self.sem, self.turn * self.per_turn + self.before + self.n)

    def end(self):
        assert self.per_turn == 0 or self.n == self.per_turn, self.n


def cols(start, n):
    return bass.ds(start, n)


LEAD = 8


class Steps:

    def __init__(self, sem):
        self.sem = sem

    def open(self, eng):
        eng.sem_inc(self.sem, LEAD)

    def after(self, n):
        return n + (LEAD + 1)

    def wait(self, eng, n):
        eng.wait_ge(self.sem, self.after(n))


class Shared:
    pass


def scope(nc):
    ctx = ExitStack()
    phase = nc.next_id()

    def sb(name, shape, dt=F32):
        return ctx.enter_context(nc.sbuf_tensor(f"{name}_{phase}", shape, dt))

    sems = []

    def close():
        if sems:
            nc.clear_and_free_semaphores(sems)
            nc.all_engine_barrier()

    ctx.callback(close)

    def sem(name):
        sems.append(nc.alloc_semaphore(f"{name}_{phase}"))
        return sems[-1]

    def steps(name):
        return Steps(sem(name))

    return ctx, sb, sem, steps


def load_phase(nc, S, loads):
    ctx, sb, sem, steps = scope(nc)
    with ctx:
        loaded, made = sem("loaded"), sem("made")
        with nc.Block() as block:
            @block.sync
            def _(sp):
                for dst, src in loads:
                    sp.dma_start(dst, src).then_inc(loaded, 16)
                sp.wait_ge(loaded, 16 * len(loads))

            @block.gpsimd
            def _(pool):
                c = Chain(pool, made)
                for m in (S.ident, S.ident_b):
                    c.run(nc.gpsimd.memset(m[:], 0.0))
                    c.run(nc.gpsimd.affine_select(out=m[:], in_=m[:], compare_op=ALU.not_equal, fill=1.0, base=0,
                                                  pattern=[[-1, P]], channel_multiplier=1))
                c.run(nc.gpsimd.memset(S.zeros[:], 0.0))
                c.run(nc.gpsimd.memset(S.head_mask[:], 1.0))
                v = S.head_mask[:].rearrange("p (h d) -> p h d", h=H)
                c.run(nc.gpsimd.affine_select(out=v, in_=v, compare_op=ALU.is_ge, fill=0.0, base=0,
                                              pattern=[[-HD, H], [0, HD]], channel_multiplier=1))
                c.run(nc.gpsimd.affine_select(out=v, in_=v, compare_op=ALU.is_ge, fill=0.0, base=HD - 1,
                                              pattern=[[HD, H], [0, HD]], channel_multiplier=-1))
                c.run(nc.gpsimd.memset(S.prefix[:], 1.0))
                c.run(nc.gpsimd.affine_select(out=S.prefix[:], in_=S.prefix[:], compare_op=ALU.is_ge, fill=0.0,
                                              base=0, pattern=[[1, P]], channel_multiplier=-1))
                c.run(nc.gpsimd.memset(S.ones_b[:], 1.0))
                for m, sign in ((S.mask_qk, -1), (S.mask_kq, 1)):
                    c.run(nc.gpsimd.memset(m[:], 0.0))
                    c.run(nc.gpsimd.affine_select(out=m[:], in_=m[:], compare_op=ALU.is_ge, fill=MASKED, base=0,
                                                  pattern=[[sign, P]], channel_multiplier=-sign))
                c.run(nc.gpsimd.iota(S.first_rank[:], pattern=[[0, TILES], [-1, E]], base=E, channel_multiplier=0,
                                     allow_small_or_imprecise_dtypes=True))
                c.run(nc.gpsimd.memset(S.carry_on[:], 1.0))
                c.run(nc.gpsimd.memset(S.carry_on[:].rearrange("p (e t) -> p e t", e=E)[:, :, 0:1], 0.0))
                c.run(nc.gpsimd.iota(S.tile_start[:], pattern=[[P, S.tile_start.shape[1]]], base=0,
                                     channel_multiplier=0, allow_small_or_imprecise_dtypes=True))


MASKED = -3.0e38


def stats_tail(nc, dve, c, st, tmp, mean, rstd, var_ready, std_ready):
    stv = st[:].rearrange("p (t s) -> p s t", s=6)
    c.run(nc.vector.tensor_tensor(tmp[:, 1], stv[:, 1], stv[:, 4], ALU.subtract))
    nc.vector.tensor_tensor(tmp[:, 2], stv[:, 2], stv[:, 5], ALU.add)
    c.run(nc.vector.tensor_tensor(tmp[:, 0], stv[:, 1], stv[:, 4], ALU.add))
    nc.vector.tensor_scalar(mean[:], tmp[:, 0], 0.5, None, ALU.mult)
    c.run(nc.vector.tensor_tensor(tmp[:, 3], tmp[:, 1], tmp[:, 1], ALU.mult))
    nc.vector.scalar_tensor_tensor(tmp[:, 2], tmp[:, 3], float(D // 4), tmp[:, 2], ALU.mult,
                                   ALU.add).then_inc(var_ready, 1)
    dve.wait_ge(std_ready, 1)
    c.run(nc.vector.reciprocal(rstd[:], tmp[:, 1]))


def norm_stats(nc, S):
    ctx, sb, sem, steps = scope(nc)
    with ctx:
        st = sb("bn", [P, TILES * 6])
        tmp = sb("bn_tmp", [P, 4, TILES])
        bn, chain, var_ready, std_ready = sem("bn"), sem("chain"), sem("var_ready"), sem("std_ready")
        with nc.Block() as block:
            @block.vector
            def _(dve):
                with dve.Fori(0, GROUPS) as g:
                    for k in range(GT):
                        op = nc.vector.bn_stats(st[:, cols((g * GT + k) * 6, 6)], S.x[:, cols((g * GT + k) * P, P)])
                    op.then_inc(bn, 1)
                dve.wait_ge(bn, GROUPS)
                stats_tail(nc, dve, Chain(dve, chain), st, tmp, S.mean, S.rstd, var_ready, std_ready)

            @block.scalar
            def _(act):
                act.wait_ge(var_ready, 1)
                nc.scalar.activation(tmp[:, 1], tmp[:, 2], ACT.Sqrt, bias=S.eps[:], scale=1.0 / D).then_inc(std_ready, 1)


def normalize_tile(nc, S, out, t):
    return nc.vector.tensor_scalar(out, S.x[:, cols(t * P, P)], S.mean[:, cols(t, 1)], S.rstd[:, cols(t, 1)],
                                   ALU.subtract, ALU.mult)


def linear_attention(nc, S):
    ctx, sb, sem, steps = scope(nc)
    ps = S.ps
    VA = 2 * P + 1
    SW = P + H
    with ctx:
        xn = sb("xn", [P, 2, GROUP])
        xT = sb("xT", [P, 2, GROUP])
        qT = sb("qT", [P, 2, GROUP])
        qneg = sb("qneg", [P, 2, GROUP])
        kv = sb("kv", [P, 2, GT, VA])
        kneg = sb("kneg", [P, 2, GT, P])
        ksum = sb("ksum", [P, 1])
        state = sb("state", [P, SW])
        den = sb("den", [P, GT * H])
        y = sb("y", [P, 2, GROUP])
        yT = sb("yT", [P, 2, GROUP])
        chain, late_loaded, cleared = sem("chain"), sem("late_loaded"), sem("cleared")
        (normed, transposed, xT_ready, q_mm, q_neg, q_exp, q_ready, kv_mm, kv_biased, k_exp, k_ready, s_mm, s_ready,
         n_mm, y_ready, yT_mm, yT_ready, o_mm, x_ready, x_biased) = [steps(n) for n in (
             "normed transposed xT_ready q_mm q_neg q_exp q_ready kv_mm kv_biased k_exp k_ready s_mm s_ready "
             "n_mm y_ready yT_mm yT_ready o_mm x_ready x_biased").split()]
        T, Q, KV, ST, NUM, YT = 0, 1, (2, 3), 4, (5, 6), 7
        with nc.Block() as block:
            @block.sync
            def _(sp):
                for dst, src in S.late_loads:
                    sp.dma_start(dst, src).then_inc(late_loaded, 16)
                sp.dma_start(S.x_slots[:, :].rearrange("(t p) d -> p t d", p=P),
                             S.zeros[:].rearrange("p (o d) -> p o d", o=1).broadcast_to([P, SLOT_TILES, D])
                             ).then_inc(cleared, 16)
                sp.wait_ge(late_loaded, 16 * len(S.late_loads))
                sp.wait_ge(cleared, 16)

            @block.tensor
            def _(pe):
                for s in (transposed, q_mm, kv_mm, s_mm, n_mm, yT_mm, o_mm):
                    s.open(pe)
                with pe.Fori(0, BATCH) as b:
                    for s in (0, 1):
                        g = b * 2 + s
                        normed.wait(pe, g)
                        xT_ready.wait(pe, g - 1)
                        for k in range(GT):
                            op = nc.tensor.transpose(ps[:, T, k * P:(k + 1) * P], xn[:, s, k * P:(k + 1) * P], S.ident[:])
                        op.then_inc(transposed.sem, 1)
                        xT_ready.wait(pe, g)
                        q_ready.wait(pe, g - 1)
                        nc.tensor.matmul(ps[:, Q, :], S.a0_wq[:], xT[:, s, :], start=True, stop=True).then_inc(q_mm.sem, 1)
                        for half in (0, 1):
                            kv_biased.wait(pe, g * 2 + half - 2)
                            for k in (0, 1):
                                op = nc.tensor.matmul(ps[:, KV[half], k * 2 * P:(k + 1) * 2 * P],
                                                      xT[:, s, (2 * half + k) * P:(2 * half + k + 1) * P],
                                                      S.a0_wkv[:], start=True, stop=True)
                            op.then_inc(kv_mm.sem, 1)
                    x_ready.wait(pe, b * 2 - 1)
                    for s in (0, 1):
                        k_ready.wait(pe, b * 2 + s)
                        for k in range(GT):
                            op = nc.tensor.matmul(ps[:, ST, 0:P + 1], kv[:, s, k, 0:P], kv[:, s, k, P:VA],
                                                  start=(s == 0 and k == 0), stop=(s == 1 and k == GT - 1))
                    op.then_inc(s_mm.sem, 1)
                    s_ready.wait(pe, b)
                    for s in (0, 1):
                        g = b * 2 + s
                        q_ready.wait(pe, g)
                        for half in (0, 1):
                            y_ready.wait(pe, g * 2 + half - 2)
                            for k in (0, 1):
                                op = nc.tensor.matmul(ps[:, NUM[half], k * SW:(k + 1) * SW],
                                                      qT[:, s, (2 * half + k) * P:(2 * half + k + 1) * P],
                                                      state[:], start=True, stop=True)
                            op.then_inc(n_mm.sem, 1)
                    for s in (0, 1):
                        g = b * 2 + s
                        y_ready.wait(pe, g * 2 + 1)
                        yT_ready.wait(pe, g - 1)
                        for k in range(GT):
                            op = nc.tensor.transpose(ps[:, YT, k * P:(k + 1) * P], y[:, s, k * P:(k + 1) * P], S.ident[:])
                        op.then_inc(yT_mm.sem, 1)
                        yT_ready.wait(pe, g)
                        x_ready.wait(pe, g - 1)
                        for k in range(GT):
                            op = nc.tensor.matmul(ps[:, ST, k * P:(k + 1) * P], yT[:, s, k * P:(k + 1) * P],
                                                  S.a0_wc[:], start=True, stop=True)
                        op.then_inc(o_mm.sem, 1)

            @block.scalar
            def _(act):
                for s in (xT_ready, q_exp, k_exp, yT_ready):
                    s.open(act)
                nc.scalar.activation(S.act_warm[:], S.eps[:], ACT.Exp)
                with act.Fori(0, BATCH) as b:
                    for s in (0, 1):
                        g = b * 2 + s
                        transposed.wait(act, g)
                        nc.scalar.activation(xT[:, s, :], ps[:, T, :], ACT.Copy).then_inc(xT_ready.sem, 1)
                        q_neg.wait(act, g)
                        nc.scalar.activation(qneg[:, s, :], qneg[:, s, :], ACT.Exp).then_inc(q_exp.sem, 1)
                        kv_biased.wait(act, g * 2 + 1)
                        nc.scalar.activation(kneg[:, s, :, :], kneg[:, s, :, :], ACT.Exp).then_inc(k_exp.sem, 1)
                    for s in (0, 1):
                        g = b * 2 + s
                        yT_mm.wait(act, g)
                        nc.scalar.activation(yT[:, s, :], ps[:, YT, :], ACT.Copy).then_inc(yT_ready.sem, 1)

            @block.gpsimd
            def _(pool):
                x_biased.open(pool)
                with pool.Fori(0, GROUPS) as g:
                    normed.wait(pool, g)
                    nc.gpsimd.tensor_tensor(S.x[:, cols(g * GROUP, GROUP)], S.x[:, cols(g * GROUP, GROUP)],
                                            S.a0_bc[:], ALU.add).then_inc(x_biased.sem, 1)

            @block.vector
            def _(dve):
                for s in (normed, q_neg, q_ready, kv_biased, k_ready, s_ready, y_ready, x_ready):
                    s.open(dve)
                c0 = Chain(dve, chain)
                c0.run(nc.vector.memset(kv[:], 1.0))
                with dve.Fori(0, BATCH) as b:
                    c = Chain(dve, chain, b, 14, 1)
                    for s in (0, 1):
                        g = b * 2 + s
                        transposed.wait(dve, g - 2)
                        for k in range(GT):
                            op = normalize_tile(nc, S, xn[:, s, k * P:(k + 1) * P], g * GT + k)
                        op.then_inc(normed.sem, 1)
                    for s in (0, 1):
                        g = b * 2 + s
                        q_mm.wait(dve, g)
                        nc.vector.tensor_scalar(qneg[:, s, :], ps[:, Q, :], S.a0_bq[:], 0.0, ALU.add,
                                                ALU.min).then_inc(q_neg.sem, 1)
                        for half in (0, 1):
                            kv_mm.wait(dve, g * 2 + half)
                            z = kv[:, s, 2 * half:2 * half + 2, :]
                            c.run(nc.vector.tensor_tensor(z[:, :, 0:2 * P],
                                                          ps[:, KV[half], :].rearrange("p (t c) -> p t c", t=2),
                                                          S.a0_bkv[:].rearrange("p (t c) -> p t c", t=2), ALU.add))
                            nc.vector.tensor_scalar(kneg[:, s, 2 * half:2 * half + 2, :], z[:, :, 0:P], 0.0, None,
                                                    ALU.min).then_inc(kv_biased.sem, 1)
                        q_exp.wait(dve, g)
                        nc.vector.scalar_tensor_tensor(qT[:, s, :], ps[:, Q, :], S.a0_bq1[:], qneg[:, s, :], ALU.add,
                                                       ALU.max).then_inc(q_ready.sem, 1)
                        k_exp.wait(dve, g)
                        nc.vector.scalar_tensor_tensor(kv[:, s, :, 0:P], kv[:, s, :, 0:P], 1.0, kneg[:, s, :, :],
                                                       ALU.add, ALU.max).then_inc(k_ready.sem, 1)
                    s_mm.wait(dve, b)
                    c.run(nc.vector.tensor_copy(ksum[:], ps[:, ST, P:P + 1]))
                    c.run(nc.vector.tensor_tensor(state[:, 0:P], ps[:, ST, 0:P], S.head_mask[:], ALU.mult))
                    nc.vector.tensor_scalar(state[:, P:SW], S.head_mask[:].rearrange("p (h d) -> p h d", h=H)[:, :, 0],
                                            ksum[:], None, ALU.mult).then_inc(s_ready.sem, 1)
                    for s in (0, 1):
                        g = b * 2 + s
                        for half in (0, 1):
                            n_mm.wait(dve, g * 2 + half)
                            num = ps[:, NUM[half], 0:2 * SW].rearrange("p (t c) -> p t c", t=2)
                            r = den[:, half * 2 * H:(half + 1) * 2 * H]
                            c.run(nc.vector.tensor_scalar(r.rearrange("p (t h) -> p t h", t=2), num[:, :, P:SW], 1e-6,
                                                          None, ALU.add))
                            c.run(nc.vector.reciprocal(r, r))
                            for k in (0, 1):
                                o = y[:, s, (2 * half + k) * P:(2 * half + k + 1) * P].rearrange("p (h d) -> p h d", h=H)
                                op = nc.vector.tensor_tensor(
                                    o, num[:, k, 0:P].rearrange("p (h d) -> p h d", h=H),
                                    r[:, k * H:(k + 1) * H].rearrange("p (h o) -> p h o", o=1).broadcast_to([P, H, HD]),
                                    ALU.mult)
                            op.then_inc(y_ready.sem, 1)
                    for s in (0, 1):
                        g = b * 2 + s
                        o_mm.wait(dve, g)
                        x_biased.wait(dve, g)
                        nc.vector.tensor_tensor(S.x[:, cols(g * GROUP, GROUP)], S.x[:, cols(g * GROUP, GROUP)],
                                                ps[:, ST, :], ALU.add).then_inc(x_ready.sem, 1)
                    c.end()


def store_phase(nc, S, out):
    ctx, sb, sem, steps = scope(nc)
    with ctx:
        stored = sem("stored")
        with nc.Block() as block:
            @block.sync
            def _(sp):
                sp.dma_start(out.rearrange("b (t p) d -> p (b t) d", p=P),
                             S.x[:].rearrange("p (t d) -> p t d", d=D)).then_inc(stored, 16)
                sp.wait_ge(stored, 16)


def bcast(v, n):
    return v.rearrange("p (a o) -> p a o", o=1).broadcast_to([P, v.shape[-1], n])


def by_tile(v):
    return v.rearrange("p (t e) -> p t e", e=E)


def by_expert(v):
    return v.rearrange("p (t e) -> p e t", e=E)


def per_expert(v, n=TILES):
    return v.rearrange("p (o e) -> p o e", o=1).broadcast_to([P, n, E])


def softmax_start(nc, dve, c, logits, mx, shifted):
    c.run(nc.vector.tensor_reduce(mx, logits, AX.X, ALU.max))
    return nc.vector.tensor_tensor(by_tile(shifted), logits, bcast(mx, E), ALU.subtract)


def softmax_end(nc, c, exped, total, gates):
    c.run(nc.vector.tensor_reduce(total, by_tile(exped), AX.X, ALU.add))
    c.run(nc.vector.reciprocal(total, total))
    c.run(nc.vector.tensor_tensor(by_tile(gates), by_tile(exped), bcast(total, E), ALU.mult))


def pick_largest(nc, S, c, values, mx, work, onehot, largest=None):
    largest = mx if largest is None else largest
    c.run(nc.vector.tensor_reduce(largest, by_tile(values), AX.X, ALU.max))
    c.run(nc.vector.tensor_tensor(by_tile(work), by_tile(values), bcast(largest, E), ALU.is_equal))
    c.run(nc.vector.tensor_tensor(work, work, S.first_rank[:], ALU.mult))
    c.run(nc.vector.tensor_reduce(mx, by_tile(work), AX.X, ALU.max))
    c.run(nc.vector.tensor_tensor(by_tile(onehot), by_tile(work), bcast(mx, E), ALU.is_equal))


def count_matmuls(nc, S, bank, mask):
    W = TILES * E
    nc.tensor.matmul(bank[:, 0:W], S.prefix[:], mask, start=True, stop=True)
    return nc.tensor.matmul(bank[:, W:2 * W], S.ones_b[:], mask, start=True, stop=True)


def running_counts(nc, S, c, counts, totals, summed, cum):
    W = TILES * E
    c.run(nc.vector.tensor_copy(totals.rearrange("p (e t) -> p e t", e=E), by_expert(counts[:, W:2 * W])))
    c.run(nc.vector.tensor_tensor_scan(summed, S.carry_on[:], totals, 0.0, ALU.mult, ALU.add))
    c.run(nc.vector.tensor_tensor(totals, summed, totals, ALU.subtract))
    c.run(nc.vector.tensor_tensor(by_expert(cum), by_expert(counts[:, 0:W]),
                                  totals.rearrange("p (e t) -> p e t", e=E), ALU.add))


def routed_pair_ffn(nc, S):
    CAP = float(-(-TOK * 5 // (E * 4)))
    FC = 2
    ctx, sb, sem, steps = scope(nc)
    ps = S.ps
    HB, L, C, T, YB = (0, 1), 2, 3, (4, 5), 4
    W = TILES * E
    with ctx:
        xn = sb("xn", [P, 2, GROUP])
        xT = sb("xT", [P, TOK])
        xTs = sb("xT_stationary", [P, 2, GROUP])
        hT = sb("hT", [P, 2, FC, GROUP])
        mx, total = sb("mx", [P, TILES]), sb("total", [P, TILES])
        exped, gates, work, rest = sb("exped", [P, W]), sb("gates", [P, W]), sb("work", [P, W]), sb("rest", [P, W])
        best, second, mask = sb("best", [P, W]), sb("second", [P, W]), sb("mask", [P, W], BF16)
        totals, summed, cum = sb("totals", [P, W]), sb("summed", [P, W]), sb("cum", [P, W])
        comb = sb("comb", [P, W])
        chain, shifted, exp_done, masked, counted = [sem(n) for n in (
            "chain shifted exp_done masked counted").split()]
        normed, transposed, xTs_ready, xT_ready, logits_mm, h_mm, h_ready, y_mm, y_added = [steps(n) for n in (
            "normed transposed xTs_ready xT_ready logits_mm h_mm h_ready y_mm y_added").split()]

        with nc.Block() as block:
            @block.tensor
            def _(pe):
                for s in (transposed, logits_mm, h_mm, y_mm):
                    s.open(pe)

                def transpose(g, s):
                    normed.wait(pe, g)
                    xTs_ready.wait(pe, g - 2)
                    for k in range(GT):
                        op = nc.tensor.transpose(ps[:, T[s], k * P:(k + 1) * P], xn[:, s, k * P:(k + 1) * P],
                                                 S.ident[:])
                    op.then_inc(transposed.sem, 1)

                with pe.Fori(0, PAIRS) as b:
                    for s in (0, 1):
                        transpose(b * 2 + s, s)
                    for s in (0, 1):
                        g = b * 2 + s
                        xTs_ready.wait(pe, g)
                        for k in range(GT):
                            op = nc.tensor.matmul(ps[:, L, cols((g * GT + k) * E, E)],
                                                  xTs[:, s, k * P:(k + 1) * P], S.f0_wr[:], start=True, stop=True)
                        op.then_inc(logits_mm.sem, 1)

                def hidden(g, s):
                    h_ready.wait(pe, g * FC - 1)
                    for f in range(FC):
                        nc.tensor.matmul(ps[:, HB[f], :], S.f0_wg[:, f * P:(f + 1) * P],
                                         xT[:, cols(g * GROUP, GROUP)], start=True, stop=True).then_inc(h_mm.sem, 1)

                def experts(g, s, more=True):
                    h_ready.wait(pe, g * FC + FC - 1)
                    for k in range(GT):
                        for half in (0, 1):
                            n = (g * GT + k) * 2 + half
                            y_added.wait(pe, n - 4)
                            for f in range(FC):
                                op = nc.tensor.matmul(ps[:, YB + 2 * (k % 2) + half, :],
                                                      hT[:, s, f, k * P:(k + 1) * P],
                                                      S.f0_wd[:, f, half * GROUP:(half + 1) * GROUP],
                                                      start=(f == 0), stop=(f == FC - 1))
                            op.then_inc(y_mm.sem, 1)
                        if k == 1 and more:
                            hidden(g + 1, 1 - s)

                xT_ready.wait(pe, GROUPS - 1)
                hidden(0, 0)
                pe.wait_ge(masked, 1)
                count_matmuls(nc, S, ps[:, C, :], mask[:]).then_inc(counted, 1)
                with pe.Fori(0, PAIRS - 1) as j:
                    for s in (0, 1):
                        experts(j * 2 + s, s)
                experts(GROUPS - 2, 0)
                experts(GROUPS - 1, 1, False)

            @block.scalar
            def _(act):
                for s in (xTs_ready, h_ready):
                    s.open(act)
                nc.scalar.activation(S.act_warm[:], S.eps[:], ACT.Exp)
                with act.Fori(0, PAIRS) as b:
                    for s in (0, 1):
                        g = b * 2 + s
                        transposed.wait(act, g)
                        logits_mm.wait(act, g - 2)
                        xT_ready.wait(act, g - 2)
                        nc.scalar.activation(xTs[:, s, :], ps[:, T[s], :], ACT.Copy).then_inc(xTs_ready.sem, 1)
                act.wait_ge(shifted, 1)
                nc.scalar.activation(exped[:], exped[:], ACT.Exp).then_inc(exp_done, 1)
                with act.Fori(0, PAIRS) as b:
                    for s in (0, 1):
                        g = b * 2 + s
                        y_mm.wait(act, (g - 1) * GT * 2 - 1)
                        for f in range(FC):
                            h_mm.wait(act, g * FC + f)
                            nc.scalar.activation(hT[:, s, f, :], ps[:, HB[f], :], ACT.Silu).then_inc(h_ready.sem, 1)

            @block.vector
            def _(dve):
                for s in (normed, xT_ready, y_added):
                    s.open(dve)
                with dve.Fori(0, PAIRS) as b:
                    for s in (0, 1):
                        g = b * 2 + s
                        transposed.wait(dve, g - 2)
                        for k in range(GT):
                            op = normalize_tile(nc, S, xn[:, s, k * P:(k + 1) * P], g * GT + k)
                        op.then_inc(normed.sem, 1)
                    for s in (0, 1):
                        g = b * 2 + s
                        xTs_ready.wait(dve, g)
                        nc.vector.tensor_copy(xT[:, cols(g * GROUP, GROUP)], xTs[:, s, :]).then_inc(xT_ready.sem, 1)
                logits_mm.wait(dve, GROUPS - 1)
                c = Chain(dve, chain)
                softmax_start(nc, dve, c, by_tile(ps[:, L, 0:W]), mx[:], exped[:]).then_inc(shifted, 1)
                dve.wait_ge(exp_done, 1)
                softmax_end(nc, c, exped[:], total[:], gates[:])
                pick_largest(nc, S, c, gates[:], mx[:], work[:], best[:])
                c.run(nc.vector.scalar_tensor_tensor(rest[:], best[:], -2.0, gates[:], ALU.mult, ALU.add))
                pick_largest(nc, S, c, rest[:], mx[:], work[:], second[:])
                nc.vector.tensor_tensor(mask[:], best[:], second[:], ALU.add).then_inc(masked, 1)
                dve.wait_ge(counted, 1)
                running_counts(nc, S, c, ps[:, C, :], totals[:], summed[:], cum[:])
                c.run(nc.vector.scalar_tensor_tensor(cum[:], cum[:], CAP, mask[:], ALU.is_le, ALU.mult))
                c.run(nc.vector.tensor_tensor(work[:], cum[:], gates[:], ALU.mult))
                c.run(nc.vector.tensor_reduce(total[:], by_tile(work[:]), AX.X, ALU.add))
                c.run(nc.vector.tensor_scalar(total[:], total[:], 1e-6, None, ALU.add))
                c.run(nc.vector.reciprocal(total[:], total[:]))
                c.run(nc.vector.tensor_tensor(by_tile(comb[:]), by_tile(work[:]), bcast(total[:], E), ALU.mult))
                links = c.n
                with dve.Fori(0, TILES // 2) as j:
                    c = Chain(dve, chain, j, 2 * (E - 2), links)
                    for k in (0, 1):
                        t = j * 2 + k
                        xt = S.x[:, cols(t * P, P)]
                        for e in range(E):
                            if e % 4 == 0:
                                y_mm.wait(dve, t * 2 + e // 4)
                            op = nc.vector.scalar_tensor_tensor(
                                xt, ps[:, YB + 2 * k + e // 4, (e % 4) * P:(e % 4 + 1) * P],
                                comb[:, cols(t * E + e, 1)], xt, ALU.mult, ALU.add)
                            if e % 4 == 3:
                                op.then_inc(y_added.sem, 1)
                                y_added.wait(dve, t * 2 + e // 4)
                            else:
                                c.run(op)
                    c.end()


PARTS = 3
STACK = PARTS * PARTS * HD
SHIFT = 2
HEADS = BATCH * H


def project_qkv(nc, S, wq, bq, scale, wk, bk, wv, bv, vd, keep_v=False):
    ctx, sb, sem, steps = scope(nc)
    ps = S.ps
    VC = H * vd
    VB = max(1, VC // GROUP)
    KTS = SEQ // P
    T, QK, V = 0, (1, 2), 3
    with ctx:
        xn = sb("xn", [P, 2, GROUP])
        xT = sb("xT", [P, 2, GROUP])
        z = sb("z", [P, 2, GROUP])
        parts = sb("parts", [P, 2, 2, PARTS, GROUP], BF16)
        v_out = sb("v_out", [P, 8 if keep_v else VC * KTS])
        (normed, transposed, xT_ready, qk_mm, z_ready, hi_ready, rest_ready, mid_ready, lo_ready, v_mm, v_ready) = [
            steps(n) for n in ("normed transposed xT_ready qk_mm z_ready hi_ready rest_ready mid_ready lo_ready v_mm "
                               "v_ready").split()]
        parts_out = [sem("parts_out0"), sem("parts_out1")]
        v_stored = sem("v_stored")
        chain = sem("chain")
        v_view = v_out[:].rearrange("p (c t) -> p t c", t=KTS)
        VSTEPS = GT * VB if VC > GROUP else 1
        with nc.Block() as block:
            @block.tensor
            def _(pe):
                for s in (transposed, qk_mm, v_mm):
                    s.open(pe)
                with pe.Fori(0, BATCH) as b:
                    for s in (0, 1):
                        g = b * 2 + s
                        normed.wait(pe, g)
                        xT_ready.wait(pe, g - 1)
                        for k in range(GT):
                            op = nc.tensor.transpose(ps[:, T, k * P:(k + 1) * P], xn[:, s, k * P:(k + 1) * P], S.ident[:])
                        op.then_inc(transposed.sem, 1)
                        xT_ready.wait(pe, g)
                        for n, w in enumerate((wq, wk)):
                            z_ready.wait(pe, g * 2 + n - 2)
                            nc.tensor.matmul(ps[:, QK[n], :], w[:], xT[:, s, :], start=True, stop=True).then_inc(qk_mm.sem, 1)
                        if VC <= GROUP:
                            v_ready.wait(pe, g - 1)
                            for k in range(GT):
                                op = nc.tensor.matmul(ps[:, V, k * VC:(k + 1) * VC], xT[:, s, k * P:(k + 1) * P], wv[:],
                                                      start=True, stop=True)
                            op.then_inc(v_mm.sem, 1)
                        else:
                            for k in range(GT):
                                for w in range(VB):
                                    n = k * VB + w
                                    v_ready.wait(pe, g * VSTEPS + n - 4)
                                    nc.tensor.matmul(ps[:, V + n % 4, :], xT[:, s, k * P:(k + 1) * P],
                                                     wv[:, w * GROUP:(w + 1) * GROUP], start=True,
                                                     stop=True).then_inc(v_mm.sem, 1)

            @block.scalar
            def _(act):
                for s in (xT_ready, hi_ready, mid_ready):
                    s.open(act)
                with act.Fori(0, BATCH) as b:
                    for s in (0, 1):
                        g = b * 2 + s
                        transposed.wait(act, g)
                        nc.scalar.activation(xT[:, s, :], ps[:, T, :], ACT.Copy).then_inc(xT_ready.sem, 1)
                        for n in (0, 1):
                            z_ready.wait(act, g * 2 + n)
                            nc.scalar.activation(parts[:, s, n, 0, :], z[:, n, :], ACT.Copy).then_inc(hi_ready.sem, 1)
                            rest_ready.wait(act, g * 2 + n)
                            nc.scalar.activation(parts[:, s, n, 1, :], z[:, n, :], ACT.Copy).then_inc(mid_ready.sem, 1)

            @block.vector
            def _(dve):
                for s in (normed, z_ready, rest_ready, lo_ready, v_ready):
                    s.open(dve)

                def group(b, s, first):
                    g = b * 2 + s
                    transposed.wait(dve, g - 2)
                    for k in range(GT):
                        op = normalize_tile(nc, S, xn[:, s, k * P:(k + 1) * P], g * GT + k)
                    op.then_inc(normed.sem, 1)
                    if not first:
                        dve.wait_ge(parts_out[s], b * 32)
                    for n in (0, 1):
                        qk_mm.wait(dve, g * 2 + n)
                        if n == 0:
                            nc.vector.tensor_scalar(z[:, n, :], ps[:, QK[n], :], bq[:], scale, ALU.add,
                                                    ALU.mult).then_inc(z_ready.sem, 1)
                        else:
                            nc.vector.tensor_scalar(z[:, n, :], ps[:, QK[n], :], bk[:], None,
                                                    ALU.add).then_inc(z_ready.sem, 1)
                    if s == 0 and not first and not keep_v:
                        dve.wait_ge(v_stored, b * 16)
                    if keep_v:
                        v_mm.wait(dve, g)
                        nc.vector.tensor_tensor(S.v_tok[:, cols(g * GROUP, GROUP)], ps[:, V, :], bv[:],
                                                ALU.add).then_inc(v_ready.sem, 1)
                    elif VC <= GROUP:
                        v_mm.wait(dve, g)
                        nc.vector.tensor_tensor(v_view[:, s * GT:(s + 1) * GT, :],
                                                ps[:, V, :].rearrange("p (t c) -> p t c", t=GT),
                                                bv[:].rearrange("p (t c) -> p t c", t=GT), ALU.add).then_inc(v_ready.sem, 1)
                    else:
                        for k in range(GT):
                            for w in range(VB):
                                n = k * VB + w
                                v_mm.wait(dve, g * VSTEPS + n)
                                nc.vector.tensor_tensor(v_view[:, s * GT + k, w * GROUP:(w + 1) * GROUP],
                                                        ps[:, V + n % 4, :], bv[:, w * GROUP:(w + 1) * GROUP],
                                                        ALU.add).then_inc(v_ready.sem, 1)
                    for n in (0, 1):
                        hi_ready.wait(dve, g * 2 + n)
                        nc.vector.tensor_tensor(z[:, n, :], z[:, n, :], parts[:, s, n, 0, :],
                                                ALU.subtract).then_inc(rest_ready.sem, 1)
                    for n in (0, 1):
                        mid_ready.wait(dve, g * 2 + n)
                        nc.vector.tensor_tensor(parts[:, s, n, 2, :], z[:, n, :], parts[:, s, n, 1, :],
                                                ALU.subtract).then_inc(lo_ready.sem, 1)

                for s in (0, 1):
                    group(0, s, True)
                with dve.Fori(1, BATCH) as b:
                    for s in (0, 1):
                        group(b, s, False)

            @block.sync
            def _(sp):
                with sp.Fori(0, BATCH) as b:
                    for s in (0, 1):
                        for n, dst in enumerate((S.q_parts, S.k_parts)):
                            lo_ready.wait(sp, b * 4 + s * 2 + n)
                            sp.dma_start(dst[bass.ds(b, 1), :, :, :, s * GROUP:(s + 1) * GROUP]
                                         .rearrange("b a h d t -> (b h d) a t"), parts[:, s, n]).then_inc(parts_out[s], 16)
                    if not keep_v:
                        v_ready.wait(sp, b * 2 * VSTEPS + 2 * VSTEPS - 1)
                        sp.dma_start(S.v_heads[bass.ds(b * H, H), :, 0:vd * KTS].rearrange("h p c -> p h c"),
                                     v_out[:].rearrange("p (h c) -> p h c", h=H)).then_inc(v_stored, 16)
                for q in parts_out:
                    sp.wait_ge(q, 32 * BATCH)
                if not keep_v:
                    sp.wait_ge(v_stored, 16 * BATCH)


class Head:

    def __init__(self, turn, c):
        self.turn, self.c = turn, c

    def __sub__(self, n):
        return Head(self.turn, self.c - n)

    def times(self, k, plus=0):
        return self.turn * (4 * k) + (self.c * k + plus)

    def rounds(self, ring):
        return self.turn * (4 // ring) + self.c // ring

    def slot(self, ring):
        return self.c % ring


def load_stacks(sp, S, i, q_stack, k_stack, loaded):
    b, h = i.times(1) // H, i.times(1) % H
    for r in range(PARTS):
        rows = slice(r * PARTS * HD, (r + 1) * PARTS * HD)
        q = S.q_parts[bass.ds(b, 1), r, bass.ds(h, 1), :, :].rearrange("b h d t -> (b h) d t")
        sp.dma_start(q_stack[rows, :], q.broadcast_to([PARTS, HD, SEQ])).then_inc(loaded, 16)
        k = S.k_parts[bass.ds(b, 1), :, bass.ds(h, 1), :, :].rearrange("b a h d t -> (b a) (h d) t")
        sp.dma_start(k_stack[rows, :], k).then_inc(loaded, 16)


def attend(nc, S, causal, vd):
    ctx, sb, sem, steps = scope(nc)
    ps = S.ps
    KTS = SEQ // P
    VW = vd + 1 if causal else 32
    CH = SEQ // GROUP
    S1, S2, OB, MB = 0, 4, 6, 7
    MP = 96 if causal else 0
    if causal:
        MB = OB
        tiles = [(kt, c) for kt in range(KTS) for c in range(CH) if kt * P < (c + 1) * GROUP]
        groups = [tiles[0:4], tiles[4:8], tiles[8:10], tiles[10:12]]
    else:
        tiles = [(kt, c) for kt in range(KTS) for c in range(CH)]
        groups = [tiles[n:n + 4] for n in range(0, 16, 4)]
    NT = len(tiles)
    RING = 6 if causal else 8
    LOADS = 16 * (2 * PARTS + 1)
    OROWS = VW if causal else P

    with ctx:
        qs = [sb(f"q_stack{n}", [P, SEQ], BF16) for n in range(4)]
        ks = [sb(f"k_stack{n}", [P, SEQ], BF16) for n in range(4)]
        vs = [sb(f"v{n}", [P, VW, KTS]) for n in range(4)]
        prob = sb("prob", [P, RING, GROUP])
        neg_max = sb("neg_max", [P, 2, KTS])
        shift = sb("shift", [P, 2, SHIFT * KTS], BF16)
        shift_rows = sb("shift_rows", [P, 2, P], BF16)
        o_out = sb("o_out", [P, 2, SEQ if causal else GROUP])
        (s1_mm, maxed, split, m_mm, m_read, s2_mm, exped, pv_mm, o_read) = [steps(n) for n in (
            "s1_mm maxed split m_mm m_read s2_mm exped pv_mm o_read").split()]
        loaded = [sem(f"loaded{n}") for n in range(4)]
        shifted = [sem(f"shifted{n}") for n in range(2)]
        stored = [sem(f"stored{n}") for n in range(2)]
        cleared, chain = sem("cleared"), sem("chain")

        def offset(kt, c):
            return max(kt * P - c * GROUP, 0) if causal else 0

        def run(eng, step):
            last = HEADS + 2
            for c in range(4):
                step(Head(0, c), c)
            with eng.Fori(1, HEADS // 4 - 1) as turn:
                for c in range(4):
                    step(Head(turn, c), None)
            for c in range(HEADS - 4, last + 1):
                step(Head(0, c), c)

        def there(n, h):
            return n is None or 0 <= n - h < HEADS

        with nc.Block() as block:
            @block.tensor
            def _(pe):
                for s in (s1_mm, m_mm, s2_mm, pv_mm):
                    s.open(pe)

                def first_pass(i, qt):
                    bank = S1 + 2 * (qt % 2)
                    maxed.wait(pe, i.times(KTS, qt - 2))
                    q, k = qs[i.slot(4)], ks[i.slot(4)]
                    for c in range(CH):
                        n = min(GROUP, (qt + 1) * P - c * GROUP) if causal else GROUP
                        if n > 0:
                            op = nc.tensor.matmul(ps[:, bank + c, 0:n], q[0:STACK, qt * P:(qt + 1) * P],
                                                  k[0:STACK, c * GROUP:c * GROUP + n], start=True,
                                                  stop=not causal or qt * P >= (c + 1) * GROUP)
                    if causal:
                        c, at = divmod(qt * P, GROUP)
                        op = nc.tensor.matmul(ps[:, bank + c, at:at + P], S.ident_b[:], S.mask_qk[:],
                                              start=False, stop=True)
                    op.then_inc(s1_mm.sem, 1)

                def second_scores(j, n, kt, c):
                    exped.wait(pe, j.times(NT, n - 2))
                    o = offset(kt, c)
                    diagonal = causal and kt * P >= c * GROUP
                    out = ps[:, S2 + n % 2, o:GROUP]
                    op = nc.tensor.matmul(out, ks[j.slot(4)][:, kt * P:(kt + 1) * P],
                                          qs[j.slot(4)][:, c * GROUP + o:(c + 1) * GROUP], start=True, stop=not diagonal)
                    if diagonal:
                        op = nc.tensor.matmul(ps[:, S2 + n % 2, o:o + P], S.ident_b[:], S.mask_kq[:],
                                              start=False, stop=True)
                    op.then_inc(s2_mm.sem, 1)

                def weigh(j, g):
                    if g == 0:
                        o_read.wait(pe, j.times(1, -1))
                    at = sum(len(x) for x in groups[:g])
                    exped.wait(pe, j.times(NT, at + len(groups[g]) - 1))
                    for n, (kt, c) in enumerate(groups[g], at):
                        o = offset(kt, c)
                        if causal:
                            out = ps[0:VW, OB + c, o:GROUP]
                            start, stop = kt == 0, kt == (c + 1) * GROUP // P - 1
                        else:
                            quad = (c * 2 + kt % 2) * 32
                            out = ps[quad:quad + VW, OB, :]
                            start, stop = kt < 2, kt >= KTS - 2
                        nc.tensor.matmul(out, vs[j.slot(4)][:, :, kt], prob[:, n % RING, o:GROUP], start=start,
                                         stop=stop).then_inc(pv_mm.sem, 1)

                def step(i, n):
                    one, two = there(n, 0), there(n, 2)
                    if one:
                        pe.wait_ge(loaded[i.slot(4)], (i.rounds(4) + 1) * LOADS)
                    if two:
                        pe.wait_ge(shifted[i.slot(2)], ((i - 2).rounds(2) + 1) * 16)
                    j = i - 2
                    for g in range(4):
                        at = sum(len(x) for x in groups[:g])
                        mine = list(enumerate(groups[g], at))
                        half = len(mine) // 2
                        if two:
                            for m, (kt, c) in mine[:half]:
                                second_scores(j, m, kt, c)
                        if one:
                            first_pass(i, 2 * g)
                        if two:
                            for m, (kt, c) in mine[half:]:
                                second_scores(j, m, kt, c)
                        if g > 0 and two:
                            weigh(j, g - 1)
                        if g == 0 and there(n, 3):
                            weigh(i - 3, 3)
                        if one:
                            first_pass(i, 2 * g + 1)
                        if g == 1 and there(n, 1):
                            h = i - 1
                            split.wait(pe, h.times(1))
                            m_read.wait(pe, h.times(1, -1))
                            nc.tensor.transpose(ps[MP:MP + SHIFT * KTS, MB, 0:P // 2].bitcast(BF16),
                                                shift[:, h.slot(2), :], S.ident_b[:]).then_inc(m_mm.sem, 1)

                pe.wait_ge(cleared, 1)
                run(pe, step)

            @block.scalar
            def _(act):
                for s in (exped, m_read):
                    s.open(act)

                def step(i, n):
                    j = i - 2
                    for g in range(4):
                        if there(n, 2):
                            at = sum(len(x) for x in groups[:g])
                            for m, (kt, c) in enumerate(groups[g], at):
                                s2_mm.wait(act, j.times(NT, m))
                                pv_mm.wait(act, j.times(NT, m - RING))
                                o = offset(kt, c)
                                nc.scalar.activation(prob[:, m % RING, o:GROUP], ps[:, S2 + m % 2, o:GROUP],
                                                     ACT.Exp).then_inc(exped.sem, 1)
                        if g == 1 and there(n, 1):
                            h = i - 1
                            m_mm.wait(act, h.times(1))
                            if n is None or n - 3 >= 0:
                                act.wait_ge(shifted[h.slot(2)], h.rounds(2) * 16)
                            nc.scalar.activation(shift_rows[MP:MP + SHIFT * KTS, h.slot(2), :],
                                                 ps[MP:MP + SHIFT * KTS, MB, 0:P // 2].bitcast(BF16),
                                                 ACT.Copy).then_inc(m_read.sem, 1)

                nc.scalar.activation(S.act_warm[:], S.eps[:], ACT.Exp)
                run(act, step)

            @block.vector
            def _(dve):
                for s in (maxed, o_read):
                    s.open(dve)

                def step(i, n):
                    for qt in range(KTS):
                        if there(n, 0):
                            if qt == 0:
                                split.wait(dve, i.times(1, -2))
                            s1_mm.wait(dve, i.times(KTS, qt))
                            bank = S1 + 2 * (qt % 2)
                            keys = (qt + 1) * P if causal else SEQ
                            nc.vector.tensor_reduce(neg_max[:, i.slot(2), qt:qt + 1],
                                                    ps[:, bank:bank + 2, :].rearrange("p b n -> p (b n)")[:, 0:keys],
                                                    AX.X, ALU.max, negate=True).then_inc(maxed.sem, 1)
                        if qt == 1 and there(n, 3):
                            h = i - 3
                            pv_mm.wait(dve, h.times(NT, NT - 1))
                            if n is None or n - 3 >= 2:
                                dve.wait_ge(stored[h.slot(2)], h.rounds(2) * 16)
                            src = ps[0:OROWS, OB:OB + 2, :] if causal else ps[:, OB, :]
                            dst = o_out[0:OROWS, h.slot(2), :]
                            if causal:
                                dst = dst.rearrange("p (c n) -> p c n", c=CH)
                            nc.vector.tensor_copy(dst, src).then_inc(o_read.sem, 1)

                run(dve, step)

            @block.gpsimd
            def _(pool):
                split.open(pool)
                for n in range(4):
                    nc.gpsimd.memset(qs[n][:], 0.0)
                    nc.gpsimd.memset(ks[n][:], 1.0)
                    nc.gpsimd.memset(vs[n][:, vd + 1:VW, :], 0.0) if VW > vd + 1 else None
                    op = nc.gpsimd.memset(vs[n][:, vd:vd + 1, :], 1.0)
                op.then_inc(cleared, 1)

                def heads(i):
                    maxed.wait(pool, i.times(KTS, KTS - 1))
                    m_mm.wait(pool, i.times(1, -2))
                    hi = shift[:, i.slot(2), 0:KTS]
                    nc.gpsimd.tensor_tensor(hi, neg_max[:, i.slot(2), :], S.zeros[:, 0:KTS],
                                            ALU.add).then_inc(chain, 1)
                    pool.wait_ge(chain, i.times(1, 1))
                    nc.gpsimd.tensor_tensor(shift[:, i.slot(2), KTS:2 * KTS], neg_max[:, i.slot(2), :], hi,
                                            ALU.subtract).then_inc(split.sem, 1)

                with pool.Fori(0, HEADS // 4) as turn:
                    for c in range(4):
                        heads(Head(turn, c))

            @block.sync
            def _(sp):
                sp.wait_ge(cleared, 1)

                def load(i, n):
                    if n is None or n >= 4:
                        pv_mm.wait(sp, i.times(NT, -3 * NT - 1))
                    at, slot = i.times(1), i.slot(4)
                    load_stacks(sp, S, i, qs[slot], ks[slot], loaded[slot])
                    sp.dma_start(vs[slot][:, 0:vd, :],
                                 S.v_heads[bass.ds(at, 1), :, 0:vd * KTS].rearrange("a p (d t) -> (a p) d t", t=KTS)
                                 ).then_inc(loaded[slot], 16)

                def step(i, n):
                    if n is None or n + 1 < HEADS:
                        load(i - (-1), None if n is None else n + 1)
                    if there(n, 3):
                        h = i - 3
                        o_read.wait(sp, h.times(1))
                        at = h.times(1)
                        if causal:
                            sp.dma_start(S.o_wide[bass.ds(at, 1), :, :].rearrange("a r n -> (a r) n"),
                                         o_out[0:OROWS, h.slot(2), :]).then_inc(stored[h.slot(2)], 16)
                        else:
                            sp.dma_start(S.o_quads[bass.ds(at, 1), :, :].rearrange("a r n -> (a r) n"),
                                         o_out[:, h.slot(2), :]).then_inc(stored[h.slot(2)], 16)
                    if there(n, 1):
                        h = i - 1
                        m_read.wait(sp, h.times(1))
                        sp.dma_start(qs[h.slot(4)][STACK:STACK + SHIFT, :].rearrange("r (q t) -> r q t", t=P),
                                     shift_rows[MP:MP + SHIFT * KTS, h.slot(2), :]).then_inc(shifted[h.slot(2)], 16)

                load(Head(0, 0), 0)
                run(sp, step)
                for s in stored:
                    sp.wait_ge(s, 16 * HEADS // 2)


def reciprocal_sums(nc, S, rows, out):
    ctx, sb, sem, steps = scope(nc)
    with ctx:
        part = sb("sums", [P, len(rows), GROUP])
        loaded, chain, ready, stored = sem("loaded"), sem("chain"), sem("ready"), sem("stored")
        with nc.Block() as block:
            @block.sync
            def _(sp):
                n = 0
                for k, some in enumerate(rows):
                    for at, src in some:
                        sp.dma_start(part[at, k, :], src).then_inc(loaded, 16)
                        n += 1
                sp.wait_ge(ready, 1)
                sp.dma_start(out, part[:, 0, :]).then_inc(stored, 16)
                sp.wait_ge(stored, 16)

            @block.vector
            def _(dve):
                dve.wait_ge(loaded, 16 * sum(len(x) for x in rows))
                c = Chain(dve, chain)
                if len(rows) == 2:
                    c.run(nc.vector.tensor_tensor(part[:, 0, :], part[:, 0, :], part[:, 1, :], ALU.add))
                nc.vector.reciprocal(part[:, 0, :], part[:, 0, :]).then_inc(ready, 1)


def attention_output(nc, S, wo, bo):
    quads = S.o_quads[:, :, :].rearrange("a (c q r) n -> a c q r n", c=2, q=2)
    reciprocal_sums(nc, S, [[(slice(0, P), quads[:, :, q, HD, :].rearrange("a c n -> (a c) n"))] for q in (0, 1)],
                    S.r_sums[:, :, :].rearrange("a c n -> (a c) n"))
    ctx, sb, sem, steps = scope(nc)
    ps = S.ps
    with ctx:
        num = sb("num", [P, 2, 2, GROUP])
        r = sb("r", [P, 2, GROUP])
        oT = sb("oT", [P, 2, GROUP])
        loaded = [sem("loaded0"), sem("loaded1")]
        added, x_biased, o_ready, y_mm, x_ready = [steps(n) for n in "added x_biased o_ready y_mm x_ready".split()]
        with nc.Block() as block:
            @block.sync
            def _(sp):
                with sp.Fori(0, BATCH) as b:
                    for c in (0, 1):
                        o_ready.wait(sp, b * 2 + c - 2)
                        for q in (0, 1):
                            src = quads[bass.ds(b * H, H), c, q, 0:HD, :]
                            sp.dma_start(num[:, c, q, :], src.rearrange("h r n -> h r n")).then_inc(loaded[c], 16)
                        sp.dma_start(r[:, c, :],
                                     S.r_sums[bass.ds(b * H, H), c:c + 1, :].broadcast_to([H, HD, GROUP])
                                     ).then_inc(loaded[c], 16)

            @block.gpsimd
            def _(pool):
                added.open(pool)
                x_biased.open(pool)
                with pool.Fori(0, BATCH) as b:
                    for c in (0, 1):
                        x = S.x[:, cols((b * 2 + c) * GROUP, GROUP)]
                        nc.gpsimd.tensor_tensor(x, x, bo[:], ALU.add).then_inc(x_biased.sem, 1)
                        pool.wait_ge(loaded[c], b * 48 + 48)
                        nc.gpsimd.tensor_tensor(num[:, c, 0, :], num[:, c, 0, :], num[:, c, 1, :],
                                                ALU.add).then_inc(added.sem, 1)

            @block.vector
            def _(dve):
                o_ready.open(dve)
                x_ready.open(dve)
                with dve.Fori(0, BATCH) as b:
                    for c in (0, 1):
                        g = b * 2 + c
                        added.wait(dve, g)
                        dve.wait_ge(loaded[c], b * 48 + 48)
                        y_mm.wait(dve, g - 2)
                        nc.vector.tensor_tensor(oT[:, c, :], num[:, c, 0, :], r[:, c, :], ALU.mult).then_inc(o_ready.sem, 1)
                    for c in (0, 1):
                        g = b * 2 + c
                        y_mm.wait(dve, g)
                        x_biased.wait(dve, g)
                        x = S.x[:, cols(g * GROUP, GROUP)]
                        nc.vector.tensor_tensor(x, x, ps[:, c, :], ALU.add).then_inc(x_ready.sem, 1)

            @block.tensor
            def _(pe):
                y_mm.open(pe)
                with pe.Fori(0, BATCH) as b:
                    for c in (0, 1):
                        g = b * 2 + c
                        o_ready.wait(pe, g)
                        x_ready.wait(pe, g - 2)
                        for k in range(GT):
                            op = nc.tensor.matmul(ps[:, c, k * P:(k + 1) * P], oT[:, c, k * P:(k + 1) * P], wo[:],
                                                  start=True, stop=True)
                        op.then_inc(y_mm.sem, 1)


def wide_attention_output(nc, S, wo, bo):
    VD = LATENT
    FC = H * VD // P
    reciprocal_sums(nc, S, [[(slice(c * HEADS, (c + 1) * HEADS), S.o_wide[:, VD, c * GROUP:(c + 1) * GROUP])
                             for c in (0, 1)]], S.r_wide[:, :, :].rearrange("c a n -> (c a) n"))
    ctx, sb, sem, steps = scope(nc)
    ps = S.ps
    with ctx:
        num = sb("num", [P, 2, FC, GROUP])
        r = sb("r", [H, 2, GROUP])
        oT = sb("oT", [P, 2, FC, GROUP])
        pick = sb("pick", [H, FC * P])
        made = sem("made")
        loaded = [sem("loaded0"), sem("loaded1")]
        r_mm, o_ready, x_biased, y_mm, x_ready = [steps(n) for n in "r_mm o_ready x_biased y_mm x_ready".split()]
        with nc.Block() as block:
            @block.sync
            def _(sp):
                with sp.Fori(0, BATCH) as b:
                    for c in (0, 1):
                        o_ready.wait(sp, (b * 2 + c) * FC - FC - 1)
                        for h in (0, 1):
                            src = S.o_wide[bass.ds(b * H, H), 0:VD, c * GROUP:(c + 1) * GROUP]
                            src = src.rearrange("(f h) l n -> h l f n", h=2)[h]
                            sp.dma_start(num[h * VD:(h + 1) * VD, c, :, :], src).then_inc(loaded[c], 16)
                        sp.dma_start(r[:, c, :], S.r_wide[c, bass.ds(b * H, H), :]).then_inc(loaded[c], 16)

            @block.gpsimd
            def _(pool):
                x_biased.open(pool)
                v = pick[:].rearrange("p (f h l) -> p f h l", f=FC, h=2)
                nc.gpsimd.memset(pick[:], 1.0).then_inc(made, 1)
                pool.wait_ge(made, 1)
                nc.gpsimd.affine_select(out=v, in_=v, compare_op=ALU.is_equal, fill=0.0, base=0,
                                        pattern=[[-2, FC], [-1, 2], [0, VD]], channel_multiplier=1).then_inc(made, 1)
                with pool.Fori(0, GROUPS) as g:
                    x = S.x[:, cols(g * GROUP, GROUP)]
                    nc.gpsimd.tensor_tensor(x, x, bo[:], ALU.add).then_inc(x_biased.sem, 1)

            @block.vector
            def _(dve):
                o_ready.open(dve)
                x_ready.open(dve)
                with dve.Fori(0, BATCH) as b:
                    for c in (0, 1):
                        g = b * 2 + c
                        y_mm.wait(dve, g - 2)
                        for f in range(FC):
                            r_mm.wait(dve, g * FC + f)
                            nc.vector.tensor_tensor(oT[:, c, f, :], num[:, c, f, :], ps[:, f % 4, :],
                                                    ALU.mult).then_inc(o_ready.sem, 1)
                        y_mm.wait(dve, g)
                        x_biased.wait(dve, g)
                        x = S.x[:, cols(g * GROUP, GROUP)]
                        nc.vector.tensor_tensor(x, x, ps[:, 4:8, 0:P], ALU.add).then_inc(x_ready.sem, 1)

            @block.tensor
            def _(pe):
                r_mm.open(pe)
                y_mm.open(pe)
                pe.wait_ge(made, 2)
                with pe.Fori(0, BATCH) as b:
                    for c in (0, 1):
                        g = b * 2 + c
                        pe.wait_ge(loaded[c], b * 48 + 48)
                        for f in range(FC):
                            o_ready.wait(pe, g * FC + f - 4)
                            nc.tensor.matmul(ps[:, f % 4, :], pick[:, f * P:(f + 1) * P], r[:, c, :], start=True,
                                             stop=True).then_inc(r_mm.sem, 1)
                        o_ready.wait(pe, g * FC + FC - 1)
                        x_ready.wait(pe, g - 1)
                        for k in range(GT):
                            for f in range(FC):
                                op = nc.tensor.matmul(ps[:, 4 + k, 0:P], oT[:, c, f, k * P:(k + 1) * P], wo[:, f, :],
                                                      start=(f == 0), stop=(f == FC - 1))
                        op.then_inc(y_mm.sem, 1)


LATENT = 64


def full_attention(nc, S):
    project_qkv(nc, S, S.b0_wq, S.b0_bq, HD ** -0.5, S.b0_wk, S.b0_bk, S.b0_wv, S.b0_bv, HD)
    attend(nc, S, False, HD)
    attention_output(nc, S, S.b0_wo, S.b0_bo)


def fold_latent_key(nc, S):
    ctx, sb, sem, steps = scope(nc)
    ps = S.ps
    L = LATENT
    with ctx:
        outer = sb("outer", [L, H * HD])
        ones = sb("ones", [L, 1])
        made, folded = sem("made"), sem("folded")
        with nc.Block() as block:
            @block.vector
            def _(dve):
                nc.vector.memset(ones[:], 1.0)
                nc.vector.tensor_tensor(outer[:].rearrange("p (h d) -> p h d", h=H),
                                        S.a1_bkl[:].rearrange("p (h o) -> p h o", o=1).broadcast_to([L, H, HD]),
                                        S.a1_wc[:].rearrange("p (o d) -> p o d", o=1).broadcast_to([L, H, HD]),
                                        ALU.mult).then_inc(made, 1)
                dve.wait_ge(folded, 1)
                nc.vector.tensor_copy(S.a1_wk2[:], ps[:, 0, 0:P])
                nc.vector.tensor_copy(S.a1_bk2[:], ps[:, 1, 0:1])

            @block.tensor
            def _(pe):
                for h in range(H):
                    nc.tensor.matmul(ps[:, 0, h * HD:(h + 1) * HD], S.a1_wkl[:, h * P:(h + 1) * P], S.a1_wc[:],
                                     start=True, stop=True)
                pe.wait_ge(made, 1)
                nc.tensor.matmul(ps[:, 1, 0:1], outer[:], ones[:], start=True, stop=True).then_inc(folded, 1)


def causal_attention(nc, S):
    fold_latent_key(nc, S)
    project_qkv(nc, S, S.a1_wq, S.a1_bq, LATENT ** -0.5, S.a1_wk2, S.a1_bk2, S.a1_wv, S.a1_bv, LATENT)
    attend(nc, S, True, LATENT)
    wide_attention_output(nc, S, S.a1_wo, S.a1_bo)


def row_attention(nc, S):
    ctx, sb, sem, steps = scope(nc)
    with ctx:
        S.v_tok = sb("v_tok", [P, TOK])
        S.weight = sb("weight", [P, TILES * H])
        project_qkv(nc, S, S.b1_wq, S.b1_bq, HD ** -0.5, S.b1_wk, S.b1_bk, S.b1_wv, S.b1_bv, HD, keep_v=True)
        attention_row_sums(nc, S)
        weighted_values_output(nc, S, S.b1_wo, S.b1_bo)


def attention_row_sums(nc, S):
    ctx, sb, sem, steps = scope(nc)
    ps = S.ps
    KTS = SEQ // P
    LOADS = 16 * 2 * PARTS
    with ctx:
        qs = [sb(f"q_stack{n}", [P, SEQ], BF16) for n in range(4)]
        ks = [sb(f"k_stack{n}", [P, SEQ], BF16) for n in range(4)]
        neg_max = sb("neg_max", [P, 2, KTS])
        sums = sb("sums", [P, HEADS * KTS])
        inverse = sb("inverse", [P, HEADS * KTS])
        s_mm, maxed, summed = [steps(n) for n in "s_mm maxed summed".split()]
        chain = sem("chain")
        loaded = [sem(f"loaded{n}") for n in range(4)]
        cleared = sem("cleared")

        def heads(eng, step):
            with eng.Fori(0, HEADS // 4) as turn:
                for c in range(4):
                    step(Head(turn, c))

        with nc.Block() as block:
            @block.tensor
            def _(pe):
                s_mm.open(pe)
                pe.wait_ge(cleared, 1)

                def step(i):
                    pe.wait_ge(loaded[i.slot(4)], (i.rounds(4) + 1) * LOADS)
                    for qt in range(KTS):
                        summed.wait(pe, i.times(KTS, qt - 4))
                        for c in (0, 1):
                            op = nc.tensor.matmul(ps[:, 2 * (qt % 4) + c, :], qs[i.slot(4)][:, qt * P:(qt + 1) * P],
                                                  ks[i.slot(4)][:, c * GROUP:(c + 1) * GROUP], start=True, stop=True)
                        op.then_inc(s_mm.sem, 1)

                heads(pe, step)

            @block.vector
            def _(dve):
                maxed.open(dve)

                def step(i):
                    summed.wait(dve, i.times(KTS, -KTS - 1))
                    for qt in range(KTS):
                        s_mm.wait(dve, i.times(KTS, qt))
                        nc.vector.tensor_reduce(neg_max[:, i.slot(2), qt:qt + 1],
                                                ps[:, 2 * (qt % 4):2 * (qt % 4) + 2, :], AX.XY, ALU.max,
                                                negate=True).then_inc(maxed.sem, 1)

                heads(dve, step)
                summed.wait(dve, HEADS * KTS - 1)
                c = Chain(dve, chain)
                c.run(nc.vector.reciprocal(inverse[:], sums[:]))
                for b in range(BATCH):
                    mine = slice(b * H * KTS, (b + 1) * H * KTS)
                    nc.vector.tensor_tensor(S.weight[:, mine].rearrange("p (t h) -> p h t", h=H),
                                            sums[:, mine].rearrange("p (h t) -> p h t", h=H),
                                            inverse[:, mine].rearrange("p (h t) -> p h t", h=H), ALU.mult)

            @block.scalar
            def _(act):
                summed.open(act)
                nc.scalar.activation(S.act_warm[:], S.eps[:], ACT.Exp)

                def step(i):
                    for qt in range(KTS):
                        maxed.wait(act, i.times(KTS, qt))
                        s = ps[:, 2 * (qt % 4):2 * (qt % 4) + 2, :]
                        nc.scalar.activation(s, s, ACT.Exp, bias=neg_max[:, i.slot(2), qt:qt + 1],
                                             accum_out=sums[:, cols(i.times(KTS, qt), 1)]).then_inc(summed.sem, 1)

                heads(act, step)

            @block.gpsimd
            def _(pool):
                for n in range(4):
                    nc.gpsimd.memset(qs[n][:], 0.0)
                    op = nc.gpsimd.memset(ks[n][:], 0.0)
                op.then_inc(cleared, 1)

            @block.sync
            def _(sp):
                sp.wait_ge(cleared, 1)

                def step(i):
                    s_mm.wait(sp, i.times(KTS, -3 * KTS - 1))
                    load_stacks(sp, S, i, qs[i.slot(4)], ks[i.slot(4)], loaded[i.slot(4)])

                for c in range(4):
                    load_stacks(sp, S, Head(0, c), qs[c], ks[c], loaded[c])
                with sp.Fori(1, HEADS // 4) as turn:
                    for c in range(4):
                        step(Head(turn, c))


def weighted_values_output(nc, S, wo, bo):
    ctx, sb, sem, steps = scope(nc)
    ps = S.ps
    with ctx:
        y = sb("y", [P, 2, GROUP])
        yT = sb("yT", [P, 2, GROUP])
        y_ready, transposed, yT_ready, o_mm, x_biased, x_ready = [steps(n) for n in (
            "y_ready transposed yT_ready o_mm x_biased x_ready").split()]
        with nc.Block() as block:
            @block.tensor
            def _(pe):
                transposed.open(pe)
                o_mm.open(pe)
                with pe.Fori(0, BATCH) as b:
                    for s in (0, 1):
                        g = b * 2 + s
                        y_ready.wait(pe, g)
                        yT_ready.wait(pe, g - 2)
                        for k in range(GT):
                            op = nc.tensor.transpose(ps[:, s, k * P:(k + 1) * P], y[:, s, k * P:(k + 1) * P], S.ident[:])
                        op.then_inc(transposed.sem, 1)
                    for s in (0, 1):
                        g = b * 2 + s
                        yT_ready.wait(pe, g)
                        x_ready.wait(pe, g - 2)
                        for k in range(GT):
                            op = nc.tensor.matmul(ps[:, 2 + s, k * P:(k + 1) * P], yT[:, s, k * P:(k + 1) * P], wo[:],
                                                  start=True, stop=True)
                        op.then_inc(o_mm.sem, 1)

            @block.scalar
            def _(act):
                yT_ready.open(act)
                with act.Fori(0, BATCH) as b:
                    for s in (0, 1):
                        g = b * 2 + s
                        transposed.wait(act, g)
                        o_mm.wait(act, g - 2)
                        nc.scalar.activation(yT[:, s, :], ps[:, s, :], ACT.Copy).then_inc(yT_ready.sem, 1)

            @block.gpsimd
            def _(pool):
                x_biased.open(pool)
                with pool.Fori(0, GROUPS) as g:
                    x = S.x[:, cols(g * GROUP, GROUP)]
                    nc.gpsimd.tensor_tensor(x, x, bo[:], ALU.add).then_inc(x_biased.sem, 1)

            @block.vector
            def _(dve):
                y_ready.open(dve)
                x_ready.open(dve)
                with dve.Fori(0, BATCH) as b:
                    for s in (0, 1):
                        g = b * 2 + s
                        transposed.wait(dve, g - 2)
                        w = S.weight[:, cols(g * GT * H, GT * H)]
                        nc.vector.tensor_tensor(y[:, s, :].rearrange("p (h d) -> p h d", d=HD),
                                                S.v_tok[:, cols(g * GROUP, GROUP)].rearrange("p (h d) -> p h d", d=HD),
                                                bcast(w, HD), ALU.mult).then_inc(y_ready.sem, 1)
                    for s in (0, 1):
                        g = b * 2 + s
                        o_mm.wait(dve, g)
                        x_biased.wait(dve, g)
                        x = S.x[:, cols(g * GROUP, GROUP)]
                        nc.vector.tensor_tensor(x, x, ps[:, 2 + s, :], ALU.add).then_inc(x_ready.sem, 1)


def route_best(nc, S):
    ctx, sb, sem, steps = scope(nc)
    ps = S.ps
    T, L, C = (0, 1), 2, 3
    W = TILES * E
    with ctx:
        xn = sb("xn", [P, 2, GROUP])
        xT = sb("xT", [P, 2, GROUP])
        st = sb("bn", [P, TILES * 6])
        tmp = sb("bn_tmp", [P, 4, TILES])
        mean, rstd = sb("mean2", [P, TILES]), sb("rstd2", [P, TILES])
        mx, total = sb("mx", [P, TILES]), sb("total", [P, TILES])
        logits, exped, gates, work = sb("logits", [P, W]), sb("exped", [P, W]), sb("gates", [P, W]), sb("work", [P, W])
        best, mask = sb("best", [P, W]), sb("mask", [P, W], BF16)
        totals, summed, cum = sb("totals", [P, W]), sb("summed", [P, W]), sb("cum", [P, W])
        rank = sb("rank", [P, TILES])
        filled = sb("filled", [P, E, TILES])
        tiles_of, base = sb("tiles_of", [P, E]), sb("base", [P, E])
        ones = sb("ones", [P, E])
        slot_f, expert_f = sb("slot_f", [P, TILES]), sb("expert_f", [P, SLOT_TILES])
        reached = sb("reached", [P, SLOT_TILES, E - 1])
        chain, bn, shifted, exp_done, masked, counted, var_ready, std_ready = [sem(n) for n in (
            "chain bn shifted exp_done masked counted var_ready std_ready").split()]
        normed, transposed, copied, xT_ready, l_mm = [steps(n) for n in (
            "normed transposed copied xT_ready l_mm").split()]
        with nc.Block() as block:
            @block.tensor
            def _(pe):
                transposed.open(pe)
                l_mm.open(pe)
                with pe.Fori(0, PAIRS) as b:
                    for s in (0, 1):
                        g = b * 2 + s
                        normed.wait(pe, g)
                        xT_ready.wait(pe, g - 2)
                        for k in range(GT):
                            op = nc.tensor.transpose(ps[:, T[s], k * P:(k + 1) * P], xn[:, s, k * P:(k + 1) * P],
                                                     S.ident[:])
                        op.then_inc(transposed.sem, 1)
                    for s in (0, 1):
                        g = b * 2 + s
                        xT_ready.wait(pe, g)
                        for k in range(GT):
                            op = nc.tensor.matmul(ps[:, L, cols((g * GT + k) * E, E)], xT[:, s, k * P:(k + 1) * P],
                                                  S.f1_wr[:], start=True, stop=True)
                        op.then_inc(l_mm.sem, 1)
                pe.wait_ge(masked, 1)
                count_matmuls(nc, S, ps[:, C, :], mask[:]).then_inc(counted, 1)

            @block.scalar
            def _(act):
                copied.open(act)
                xT_ready.open(act)
                with act.Fori(0, PAIRS) as b:
                    for s in (0, 1):
                        g = b * 2 + s
                        normed.wait(act, g)
                        nc.scalar.activation(S.normed2[:, cols(g * GROUP, GROUP)], xn[:, s, :],
                                             ACT.Copy).then_inc(copied.sem, 1)
                        transposed.wait(act, g)
                        l_mm.wait(act, g - 2)
                        nc.scalar.activation(xT[:, s, :], ps[:, T[s], :], ACT.Copy).then_inc(xT_ready.sem, 1)
                act.wait_ge(var_ready, 1)
                nc.scalar.activation(tmp[:, 1], tmp[:, 2], ACT.Sqrt, bias=S.eps[:], scale=1.0 / D).then_inc(std_ready, 1)
                nc.scalar.activation(S.act_warm[:], S.eps[:], ACT.Exp)
                act.wait_ge(shifted, 1)
                nc.scalar.activation(exped[:], exped[:], ACT.Exp).then_inc(exp_done, 1)

            @block.vector
            def _(dve):
                normed.open(dve)
                with dve.Fori(0, PAIRS) as b:
                    for s in (0, 1):
                        g = b * 2 + s
                        transposed.wait(dve, g - 2)
                        copied.wait(dve, g - 2)
                        for k in range(GT):
                            op = normalize_tile(nc, S, xn[:, s, k * P:(k + 1) * P], g * GT + k)
                        op.then_inc(normed.sem, 1)
                    for s in (0, 1):
                        g = b * 2 + s
                        normed.wait(dve, g)
                        for k in range(GT):
                            op = nc.vector.bn_stats(st[:, cols((g * GT + k) * 6, 6)], xn[:, s, k * P:(k + 1) * P])
                        op.then_inc(bn, 1)
                        dve.wait_ge(bn, g + 1)
                c = Chain(dve, chain)
                stats_tail(nc, dve, c, st, tmp, mean, rstd, var_ready, std_ready)
                l_mm.wait(dve, GROUPS - 1)
                nc.vector.memset(ones[:], 1.0)
                c.run(nc.vector.tensor_tensor(by_tile(logits[:]), by_tile(ps[:, L, 0:W]), per_expert(S.f1_br[:]),
                                              ALU.add))
                softmax_start(nc, dve, c, by_tile(logits[:]), mx[:], exped[:]).then_inc(shifted, 1)
                copied.wait(dve, GROUPS - 1)
                with dve.Fori(0, TILES) as t:
                    v = S.normed2[:, cols(t * P, P)]
                    nc.vector.tensor_scalar(v, v, mean[:, cols(t, 1)], rstd[:, cols(t, 1)], ALU.subtract, ALU.mult)
                dve.wait_ge(exp_done, 1)
                softmax_end(nc, c, exped[:], total[:], gates[:])
                pick_largest(nc, S, c, gates[:], mx[:], work[:], best[:], S.gate[:])
                nc.vector.tensor_copy(mask[:], best[:]).then_inc(masked, 1)
                dve.wait_ge(counted, 1)
                running_counts(nc, S, c, ps[:, C, :], totals[:], summed[:], cum[:])
                count = summed[:].rearrange("p (e t) -> p e t", e=E)[:, :, TILES - 1]
                c.run(nc.vector.tensor_tensor(work[:], cum[:], best[:], ALU.mult))
                nc.vector.tensor_reduce(rank[:], by_tile(work[:]), AX.X, ALU.add)
                c.run(nc.vector.tensor_tensor(filled[:], bcast(count, TILES),
                                              S.tile_start[:, 0:TILES].rearrange("p (o k) -> p o k", o=1)
                                              .broadcast_to([P, E, TILES]), ALU.is_gt))
                c.run(nc.vector.tensor_reduce(tiles_of[:], filled[:], AX.X, ALU.add))
                c.run(nc.vector.tensor_tensor_scan(base[:], ones[:], tiles_of[:], 0.0, ALU.mult, ALU.add))
                c.run(nc.vector.tensor_tensor(base[:], base[:], tiles_of[:], ALU.subtract))
                c.run(nc.vector.tensor_scalar(base[:], base[:], float(P), None, ALU.mult))
                c.run(nc.vector.tensor_tensor(by_tile(work[:]), by_tile(best[:]), per_expert(base[:]), ALU.mult))
                c.run(nc.vector.tensor_reduce(slot_f[:], by_tile(work[:]), AX.X, ALU.add))
                c.run(nc.vector.scalar_tensor_tensor(slot_f[:], slot_f[:], -1.0, rank[:], ALU.add, ALU.add))
                nc.vector.tensor_copy(S.slot[:], slot_f[:])
                c.run(nc.vector.tensor_tensor(reached[:], bcast(S.tile_start[:], E - 1),
                                              base[:, 1:E].rearrange("p (o e) -> p o e", o=1)
                                              .broadcast_to([P, SLOT_TILES, E - 1]), ALU.is_ge))
                c.run(nc.vector.tensor_reduce(expert_f[:], reached[:], AX.X, ALU.add))
                nc.vector.tensor_copy(S.tile_expert[:], expert_f[:])


def expert_tiles(nc, S):
    ctx, sb, sem, steps = scope(nc)
    ps = S.ps
    F = 4 * P
    FC = F // P
    TURNS = SLOT_TILES // 4
    XB, HB, TB, YB = (0, 1), (2, 3), (4, 5), (6, 7)
    with ctx:
        xs = sb("xs", [P, 4, P])
        xsT = sb("xsT", [P, 2, P])
        h = sb("h", [P, 2, F])
        hT = sb("hT", [P, 2, F])
        y = sb("y", [P, 2, P])
        back = sb("back", [P, TOK])
        scattered = sem("scattered")
        gathered = [sem(f"gathered{g}") for g in range(GROUPS)]
        loaded = [sem(f"loaded{n}") for n in range(4)]
        stored = [sem("stored0"), sem("stored1")]
        x_mm, xT_ready, h_mm, h_ready, hT_mm, hT_ready, y_mm, y_ready = [steps(n) for n in (
            "x_mm xT_ready h_mm h_ready hT_mm hT_ready y_mm y_ready").split()]
        with nc.Block() as block:
            @block.gpsimd
            def _(pool):
                for t in range(TILES):
                    nc.gpsimd.indirect_dma_start(
                        S.x_slots[:, :], bass.IndirectOffsetOnAxis(ap=S.slot[:, t:t + 1], axis=0),
                        S.normed2[:, t * P:(t + 1) * P], None).then_inc(scattered, 16)
                pool.wait_ge(scattered, 16 * TILES)

            @block.sync
            def _(sp):
                sp.wait_ge(scattered, 16 * TILES)

                def load(j, n):
                    for s in (0, 1):
                        sp.dma_start(xs[:, 2 * n + s, :], S.x_slots[bass.ds((j * 4 + (2 * n + s)) * P, P), :]
                                     ).then_inc(loaded[2 * n + s], 16)

                def store(j, n):
                    for s in (0, 1):
                        t = j * 4 + (2 * n + s)
                        y_ready.wait(sp, t)
                        sp.dma_start(S.y_slots[bass.ds(t * P, P), :], y[:, s, :]).then_inc(stored[s], 16)

                load(0, 0)
                load(0, 1)
                with sp.Fori(0, TURNS - 1) as j:
                    for n in (0, 1):
                        x_mm.wait(sp, j * 4 + (2 * n + 1))
                        load(j + 1, n)
                        store(j, n)
                for n in (0, 1):
                    store(TURNS - 1, n)
                for s in (0, 1):
                    sp.wait_ge(stored[s], 16 * SLOT_TILES // 2)

            def pairs(eng, step):
                step((0, 0), None)
                step((0, 1), (0, 0))
                with eng.Fori(1, TURNS) as j:
                    step((j, 0), (j - 1, 1))
                    step((j, 1), (j, 0))
                step(None, (TURNS - 1, 1))

            def tiles(pair):
                j, n = pair
                return [(j * 4 + (2 * n + s), s) for s in (0, 1)]

            def experts(eng, pair):
                return [eng.value_load(S.tile_expert[0:1, bass.ds(t, 1)], min_val=0, max_val=E - 1)
                        for t, s in tiles(pair)]

            @block.tensor
            def _(pe):
                for s in (x_mm, h_mm, hT_mm, y_mm):
                    s.open(pe)

                def step(front, back):
                    if front:
                        j, n = front
                        e = experts(pe, front)
                        for t, s in tiles(front):
                            pe.wait_ge(loaded[2 * n + s], j * 16 + 16)
                            xT_ready.wait(pe, t - 2)
                            nc.tensor.transpose(ps[:, XB[s], 0:P], xs[:, 2 * n + s, :], S.ident[:]).then_inc(x_mm.sem, 1)
                    if back:
                        for t, s in tiles(back):
                            h_ready.wait(pe, t)
                            hT_ready.wait(pe, t - 2)
                            for f in range(FC):
                                op = nc.tensor.transpose(ps[:, TB[s], f * P:(f + 1) * P], h[:, s, f * P:(f + 1) * P],
                                                         S.ident[:])
                            op.then_inc(hT_mm.sem, 1)
                    if front:
                        for t, s in tiles(front):
                            xT_ready.wait(pe, t)
                            h_ready.wait(pe, t - 2)
                            nc.tensor.matmul(ps[:, HB[s], :], xsT[:, s, :], S.f1_w1[:, cols(e[s] * F, F)], start=True,
                                             stop=True).then_inc(h_mm.sem, 1)
                    if back:
                        e = experts(pe, back)
                        for t, s in tiles(back):
                            hT_ready.wait(pe, t)
                            y_ready.wait(pe, t - 2)
                            for f in range(FC):
                                op = nc.tensor.matmul(ps[:, YB[s], 0:P], hT[:, s, f * P:(f + 1) * P],
                                                      S.f1_w2[:, cols(e[s] * F + f * P, P)], start=(f == 0),
                                                      stop=(f == FC - 1))
                            op.then_inc(y_mm.sem, 1)

                pairs(pe, step)

            @block.scalar
            def _(act):
                xT_ready.open(act)
                hT_ready.open(act)

                def step(front, back):
                    if front:
                        for t, s in tiles(front):
                            x_mm.wait(act, t)
                            h_mm.wait(act, t - 2)
                            nc.scalar.activation(xsT[:, s, :], ps[:, XB[s], 0:P], ACT.Identity, bias=S.f1_lnb[:],
                                                 scale=S.f1_lng[:]).then_inc(xT_ready.sem, 1)
                    if back:
                        for t, s in tiles(back):
                            hT_mm.wait(act, t)
                            y_mm.wait(act, t - 2)
                            nc.scalar.activation(hT[:, s, :], ps[:, TB[s], :], ACT.Relu).then_inc(hT_ready.sem, 1)

                pairs(act, step)

            @block.vector
            def _(dve):
                h_ready.open(dve)
                y_ready.open(dve)

                def step(front, back):
                    if front:
                        e = experts(dve, front)
                        for t, s in tiles(front):
                            h_mm.wait(dve, t)
                            hT_mm.wait(dve, t - 2)
                            nc.vector.tensor_tensor(h[:, s, :], ps[:, HB[s], :], S.f1_b1[:, cols(e[s] * F, F)],
                                                    ALU.add).then_inc(h_ready.sem, 1)
                    if back:
                        j, n = back
                        e = experts(dve, back)
                        for t, s in tiles(back):
                            y_mm.wait(dve, t)
                            if not (isinstance(j, int) and j + n == 0):
                                dve.wait_ge(stored[s], (j * 2 + n) * 16)
                            nc.vector.tensor_tensor(y[:, s, :], ps[:, YB[s], 0:P], S.f1_b2[:, cols(e[s] * P, P)],
                                                    ALU.add).then_inc(y_ready.sem, 1)

                pairs(dve, step)
        with nc.Block() as block:
            @block.gpsimd
            def _(pool):
                for t in range(TILES):
                    nc.gpsimd.indirect_dma_start(
                        back[:, t * P:(t + 1) * P], None, S.y_slots[:, :],
                        bass.IndirectOffsetOnAxis(ap=S.slot[:, t:t + 1], axis=0)).then_inc(gathered[t // GT], 16)

            @block.vector
            def _(dve):
                for g in range(GROUPS):
                    dve.wait_ge(gathered[g], 16 * GT)
                    for t in range(g * GT, (g + 1) * GT):
                        x = S.x[:, t * P:(t + 1) * P]
                        nc.vector.scalar_tensor_tensor(x, back[:, t * P:(t + 1) * P], S.gate[:, t:t + 1], x,
                                                       ALU.mult, ALU.add)


def best_expert_ffn(nc, S):
    ctx, sb, sem, steps = scope(nc)
    with ctx:
        S.normed2 = sb("normed2", [P, TOK])
        S.gate = sb("gate", [P, TILES])
        S.slot = sb("slot", [P, TILES], I32)
        S.tile_expert = sb("tile_expert", [P, SLOT_TILES], I32)
        route_best(nc, S)
        expert_tiles(nc, S)


def program(nc, a, out, start=0, upto=8):
    S = Shared()
    with ExitStack() as ctx:
        loads = []

        def sb(name, shape, dt=F32):
            return ctx.enter_context(nc.sbuf_tensor(name, shape, dt))

        def weight(name, shape, src=None):
            t = sb("w_" + name, shape)
            loads.append((t[:], a[name] if src is None else src))
            return t

        def column(name):
            return weight(name + "_col", [P, 1], a[name].rearrange("(p o) -> p o", o=1))

        def row(name, times=1):
            n = a[name].shape[0]
            t = sb("w_" + name + "_row", [P, times * n])
            for i in range(times):
                loads.append((t[:, i * n:(i + 1) * n], a[name].partition_broadcast(P)))
            return t

        S.ps = ctx.enter_context(nc.psum_tensor("ps", [P, 8, 512], F32))
        S.x = sb("x_res", [P, TOK])
        loads.append((S.x[:].rearrange("p (t d) -> p t d", d=D), a["x"].rearrange("(t p) d -> p t d", p=P)))
        S.mean, S.rstd = sb("mean", [P, TILES]), sb("rstd", [P, TILES])
        S.eps, S.act_warm = sb("eps", [P, 1]), sb("act_warm", [P, 1])
        S.ident, S.ident_b = sb("ident", [P, P]), sb("ident_b", [P, P], BF16)
        S.head_mask = sb("head_mask", [P, P])
        S.prefix, S.ones_b = sb("prefix", [P, P], BF16), sb("ones_b", [P, P], BF16)
        S.mask_qk, S.mask_kq = sb("mask_qk", [P, P], BF16), sb("mask_kq", [P, P], BF16)
        S.first_rank, S.carry_on = sb("first_rank", [P, TILES * E]), sb("carry_on", [P, E * TILES])
        S.tile_start = sb("tile_start", [P, SLOT_TILES])

        S.a0_wq, S.a0_wkv, S.a0_wc = weight("a0_wqT", [P, D]), weight("a0_wkvT", [P, 2 * D]), weight("a0_wcT", [P, D])
        S.a0_bq, S.a0_bkv, S.a0_bc = column("a0_bq"), row("a0_bkv", 2), row("a0_bc", GT)
        S.a0_bq1 = sb("a0_bq1", [P, 1])
        first_loads = len(loads)

        S.f0_wr, S.f0_wg = weight("f0_wrT", [P, E]), weight("f0_wgT", [P, 2 * P])
        S.f0_wd = sb("f0_wd", [P, 2, E * D])
        loads.append((S.f0_wd[:], a["f0_wdT"].rearrange("(f p) n -> p f n", p=P)))

        S.b0_wq, S.b0_wk, S.b0_wv = weight("b0_wqT", [P, D]), weight("b0_wkT", [P, D]), weight("b0_wvT", [P, D])
        S.b0_bq, S.b0_bk, S.b0_bv = column("b0_bq"), column("b0_bk"), row("b0_bv", GT)
        S.b0_wo, S.b0_bo = weight("b0_woT", [P, D]), row("b0_bo", GT)

        S.a1_wq, S.a1_bq, S.a1_wkl = weight("a1_wq", [P, D]), column("a1_bq"), weight("a1_wkl", [LATENT, H * D])
        S.a1_bkl, S.a1_wc = weight("a1_bkl", [LATENT, H]), weight("a1_wcT", [LATENT, HD])
        S.a1_wk2, S.a1_bk2 = sb("a1_wk2", [P, P]), sb("a1_bk2", [P, 1])
        S.a1_wv, S.a1_bv = weight("a1_wv", [P, H * LATENT]), row("a1_bv")
        S.a1_wo = sb("a1_wo", [P, H * LATENT // P, D])
        loads.append((S.a1_wo[:], a["a1_wo"].rearrange("(f p) n -> p f n", p=P)))
        S.a1_bo = row("a1_bo", GT)
        S.b1_wq, S.b1_wk, S.b1_wv = weight("b1_wqT", [P, D]), weight("b1_wkT", [P, D]), weight("b1_wvT", [P, D])
        S.b1_bq, S.b1_bk, S.b1_bv = column("b1_bq"), column("b1_bk"), row("b1_bv", GT)
        S.b1_wo, S.b1_bo = weight("b1_woT", [P, D]), row("b1_bo", GT)
        S.f1_wr, S.f1_br = weight("f1_wr", [P, E]), row("f1_br")
        S.f1_lng, S.f1_lnb = column("f1_lng"), column("f1_lnb")
        S.f1_w1, S.f1_b1 = weight("f1_w1", [P, E * 4 * P]), row("f1_b1")
        S.f1_w2, S.f1_b2 = weight("f1_w2", [P, E * 4 * P]), row("f1_b2")
        S.zeros = sb("zeros", [P, D])

        S.x_slots = nc.dram_tensor("x_slots", [SLOT_TILES * P, D], F32)
        S.y_slots = nc.dram_tensor("y_slots", [SLOT_TILES * P, D], F32)
        S.q_parts = nc.dram_tensor("q_parts", [BATCH, PARTS, H, HD, SEQ], BF16)
        S.k_parts = nc.dram_tensor("k_parts", [BATCH, PARTS, H, HD, SEQ], BF16)
        S.v_heads = nc.dram_tensor("v_heads", [HEADS, P, LATENT * SEQ // P], F32)
        S.o_quads = nc.dram_tensor("o_quads", [HEADS, P, GROUP], F32)
        S.o_wide = nc.dram_tensor("o_wide", [HEADS, LATENT + 1, SEQ], F32)
        S.r_wide = nc.dram_tensor("r_wide", [2, HEADS, GROUP], F32)
        S.r_sums = nc.dram_tensor("r_sums", [HEADS, 2, GROUP], F32)

        if start == 0:
            S.late_loads = loads[first_loads:]
            loads = loads[:first_loads]
        load_phase(nc, S, loads)
        with nc.Block() as block:
            @block.vector
            def _(dve):
                nc.vector.tensor_scalar(S.a0_bq1[:], S.a0_bq[:], 1.0, None, ALU.add)
                nc.vector.memset(S.eps[:], EPS)
        if start > 0:
            with nc.Block() as block:
                @block.sync
                def _(sp):
                    q=nc.alloc_semaphore("tq")
                    sp.dma_start(S.x_slots[:, :].rearrange("(t p) d -> p t d", p=P),
                             S.zeros[:].rearrange("p (o d) -> p o d", o=1).broadcast_to([P, SLOT_TILES, D])
                             ).then_inc(q, 16)
                    sp.wait_ge(q, 16)
        layers = (linear_attention, routed_pair_ffn, full_attention, routed_pair_ffn,
                  causal_attention, best_expert_ffn, row_attention, best_expert_ffn)
        for layer in layers[start:upto]:
            norm_stats(nc, S)
            layer(nc, S)
        store_phase(nc, S, out)


SLOT_TILES = 40


def arrays_of(i):
    import numpy as np

    def T(w):
        return np.ascontiguousarray(w.T)

    g = {k: np.asarray(v) for k, v in i.items()}
    w_in = g["L1_attn_b_w_in"].reshape(H, PARTS, HD, D)
    b_in = g["L1_attn_b_b_in"].reshape(H, PARTS, HD)
    return {
        **{f"b1_w{c}T": T(w_in[:, n].reshape(D, D)) for n, c in enumerate("qkv")},
        **{f"b1_b{c}": b_in[:, n].reshape(D) for n, c in enumerate("qkv")},
        "b1_woT": T(g["L1_attn_b_w_out"]),
        "b1_bo": g["L1_attn_b_b_out"],
        "a1_wq": g["L1_attn_a_Wq"],
        "a1_bq": g["L1_attn_a_bq"],
        "a1_wkl": g["L1_attn_a_Wk"].reshape(D, H, LATENT).transpose(2, 1, 0).reshape(LATENT, H * D),
        "a1_bkl": T(g["L1_attn_a_bk"].reshape(H, LATENT)),
        "a1_wcT": T(g["L1_attn_a_Wc"]),
        "a1_wv": g["L1_attn_a_Wv"],
        "a1_bv": g["L1_attn_a_bv"],
        "a1_wo": g["L1_attn_a_Wo"],
        "a1_bo": g["L1_attn_a_bo"],
        "f1_wr": g["L1_ffn_Wr"],
        "f1_br": g["L1_ffn_br"],
        "f1_lng": g["L1_ffn_ln_g"],
        "f1_lnb": g["L1_ffn_ln_b"],
        "f1_w1": g["L1_ffn_W1"].transpose(1, 0, 2).reshape(D, E * 4 * P),
        "f1_b1": g["L1_ffn_b1"].reshape(E * 4 * P),
        "f1_w2": g["L1_ffn_W2"].reshape(E, 4, P, D).transpose(2, 0, 1, 3).reshape(P, E * 4 * D),
        "f1_b2": g["L1_ffn_b2"].reshape(E * D),
        "x": g["L0_attn_a_x"].reshape(TOK, D),
        "a0_wqT": T(g["L0_attn_a_Wq"]),
        "a0_wkvT": np.concatenate([T(g["L0_attn_a_Wk"]), T(g["L0_attn_a_Wv"])], axis=1),
        "a0_bkv": np.concatenate([g["L0_attn_a_bk"], g["L0_attn_a_bv"]]),
        "a0_bq": g["L0_attn_a_bq"],
        "a0_wcT": T(g["L0_attn_a_Wc"]),
        "a0_bc": g["L0_attn_a_bc"],
        **{f"b0_w{c}T": T(g[f"L0_attn_b_W{c}"]) for c in "qkvo"},
        **{f"b0_b{c}": g[f"L0_attn_b_b{c}"] for c in "qkvo"},
        "f0_wrT": T(g["L0_ffn_w_router"]),
        "f0_wgT": T(g["L0_ffn_w_gate"]),
        "f0_wdT": np.ascontiguousarray(g["L0_ffn_w_down"].transpose(2, 0, 1)).reshape(2 * P, E * D),
    }


def kernel(**inputs):
    import numpy as np
    import concourse.bacc as bacc
    from concourse.bass_utils import run_bass_kernel_spmd

    nc = bacc.Bacc("TRN2", target_bir_lowering=False, num_devices=1)
    arrays = {f"in_{k}": v for k, v in arrays_of(inputs).items()}
    a = {k[3:]: nc.dram_tensor(k, v.shape, mybir.dt.from_np(v.dtype), kind="ExternalInput").ap()
         for k, v in arrays.items()}
    out = nc.dram_tensor("out", (BATCH, SEQ, D), F32, kind="ExternalOutput").ap()
    program(nc, a, out)
    r = run_bass_kernel_spmd(nc, [arrays], core_ids=[0])
    return r.results[0]["out"]
```

```python
import concourse.bass as bass
from concourse import mybir
from contextlib import ExitStack

F32 = mybir.dt.float32
BF16 = mybir.dt.bfloat16
I32 = mybir.dt.int32
ALU = mybir.AluOpType
ACT = mybir.ActivationFunctionType
AX = mybir.AxisListType

P = 128
BATCH, SEQ, D = 4, 1024, 128
TOK = BATCH * SEQ
TILES = TOK // P
GROUP = 512
GROUPS = TOK // GROUP
GT = GROUP // P
PAIRS = GROUPS // 2
H, HD = 16, 8
E = 8
EPS = 1e-5


class Chain:

    def __init__(self, eng, sem, turn=0, per_turn=0, before=0):
        self.eng, self.sem, self.turn, self.per_turn, self.before, self.n = eng, sem, turn, per_turn, before, 0

    def run(self, op):
        self.n += 1
        op.then_inc(self.sem, 1)
        self.eng.wait_ge(self.sem, self.turn * self.per_turn + self.before + self.n)

    def end(self):
        assert self.per_turn == 0 or self.n == self.per_turn, self.n


def cols(start, n):
    return bass.ds(start, n)


LEAD = 8


class Steps:

    def __init__(self, sem):
        self.sem = sem

    def open(self, eng):
        eng.sem_inc(self.sem, LEAD)

    def after(self, n):
        return n + (LEAD + 1)

    def wait(self, eng, n):
        eng.wait_ge(self.sem, self.after(n))


class Shared:
    pass


def scope(nc):
    ctx = ExitStack()
    phase = nc.next_id()

    def sb(name, shape, dt=F32):
        return ctx.enter_context(nc.sbuf_tensor(f"{name}_{phase}", shape, dt))

    sems = []

    def close():
        if sems:
            nc.clear_and_free_semaphores(sems)
            nc.all_engine_barrier()

    ctx.callback(close)

    def sem(name):
        sems.append(nc.alloc_semaphore(f"{name}_{phase}"))
        return sems[-1]

    def steps(name):
        return Steps(sem(name))

    return ctx, sb, sem, steps


def load_phase(nc, S, loads):
    ctx, sb, sem, steps = scope(nc)
    with ctx:
        loaded, made = sem("loaded"), sem("made")
        with nc.Block() as block:
            @block.sync
            def _(sp):
                for dst, src in loads:
                    sp.dma_start(dst, src).then_inc(loaded, 16)
                sp.wait_ge(loaded, 16 * len(loads))

            @block.gpsimd
            def _(pool):
                c = Chain(pool, made)
                for m in (S.ident, S.ident_b):
                    c.run(nc.gpsimd.memset(m[:], 0.0))
                    c.run(nc.gpsimd.affine_select(out=m[:], in_=m[:], compare_op=ALU.not_equal, fill=1.0, base=0,
                                                  pattern=[[-1, P]], channel_multiplier=1))
                c.run(nc.gpsimd.memset(S.zeros[:], 0.0))
                c.run(nc.gpsimd.memset(S.head_mask[:], 1.0))
                v = S.head_mask[:].rearrange("p (h d) -> p h d", h=H)
                c.run(nc.gpsimd.affine_select(out=v, in_=v, compare_op=ALU.is_ge, fill=0.0, base=0,
                                              pattern=[[-HD, H], [0, HD]], channel_multiplier=1))
                c.run(nc.gpsimd.affine_select(out=v, in_=v, compare_op=ALU.is_ge, fill=0.0, base=HD - 1,
                                              pattern=[[HD, H], [0, HD]], channel_multiplier=-1))
                c.run(nc.gpsimd.memset(S.prefix[:], 1.0))
                c.run(nc.gpsimd.affine_select(out=S.prefix[:], in_=S.prefix[:], compare_op=ALU.is_ge, fill=0.0,
                                              base=0, pattern=[[1, P]], channel_multiplier=-1))
                c.run(nc.gpsimd.memset(S.ones_b[:], 1.0))
                for m, sign in ((S.mask_qk, -1), (S.mask_kq, 1)):
                    c.run(nc.gpsimd.memset(m[:], 0.0))
                    c.run(nc.gpsimd.affine_select(out=m[:], in_=m[:], compare_op=ALU.is_ge, fill=MASKED, base=0,
                                                  pattern=[[sign, P]], channel_multiplier=-sign))
                c.run(nc.gpsimd.iota(S.first_rank[:], pattern=[[-1, E]], base=E, channel_multiplier=0,
                                     allow_small_or_imprecise_dtypes=True))
                c.run(nc.gpsimd.memset(S.carry_on[:], 1.0))
                c.run(nc.gpsimd.memset(S.carry_on[:].rearrange("p (e t) -> p e t", e=E)[:, :, 0:1], 0.0))
                c.run(nc.gpsimd.iota(S.tile_start[:], pattern=[[P, S.tile_start.shape[1]]], base=0,
                                     channel_multiplier=0, allow_small_or_imprecise_dtypes=True))


MASKED = -3.0e38


def tile_stats(nc, S, t):
    return nc.vector.bn_stats(S.st[:, cols(t * 6, 6)], S.x[:, cols(t * P, P)])


def group_stats(nc, S, g):
    for k in range(GT):
        tile_stats(nc, S, g * GT + k)


def stats_tail(nc, dve, c, st, tmp, mean, rstd, var_ready, std_ready):
    stv = st[:].rearrange("p (t s) -> p s t", s=6)
    c.run(nc.vector.tensor_tensor(tmp[:, 1], stv[:, 1], stv[:, 4], ALU.subtract))
    nc.vector.tensor_tensor(tmp[:, 2], stv[:, 2], stv[:, 5], ALU.add)
    c.run(nc.vector.tensor_tensor(tmp[:, 0], stv[:, 1], stv[:, 4], ALU.add))
    nc.vector.tensor_scalar(mean[:], tmp[:, 0], 0.5, None, ALU.mult)
    c.run(nc.vector.tensor_tensor(tmp[:, 3], tmp[:, 1], tmp[:, 1], ALU.mult))
    nc.vector.scalar_tensor_tensor(tmp[:, 2], tmp[:, 3], float(D // 4), tmp[:, 2], ALU.mult,
                                   ALU.add).then_inc(var_ready, 1)
    dve.wait_ge(std_ready, 1)
    c.run(nc.vector.reciprocal(rstd[:], tmp[:, 1]))


def norm_stats(nc, S):
    ctx, sb, sem, steps = scope(nc)
    with ctx:
        tmp = sb("bn_tmp", [P, 4, TILES])
        chain, var_ready, std_ready = sem("chain"), sem("var_ready"), sem("std_ready")
        with nc.Block() as block:
            @block.vector
            def _(dve):
                stats_tail(nc, dve, Chain(dve, chain), S.st, tmp, S.mean, S.rstd, var_ready, std_ready)

            @block.scalar
            def _(act):
                act.wait_ge(var_ready, 1)
                nc.scalar.activation(tmp[:, 1], tmp[:, 2], ACT.Sqrt, bias=S.eps[:], scale=1.0 / D).then_inc(std_ready, 1)


def normalize_tile(nc, S, out, t):
    return nc.vector.tensor_scalar(out, S.x[:, cols(t * P, P)], S.mean[:, cols(t, 1)], S.rstd[:, cols(t, 1)],
                                   ALU.subtract, ALU.mult)


def linear_attention(nc, S):
    ctx, sb, sem, steps = scope(nc)
    ps = S.ps
    VA = 2 * P + 1
    SW = P + H
    with ctx:
        xn = sb("xn", [P, 2, GROUP])
        xT = sb("xT", [P, 2, GROUP])
        qT = sb("qT", [P, 2, GROUP])
        qneg = sb("qneg", [P, 2, GROUP])
        kv = sb("kv", [P, 2, GT, VA])
        kneg = sb("kneg", [P, 2, GT, P])
        ksum = sb("ksum", [P, 1])
        state = sb("state", [P, SW])
        den = sb("den", [P, GT * H])
        y = sb("y", [P, 2, GROUP])
        yT = sb("yT", [P, 2, GROUP])
        chain, late_loaded, cleared = sem("chain"), sem("late_loaded"), sem("cleared")
        (normed, transposed, xT_ready, q_mm, q_neg, q_exp, q_ready, kv_mm, kv_biased, k_exp, k_ready, s_mm, s_ready,
         n_mm, y_ready, yT_mm, yT_ready, o_mm, x_ready, x_biased) = [steps(n) for n in (
             "normed transposed xT_ready q_mm q_neg q_exp q_ready kv_mm kv_biased k_exp k_ready s_mm s_ready "
             "n_mm y_ready yT_mm yT_ready o_mm x_ready x_biased").split()]
        T, Q, KV, ST, NUM, YT = 0, 1, (2, 3), 4, (5, 6), 7
        with nc.Block() as block:
            @block.sync
            def _(sp):
                for dst, src in S.late_loads:
                    sp.dma_start(dst, src).then_inc(late_loaded, 16)
                sp.dma_start(S.x_slots[:, :].rearrange("(t p) d -> p t d", p=P),
                             S.zeros[:].rearrange("p (o d) -> p o d", o=1).broadcast_to([P, SLOT_TILES, D])
                             ).then_inc(cleared, 16)
                sp.wait_ge(late_loaded, 16 * len(S.late_loads))
                sp.wait_ge(cleared, 16)

            @block.tensor
            def _(pe):
                for s in (transposed, q_mm, kv_mm, s_mm, n_mm, yT_mm, o_mm):
                    s.open(pe)

                def transpose(b, s):
                    g = b * 2 + s
                    normed.wait(pe, g)
                    xT_ready.wait(pe, g - 1)
                    for k in range(GT):
                        op = nc.tensor.transpose(ps[:, T, k * P:(k + 1) * P], xn[:, s, k * P:(k + 1) * P], S.ident[:])
                    op.then_inc(transposed.sem, 1)

                def batch(b, last):
                    for s in (0, 1):
                        g = b * 2 + s
                        if s == 1:
                            transpose(b, 1)
                        xT_ready.wait(pe, g)
                        q_ready.wait(pe, g - 1)
                        nc.tensor.matmul(ps[:, Q, :], S.a0_wq[:], xT[:, s, :], start=True, stop=True).then_inc(q_mm.sem, 1)
                        for half in (0, 1):
                            kv_biased.wait(pe, g * 2 + half - 2)
                            for k in (0, 1):
                                op = nc.tensor.matmul(ps[:, KV[half], k * 2 * P:(k + 1) * 2 * P],
                                                      xT[:, s, (2 * half + k) * P:(2 * half + k + 1) * P],
                                                      S.a0_wkv[:], start=True, stop=True)
                            op.then_inc(kv_mm.sem, 1)
                    x_ready.wait(pe, b * 2 - 1)
                    for s in (0, 1):
                        k_ready.wait(pe, b * 2 + s)
                        for k in range(GT):
                            op = nc.tensor.matmul(ps[:, ST, 0:P + 1], kv[:, s, k, 0:P], kv[:, s, k, P:VA],
                                                  start=(s == 0 and k == 0), stop=(s == 1 and k == GT - 1))
                    op.then_inc(s_mm.sem, 1)
                    s_ready.wait(pe, b)
                    for s in (0, 1):
                        g = b * 2 + s
                        q_ready.wait(pe, g)
                        for half in (0, 1):
                            y_ready.wait(pe, g * 2 + half - 2)
                            for k in (0, 1):
                                op = nc.tensor.matmul(ps[:, NUM[half], k * SW:(k + 1) * SW],
                                                      qT[:, s, (2 * half + k) * P:(2 * half + k + 1) * P],
                                                      state[:], start=True, stop=True)
                            op.then_inc(n_mm.sem, 1)
                    for s in (0, 1):
                        g = b * 2 + s
                        y_ready.wait(pe, g * 2 + 1)
                        yT_ready.wait(pe, g - 1)
                        for k in range(GT):
                            op = nc.tensor.transpose(ps[:, YT, k * P:(k + 1) * P], y[:, s, k * P:(k + 1) * P], S.ident[:])
                        op.then_inc(yT_mm.sem, 1)
                        if s == 0 and not last:
                            transpose(b + 1, 0)
                        yT_ready.wait(pe, g)
                        x_ready.wait(pe, g - 1)
                        for k in range(GT):
                            op = nc.tensor.matmul(ps[:, ST, k * P:(k + 1) * P], yT[:, s, k * P:(k + 1) * P],
                                                  S.a0_wc[:], start=True, stop=True)
                        op.then_inc(o_mm.sem, 1)

                transpose(0, 0)
                with pe.Fori(0, BATCH - 1) as b:
                    batch(b, False)
                batch(BATCH - 1, True)

            @block.scalar
            def _(act):
                for s in (xT_ready, q_exp, k_exp, yT_ready):
                    s.open(act)
                nc.scalar.activation(S.act_warm[:], S.eps[:], ACT.Exp)

                def evacuate(b, s):
                    g = b * 2 + s
                    transposed.wait(act, g)
                    nc.scalar.activation(xT[:, s, :], ps[:, T, :], ACT.Copy).then_inc(xT_ready.sem, 1)

                def batch(b, last):
                    for s in (0, 1):
                        g = b * 2 + s
                        if s == 1:
                            evacuate(b, 1)
                        q_neg.wait(act, g)
                        nc.scalar.activation(qneg[:, s, :], qneg[:, s, :], ACT.Exp).then_inc(q_exp.sem, 1)
                        kv_biased.wait(act, g * 2 + 1)
                        nc.scalar.activation(kneg[:, s, :, :], kneg[:, s, :, :], ACT.Exp).then_inc(k_exp.sem, 1)
                    for s in (0, 1):
                        g = b * 2 + s
                        yT_mm.wait(act, g)
                        nc.scalar.activation(yT[:, s, :], ps[:, YT, :], ACT.Copy).then_inc(yT_ready.sem, 1)
                        if s == 0 and not last:
                            evacuate(b + 1, 0)

                evacuate(0, 0)
                with act.Fori(0, BATCH - 1) as b:
                    batch(b, False)
                batch(BATCH - 1, True)

            @block.gpsimd
            def _(pool):
                x_biased.open(pool)
                with pool.Fori(0, GROUPS) as g:
                    normed.wait(pool, g)
                    nc.gpsimd.tensor_tensor(S.x[:, cols(g * GROUP, GROUP)], S.x[:, cols(g * GROUP, GROUP)],
                                            S.a0_bc[:], ALU.add).then_inc(x_biased.sem, 1)

            @block.vector
            def _(dve):
                for s in (normed, q_neg, q_ready, kv_biased, k_ready, s_ready, y_ready, x_ready):
                    s.open(dve)
                c0 = Chain(dve, chain)
                c0.run(nc.vector.memset(kv[:, :, :, 2 * P:VA], 1.0))

                def normalize(b, s):
                    g = b * 2 + s
                    transposed.wait(dve, g - 2)
                    for k in range(GT):
                        op = normalize_tile(nc, S, xn[:, s, k * P:(k + 1) * P], g * GT + k)
                    op.then_inc(normed.sem, 1)

                def batch(b, last):
                    c = Chain(dve, chain, b, 14, 1)
                    for s in (0, 1):
                        g = b * 2 + s
                        q_mm.wait(dve, g)
                        nc.vector.tensor_scalar(qneg[:, s, :], ps[:, Q, :], S.a0_bq[:], 0.0, ALU.add,
                                                ALU.min).then_inc(q_neg.sem, 1)
                        for half in (0, 1):
                            kv_mm.wait(dve, g * 2 + half)
                            z = kv[:, s, 2 * half:2 * half + 2, :]
                            c.run(nc.vector.tensor_tensor(z[:, :, 0:2 * P],
                                                          ps[:, KV[half], :].rearrange("p (t c) -> p t c", t=2),
                                                          S.a0_bkv[:].rearrange("p (t c) -> p t c", t=2), ALU.add))
                            nc.vector.tensor_scalar(kneg[:, s, 2 * half:2 * half + 2, :], z[:, :, 0:P], 0.0, None,
                                                    ALU.min).then_inc(kv_biased.sem, 1)
                        q_exp.wait(dve, g)
                        nc.vector.scalar_tensor_tensor(qT[:, s, :], ps[:, Q, :], S.a0_bq1[:], qneg[:, s, :], ALU.add,
                                                       ALU.max).then_inc(q_ready.sem, 1)
                        k_exp.wait(dve, g)
                        nc.vector.scalar_tensor_tensor(kv[:, s, :, 0:P], kv[:, s, :, 0:P], 1.0, kneg[:, s, :, :],
                                                       ALU.add, ALU.max).then_inc(k_ready.sem, 1)
                    s_mm.wait(dve, b)
                    c.run(nc.vector.tensor_copy(ksum[:], ps[:, ST, P:P + 1]))
                    c.run(nc.vector.tensor_tensor(state[:, 0:P], ps[:, ST, 0:P], S.head_mask[:], ALU.mult))
                    nc.vector.tensor_scalar(state[:, P:SW], S.head_mask[:].rearrange("p (h d) -> p h d", h=H)[:, :, 0],
                                            ksum[:], None, ALU.mult).then_inc(s_ready.sem, 1)
                    for s in (0, 1):
                        g = b * 2 + s
                        for half in (0, 1):
                            n_mm.wait(dve, g * 2 + half)
                            num = ps[:, NUM[half], 0:2 * SW].rearrange("p (t c) -> p t c", t=2)
                            r = den[:, half * 2 * H:(half + 1) * 2 * H]
                            c.run(nc.vector.tensor_scalar(r.rearrange("p (t h) -> p t h", t=2), num[:, :, P:SW], 1e-6,
                                                          None, ALU.add))
                            c.run(nc.vector.reciprocal(r, r))
                            for k in (0, 1):
                                o = y[:, s, (2 * half + k) * P:(2 * half + k + 1) * P].rearrange("p (h d) -> p h d", h=H)
                                op = nc.vector.tensor_tensor(
                                    o, num[:, k, 0:P].rearrange("p (h d) -> p h d", h=H),
                                    r[:, k * H:(k + 1) * H].rearrange("p (h o) -> p h o", o=1).broadcast_to([P, H, HD]),
                                    ALU.mult)
                            op.then_inc(y_ready.sem, 1)
                    for s in (0, 1):
                        g = b * 2 + s
                        if not last:
                            normalize(b + 1, s)
                        o_mm.wait(dve, g)
                        x_biased.wait(dve, g)
                        nc.vector.tensor_tensor(S.x[:, cols(g * GROUP, GROUP)], S.x[:, cols(g * GROUP, GROUP)],
                                                ps[:, ST, :], ALU.add).then_inc(x_ready.sem, 1)
                    c.end()

                for s in (0, 1):
                    normalize(0, s)
                with dve.Fori(0, BATCH - 1) as b:
                    batch(b, False)
                batch(BATCH - 1, True)
                x_ready.wait(dve, GROUPS - 1)
                for g in range(GROUPS):
                    group_stats(nc, S, g)


def store_phase(nc, S, out):
    ctx, sb, sem, steps = scope(nc)
    with ctx:
        stored = sem("stored")
        with nc.Block() as block:
            @block.sync
            def _(sp):
                sp.dma_start(out.rearrange("b (t p) d -> p (b t) d", p=P),
                             S.x[:].rearrange("p (t d) -> p t d", d=D)).then_inc(stored, 16)
                sp.wait_ge(stored, 16)


def bcast(v, n):
    return v.rearrange("p (a o) -> p a o", o=1).broadcast_to([P, v.shape[-1], n])


def by_tile(v):
    return v.rearrange("p (t e) -> p t e", e=E)


def by_expert(v):
    return v.rearrange("p (t e) -> p e t", e=E)


def per_expert(v, n=TILES):
    return v.rearrange("p (o e) -> p o e", o=1).broadcast_to([P, n, E])


def softmax_start(nc, dve, c, logits, mx, shifted):
    c.run(nc.vector.tensor_reduce(mx, logits, AX.X, ALU.max))
    return nc.vector.tensor_tensor(by_tile(shifted), logits, bcast(mx, E), ALU.subtract)


def softmax_end(nc, c, exped, total, gates):
    c.run(nc.vector.tensor_reduce(total, by_tile(exped), AX.X, ALU.add))
    c.run(nc.vector.reciprocal(total, total))
    c.run(nc.vector.tensor_tensor(by_tile(gates), by_tile(exped), bcast(total, E), ALU.mult))


def pick_largest(nc, S, c, values, mx, work, onehot, largest=None):
    largest = mx if largest is None else largest
    c.run(nc.vector.tensor_reduce(largest, by_tile(values), AX.X, ALU.max))
    c.run(nc.vector.tensor_tensor(by_tile(work), by_tile(values), bcast(largest, E), ALU.is_equal))
    c.run(nc.vector.tensor_tensor(by_tile(work), by_tile(work), per_expert(S.first_rank[:]), ALU.mult))
    c.run(nc.vector.tensor_reduce(mx, by_tile(work), AX.X, ALU.max))
    c.run(nc.vector.tensor_tensor(by_tile(onehot), by_tile(work), bcast(mx, E), ALU.is_equal))


def count_matmuls(nc, S, bank, mask):
    W = TILES * E
    nc.tensor.matmul(bank[:, 0:W], S.prefix[:], mask, start=True, stop=True)
    return nc.tensor.matmul(bank[:, W:2 * W], S.ones_b[:], mask, start=True, stop=True)


def running_counts(nc, S, c, counts, totals, summed, cum):
    W = TILES * E
    c.run(nc.vector.tensor_copy(totals.rearrange("p (e t) -> p e t", e=E), by_expert(counts[:, W:2 * W])))
    c.run(nc.vector.tensor_tensor_scan(summed, S.carry_on[:], totals, 0.0, ALU.mult, ALU.add))
    c.run(nc.vector.tensor_tensor(totals, summed, totals, ALU.subtract))
    c.run(nc.vector.tensor_tensor(by_expert(cum), by_expert(counts[:, 0:W]),
                                  totals.rearrange("p (e t) -> p e t", e=E), ALU.add))


def routed_pair_ffn(nc, S):
    CAP = float(-(-TOK * 5 // (E * 4)))
    FC = 2
    ctx, sb, sem, steps = scope(nc)
    ps = S.ps
    HB, L, C, T, YB = (0, 1), 2, 3, (4, 5), 4
    W = TILES * E
    with ctx:
        xn = sb("xn", [P, 2, GROUP])
        xT = sb("xT", [P, TOK])
        xTs = sb("xT_stationary", [P, 2, GROUP])
        hT = sb("hT", [P, 2, FC, GROUP])
        mx, total = sb("mx", [P, TILES]), sb("total", [P, TILES])
        exped, gates, work, rest = sb("exped", [P, W]), sb("gates", [P, W]), sb("work", [P, W]), sb("rest", [P, W])
        best, second, mask = sb("best", [P, W]), sb("second", [P, W]), sb("mask", [P, W], BF16)
        totals, summed, cum = sb("totals", [P, W]), sb("summed", [P, W]), sb("cum", [P, W])
        comb = sb("comb", [P, W])
        other = sb("other", [P, 2, P])
        chain, shifted, exp_done, masked, counted, x_chain, other_chain = [sem(n) for n in (
            "chain shifted exp_done masked counted x_chain other_chain").split()]
        normed, transposed, xTs_ready, xT_ready, logits_mm, h_mm, h_ready, y_mm, y_added, joined = [steps(n) for n in (
            "normed transposed xTs_ready xT_ready logits_mm h_mm h_ready y_mm y_added joined").split()]

        with nc.Block() as block:
            @block.tensor
            def _(pe):
                for s in (transposed, logits_mm, h_mm, y_mm):
                    s.open(pe)

                def transpose(g, s):
                    normed.wait(pe, g)
                    xTs_ready.wait(pe, g - 2)
                    for k in range(GT):
                        op = nc.tensor.transpose(ps[:, T[s], k * P:(k + 1) * P], xn[:, s, k * P:(k + 1) * P],
                                                 S.ident[:])
                    op.then_inc(transposed.sem, 1)

                with pe.Fori(0, PAIRS) as b:
                    for s in (0, 1):
                        transpose(b * 2 + s, s)
                    for s in (0, 1):
                        g = b * 2 + s
                        xTs_ready.wait(pe, g)
                        for k in range(GT):
                            op = nc.tensor.matmul(ps[:, L, cols((g * GT + k) * E, E)],
                                                  xTs[:, s, k * P:(k + 1) * P], S.f0_wr[:], start=True, stop=True)
                        op.then_inc(logits_mm.sem, 1)

                def hidden(g, s):
                    h_ready.wait(pe, g * FC - 1)
                    for f in range(FC):
                        nc.tensor.matmul(ps[:, HB[f], :], S.f0_wg[:, f * P:(f + 1) * P],
                                         xT[:, cols(g * GROUP, GROUP)], start=True, stop=True).then_inc(h_mm.sem, 1)

                def experts(g, s, more=True):
                    h_ready.wait(pe, g * FC + FC - 1)
                    for k in range(GT):
                        for half in (0, 1):
                            if half == 0:
                                y_added.wait(pe, g * GT + k - 2)
                            for f in range(FC):
                                op = nc.tensor.matmul(ps[:, YB + 2 * (k % 2) + half, :],
                                                      hT[:, s, f, k * P:(k + 1) * P],
                                                      S.f0_wd[:, f, half * GROUP:(half + 1) * GROUP],
                                                      start=(f == 0), stop=(f == FC - 1))
                            op.then_inc(y_mm.sem, 1)
                        if k == 1 and more:
                            hidden(g + 1, 1 - s)

                xT_ready.wait(pe, GROUPS - 1)
                hidden(0, 0)
                pe.wait_ge(masked, 1)
                count_matmuls(nc, S, ps[:, C, :], mask[:]).then_inc(counted, 1)
                with pe.Fori(0, PAIRS - 1) as j:
                    for s in (0, 1):
                        experts(j * 2 + s, s)
                experts(GROUPS - 2, 0)
                experts(GROUPS - 1, 1, False)

            @block.scalar
            def _(act):
                for s in (xTs_ready, h_ready):
                    s.open(act)
                nc.scalar.activation(S.act_warm[:], S.eps[:], ACT.Exp)
                with act.Fori(0, PAIRS) as b:
                    for s in (0, 1):
                        g = b * 2 + s
                        transposed.wait(act, g)
                        logits_mm.wait(act, g - 2)
                        xT_ready.wait(act, g - 2)
                        nc.scalar.activation(xTs[:, s, :], ps[:, T[s], :], ACT.Copy).then_inc(xTs_ready.sem, 1)
                act.wait_ge(shifted, 1)
                nc.scalar.activation(exped[:], exped[:], ACT.Exp).then_inc(exp_done, 1)
                with act.Fori(0, PAIRS) as b:
                    for s in (0, 1):
                        g = b * 2 + s
                        y_mm.wait(act, (g - 1) * GT * 2 - 1)
                        for f in range(FC):
                            h_mm.wait(act, g * FC + f)
                            nc.scalar.activation(hT[:, s, f, :], ps[:, HB[f], :], ACT.Silu).then_inc(h_ready.sem, 1)

            @block.vector
            def _(dve):
                for s in (normed, xT_ready, y_added):
                    s.open(dve)
                with dve.Fori(0, PAIRS) as b:
                    for s in (0, 1):
                        g = b * 2 + s
                        transposed.wait(dve, g - 2)
                        for k in range(GT):
                            op = normalize_tile(nc, S, xn[:, s, k * P:(k + 1) * P], g * GT + k)
                        op.then_inc(normed.sem, 1)
                    for s in (0, 1):
                        g = b * 2 + s
                        xTs_ready.wait(dve, g)
                        nc.vector.tensor_copy(xT[:, cols(g * GROUP, GROUP)], xTs[:, s, :]).then_inc(xT_ready.sem, 1)
                logits_mm.wait(dve, GROUPS - 1)
                c = Chain(dve, chain)
                softmax_start(nc, dve, c, by_tile(ps[:, L, 0:W]), mx[:], exped[:]).then_inc(shifted, 1)
                dve.wait_ge(exp_done, 1)
                softmax_end(nc, c, exped[:], total[:], gates[:])
                pick_largest(nc, S, c, gates[:], mx[:], work[:], best[:])
                c.run(nc.vector.scalar_tensor_tensor(rest[:], best[:], -2.0, gates[:], ALU.mult, ALU.add))
                pick_largest(nc, S, c, rest[:], mx[:], work[:], second[:])
                nc.vector.tensor_tensor(mask[:], best[:], second[:], ALU.add).then_inc(masked, 1)
                dve.wait_ge(counted, 1)
                running_counts(nc, S, c, ps[:, C, :], totals[:], summed[:], cum[:])
                c.run(nc.vector.scalar_tensor_tensor(cum[:], cum[:], CAP, mask[:], ALU.is_le, ALU.mult))
                c.run(nc.vector.tensor_tensor(work[:], cum[:], gates[:], ALU.mult))
                c.run(nc.vector.tensor_reduce(total[:], by_tile(work[:]), AX.X, ALU.add))
                c.run(nc.vector.tensor_scalar(total[:], total[:], 1e-6, None, ALU.add))
                c.run(nc.vector.reciprocal(total[:], total[:]))
                c.run(nc.vector.tensor_tensor(by_tile(comb[:]), by_tile(work[:]), bcast(total[:], E), ALU.mult))
                def turn(j, first):
                    for k in (0, 1):
                        t = j * 2 + k
                        xt = S.x[:, cols(t * P, P)]
                        y_mm.wait(dve, t * 2 + 1)
                        for e in range(E // 2):
                            if e > 0:
                                dve.wait_ge(x_chain, t * 3 + e)
                            op = nc.vector.scalar_tensor_tensor(
                                xt, ps[:, YB + 2 * k, e * P:(e + 1) * P], comb[:, cols(t * E + e, 1)], xt, ALU.mult,
                                ALU.add)
                            if e < E // 2 - 1:
                                op.then_inc(x_chain, 1)
                            y = ps[:, YB + 2 * k + 1, e * P:(e + 1) * P]
                            gate = comb[:, cols(t * E + (E // 2 + e), 1)]
                            if e == 0:
                                joined.wait(dve, t - 2)
                                op = nc.vector.tensor_scalar(other[:, k, :], y, gate, None, ALU.mult)
                            else:
                                dve.wait_ge(other_chain, t * 3 + e)
                                op = nc.vector.scalar_tensor_tensor(other[:, k, :], y, gate, other[:, k, :], ALU.mult,
                                                                    ALU.add)
                            op.then_inc(other_chain if e < E // 2 - 1 else y_added.sem, 1)
                        if not (first and k == 0):
                            joined.wait(dve, t - 1)
                            tile_stats(nc, S, t - 1)

                turn(0, True)
                with dve.Fori(1, TILES // 2) as j:
                    turn(j, False)
                joined.wait(dve, TILES - 1)
                tile_stats(nc, S, TILES - 1)

            @block.gpsimd
            def _(pool):
                joined.open(pool)
                with pool.Fori(0, TILES // 2) as j:
                    for k in (0, 1):
                        t = j * 2 + k
                        xt = S.x[:, cols(t * P, P)]
                        y_added.wait(pool, t)
                        nc.gpsimd.tensor_tensor(xt, xt, other[:, k, :], ALU.add).then_inc(joined.sem, 1)


PARTS = 3
STACK = PARTS * PARTS * HD
SHIFT = 2
HEADS = BATCH * H


def project_qkv(nc, S, wq, bq, scale, wk, bk, wv, bv, vd, keep_v=False):
    ctx, sb, sem, steps = scope(nc)
    ps = S.ps
    VC = H * vd
    VB = max(1, VC // GROUP)
    wide = VC > GROUP
    KTS = SEQ // P
    T, QK, V = 0, (1, 2), 3
    with ctx:
        xn = sb("xn", [P, 2, GROUP])
        xT = sb("xT", [P, 2, GROUP])
        z = sb("z", [P, 2, 2, GROUP])
        parts = sb("parts", [P, 2, 2, PARTS, GROUP], BF16)
        v_out = [None, None] if keep_v else [sb(f"v_out{n}", [P, VC * KTS]) for n in (0, 1)]
        normed, transposed, xT_ready, qk_mm, z_ready, hi_ready, mid_ready, v_mm, v_ready = [
            steps(n) for n in "normed transposed xT_ready qk_mm z_ready hi_ready mid_ready v_mm v_ready".split()]
        rest_ready = [steps(f"rest_ready{n}") for n in (0, 1)]
        lo_ready = [steps(f"lo_ready{n}") for n in (0, 1)]
        parts_out = [sem("parts_out0"), sem("parts_out1")]
        v_stored = [sem("v_stored0"), sem("v_stored1")]
        v_view = [v and v[:].rearrange("p (c t) -> p t c", t=KTS) for v in v_out]
        VSTEPS = GT * VB if wide else 1

        def subtract(eng, ns, g, s):
            for n in ns:
                hi_ready.wait(eng, g * 2 + n)
                eng.tensor_tensor(z[:, s, n, :], z[:, s, n, :], parts[:, s, n, 0, :],
                                  ALU.subtract).then_inc(rest_ready[n].sem, 1)
            for n in ns:
                mid_ready.wait(eng, g * 2 + n)
                eng.tensor_tensor(parts[:, s, n, 2, :], z[:, s, n, :], parts[:, s, n, 1, :],
                                  ALU.subtract).then_inc(lo_ready[n].sem, 1)

        def batches(eng, group):
            for b in range(BATCH):
                for s in (0, 1):
                    last = (b, s) == (BATCH - 1, 1)
                    group(b, s, None if last else (b + (s + 1) // 2, 1 - s), b == 0)

        with nc.Block() as block:
            @block.tensor
            def _(pe):
                for s in (transposed, qk_mm, v_mm):
                    s.open(pe)

                def transpose(b, s):
                    g = b * 2 + s
                    normed.wait(pe, g)
                    xT_ready.wait(pe, g - 1)
                    for k in range(GT):
                        op = nc.tensor.transpose(ps[:, T, k * P:(k + 1) * P], xn[:, s, k * P:(k + 1) * P], S.ident[:])
                    op.then_inc(transposed.sem, 1)

                def group(b, s, after, first):
                    g = b * 2 + s
                    xT_ready.wait(pe, g)
                    for n, w in enumerate((wq, wk)):
                        z_ready.wait(pe, g * 2 + n - 2)
                        nc.tensor.matmul(ps[:, QK[n], :], w[:], xT[:, s, :], start=True, stop=True).then_inc(qk_mm.sem, 1)
                    if wide:
                        for k in range(GT):
                            if k == 1 and after:
                                transpose(*after)
                            for w in range(VB):
                                n = k * VB + w
                                v_ready.wait(pe, g * VSTEPS + n - 4)
                                nc.tensor.matmul(ps[:, V + n % 4, :], xT[:, s, k * P:(k + 1) * P],
                                                 wv[:, w * GROUP:(w + 1) * GROUP], start=True,
                                                 stop=True).then_inc(v_mm.sem, 1)
                    else:
                        if after:
                            transpose(*after)
                        v_ready.wait(pe, g - 1)
                        for k in range(GT):
                            op = nc.tensor.matmul(ps[:, V, k * VC:(k + 1) * VC], xT[:, s, k * P:(k + 1) * P], wv[:],
                                                  start=True, stop=True)
                        op.then_inc(v_mm.sem, 1)

                transpose(0, 0)
                batches(pe, group)

            @block.scalar
            def _(act):
                for s in (xT_ready, hi_ready, mid_ready):
                    s.open(act)

                def evacuate(b, s):
                    g = b * 2 + s
                    transposed.wait(act, g)
                    v_mm.wait(act, (g - 1) * VSTEPS - 1)
                    nc.scalar.activation(xT[:, s, :], ps[:, T, :], ACT.Copy).then_inc(xT_ready.sem, 1)

                def group(b, s, after, first):
                    g = b * 2 + s
                    for n in (0, 1):
                        z_ready.wait(act, g * 2 + n)
                        nc.scalar.activation(parts[:, s, n, 0, :], z[:, s, n, :], ACT.Copy).then_inc(hi_ready.sem, 1)
                    if after and not wide:
                        evacuate(*after)
                    for n in (0, 1):
                        rest_ready[n].wait(act, g)
                        nc.scalar.activation(parts[:, s, n, 1, :], z[:, s, n, :], ACT.Copy).then_inc(mid_ready.sem, 1)
                    if after and wide:
                        evacuate(*after)

                evacuate(0, 0)
                batches(act, group)

            @block.gpsimd
            def _(pool):
                for n in (0, 1) if wide else (0,):
                    rest_ready[n].open(pool)
                    lo_ready[n].open(pool)
                with pool.Fori(0, BATCH) as b:
                    for s in (0, 1):
                        subtract(pool, (0, 1) if wide else (0,), b * 2 + s, s)

            @block.vector
            def _(dve):
                for s in (normed, z_ready, v_ready):
                    s.open(dve)
                if not wide:
                    rest_ready[1].open(dve)
                    lo_ready[1].open(dve)

                def normalize(b, s):
                    g = b * 2 + s
                    transposed.wait(dve, g - 2)
                    for k in range(GT):
                        op = normalize_tile(nc, S, xn[:, s, k * P:(k + 1) * P], g * GT + k)
                    op.then_inc(normed.sem, 1)

                def group(b, s, after, first):
                    g = b * 2 + s
                    if not first:
                        dve.wait_ge(parts_out[s], b * 32)
                    for n in (0, 1):
                        qk_mm.wait(dve, g * 2 + n)
                        if n == 0:
                            nc.vector.tensor_scalar(z[:, s, n, :], ps[:, QK[n], :], bq[:], scale, ALU.add,
                                                    ALU.mult).then_inc(z_ready.sem, 1)
                        else:
                            nc.vector.tensor_scalar(z[:, s, n, :], ps[:, QK[n], :], bk[:], None,
                                                    ALU.add).then_inc(z_ready.sem, 1)
                    if after:
                        normalize(*after)
                    if s == 0 and b >= 2 and not keep_v:
                        dve.wait_ge(v_stored[b % 2], b // 2 * 16)
                    if keep_v:
                        v_mm.wait(dve, g)
                        nc.vector.tensor_tensor(S.v_tok[:, cols(g * GROUP, GROUP)], ps[:, V, :], bv[:],
                                                ALU.add).then_inc(v_ready.sem, 1)
                    elif not wide:
                        v_mm.wait(dve, g)
                        nc.vector.tensor_tensor(v_view[b % 2][:, s * GT:(s + 1) * GT, :],
                                                ps[:, V, :].rearrange("p (t c) -> p t c", t=GT),
                                                bv[:].rearrange("p (t c) -> p t c", t=GT), ALU.add).then_inc(v_ready.sem, 1)
                    else:
                        for k in range(GT):
                            for w in range(VB):
                                n = k * VB + w
                                v_mm.wait(dve, g * VSTEPS + n)
                                nc.vector.tensor_tensor(v_view[b % 2][:, s * GT + k, w * GROUP:(w + 1) * GROUP],
                                                        ps[:, V + n % 4, :], bv[:, w * GROUP:(w + 1) * GROUP],
                                                        ALU.add).then_inc(v_ready.sem, 1)
                    if not wide:
                        subtract(dve, (1,), g, s)

                normalize(0, 0)
                batches(dve, group)

            @block.sync
            def _(sp):
                for b in range(BATCH):
                    for s in (0, 1):
                        for n, dst in enumerate((S.q_parts, S.k_parts)):
                            lo_ready[n].wait(sp, b * 2 + s)
                            sp.dma_start(dst[bass.ds(b, 1), :, :, :, s * GROUP:(s + 1) * GROUP]
                                         .rearrange("b a h d t -> (b h d) a t"), parts[:, s, n]).then_inc(parts_out[s], 16)
                    if not keep_v:
                        v_ready.wait(sp, b * 2 * VSTEPS + 2 * VSTEPS - 1)
                        sp.dma_start(S.v_heads[bass.ds(b * H, H), :, 0:vd * KTS].rearrange("h p c -> p h c"),
                                     v_out[b % 2][:].rearrange("p (h c) -> p h c", h=H)).then_inc(v_stored[b % 2], 16)
                for q in parts_out:
                    sp.wait_ge(q, 32 * BATCH)
                if not keep_v:
                    for q in v_stored:
                        sp.wait_ge(q, 16 * BATCH // 2)


class Head:

    def __init__(self, turn, c):
        self.turn, self.c = turn, c

    def __sub__(self, n):
        return Head(self.turn, self.c - n)

    def times(self, k, plus=0):
        return self.turn * (4 * k) + (self.c * k + plus)

    def rounds(self, ring):
        return self.turn * (4 // ring) + self.c // ring

    def slot(self, ring):
        return self.c % ring


def load_stacks(sp, S, i, q_stack, k_stack, loaded):
    b, h = i.times(1) // H, i.times(1) % H
    for r in range(PARTS):
        rows = slice(r * PARTS * HD, (r + 1) * PARTS * HD)
        q = S.q_parts[bass.ds(b, 1), r, bass.ds(h, 1), :, :].rearrange("b h d t -> (b h) d t")
        sp.dma_start(q_stack[rows, :], q.broadcast_to([PARTS, HD, SEQ])).then_inc(loaded, 16)
        k = S.k_parts[bass.ds(b, 1), :, bass.ds(h, 1), :, :].rearrange("b a h d t -> (b a) (h d) t")
        sp.dma_start(k_stack[rows, :], k).then_inc(loaded, 16)


def attend(nc, S, causal, vd):
    ctx, sb, sem, steps = scope(nc)
    ps = S.ps
    KTS = SEQ // P
    VW = vd + 1 if causal else 32
    CH = SEQ // GROUP
    S1, S2, OB = 0, 4, 6
    MP = 96 if causal else 0
    if causal:
        tiles = [(kt, c) for kt in range(KTS) for c in range(CH) if kt * P < (c + 1) * GROUP]
        groups = [tiles[n:n + 3] for n in range(0, 12, 3)]
        order = [0, 7, 1, 6, 2, 5, 3, 4]
    else:
        tiles = [(kt, c) for kt in range(KTS) for c in range(CH)]
        groups = [tiles[n:n + 4] for n in range(0, 16, 4)]
        order = list(range(KTS))
    NT = len(tiles)
    RING = 6 if causal else 8
    LOADS = 16 * (2 * PARTS + 1)
    OROWS = VW if causal else P

    with ctx:
        qs = [sb(f"q_stack{n}", [P, SEQ], BF16) for n in range(4)]
        ks = [sb(f"k_stack{n}", [P, SEQ], BF16) for n in range(4)]
        vs = [sb(f"v{n}", [P, VW, KTS]) for n in range(4)]
        prob = sb("prob", [P, RING, GROUP])
        neg_max = sb("neg_max", [P, 2, KTS])
        shift = sb("shift", [P, 2, SHIFT * KTS], BF16)
        shift_rows = sb("shift_rows", [P, 2, P], BF16)
        o_out = sb("o_out", [P, 2, SEQ if causal else GROUP])
        (s1_mm, maxed, split, m_mm, m_read, s2_mm, exped, pv_mm, o_read) = [steps(n) for n in (
            "s1_mm maxed split m_mm m_read s2_mm exped pv_mm o_read").split()]
        loaded = [sem(f"loaded{n}") for n in range(4)]
        shifted = [sem(f"shifted{n}") for n in range(2)]
        stored = [sem(f"stored{n}") for n in range(2)]
        cleared, chain = sem("cleared"), sem("chain")

        def max_bank(h):
            return OB if causal else OB + h.slot(2)

        def offset(kt, c):
            return max(kt * P - c * GROUP, 0) if causal else 0

        def run(eng, step):
            last = HEADS + 2
            for c in range(4):
                step(Head(0, c), c)
            with eng.Fori(1, HEADS // 4 - 1) as turn:
                for c in range(4):
                    step(Head(turn, c), None)
            for c in range(HEADS - 4, last + 1):
                step(Head(0, c), c)

        def there(n, h):
            return n is None or 0 <= n - h < HEADS

        with nc.Block() as block:
            @block.tensor
            def _(pe):
                for s in (s1_mm, m_mm, s2_mm, pv_mm):
                    s.open(pe)

                def first_pass(i, m):
                    qt = order[m]
                    bank = S1 + 2 * (m % 2)
                    maxed.wait(pe, i.times(KTS, m - 2))
                    q, k = qs[i.slot(4)], ks[i.slot(4)]
                    for c in range(CH):
                        n = min(GROUP, (qt + 1) * P - c * GROUP) if causal else GROUP
                        if n > 0:
                            op = nc.tensor.matmul(ps[:, bank + c, 0:n], q[0:STACK, qt * P:(qt + 1) * P],
                                                  k[0:STACK, c * GROUP:c * GROUP + n], start=True,
                                                  stop=not causal or qt * P >= (c + 1) * GROUP)
                    if causal:
                        c, at = divmod(qt * P, GROUP)
                        op = nc.tensor.matmul(ps[:, bank + c, at:at + P], S.ident_b[:], S.mask_qk[:],
                                              start=False, stop=True)
                    op.then_inc(s1_mm.sem, 1)

                def second_scores(j, n, kt, c):
                    exped.wait(pe, j.times(NT, n - 2))
                    o = offset(kt, c)
                    diagonal = causal and kt * P >= c * GROUP
                    out = ps[:, S2 + n % 2, o:GROUP]
                    op = nc.tensor.matmul(out, ks[j.slot(4)][:, kt * P:(kt + 1) * P],
                                          qs[j.slot(4)][:, c * GROUP + o:(c + 1) * GROUP], start=True, stop=not diagonal)
                    if diagonal:
                        op = nc.tensor.matmul(ps[:, S2 + n % 2, o:o + P], S.ident_b[:], S.mask_kq[:],
                                              start=False, stop=True)
                    op.then_inc(s2_mm.sem, 1)

                def weigh(j, g):
                    if g == 0:
                        o_read.wait(pe, j.times(1, -1 if causal else -2))
                    at = sum(len(x) for x in groups[:g])
                    exped.wait(pe, j.times(NT, at + len(groups[g]) - 1))
                    for n, (kt, c) in enumerate(groups[g], at):
                        o = offset(kt, c)
                        if causal:
                            out = ps[0:VW, OB + c, o:GROUP]
                            start, stop = kt == 0, kt == (c + 1) * GROUP // P - 1
                        else:
                            quad = (c * 2 + kt % 2) * 32
                            out = ps[quad:quad + VW, OB + j.slot(2), :]
                            start, stop = kt < 2, kt >= KTS - 2
                        nc.tensor.matmul(out, vs[j.slot(4)][:, :, kt], prob[:, n % RING, o:GROUP], start=start,
                                         stop=stop).then_inc(pv_mm.sem, 1)

                def step(i, n):
                    one, two = there(n, 0), there(n, 2)
                    if one:
                        pe.wait_ge(loaded[i.slot(4)], (i.rounds(4) + 1) * LOADS)
                    if two:
                        pe.wait_ge(shifted[i.slot(2)], ((i - 2).rounds(2) + 1) * 16)
                    j = i - 2
                    for g in range(4):
                        at = sum(len(x) for x in groups[:g])
                        mine = list(enumerate(groups[g], at))
                        half = len(mine) // 2
                        if causal and g == 0 and there(n, 3):
                            weigh(i - 3, 3)
                        if two:
                            for m, (kt, c) in mine[:half]:
                                second_scores(j, m, kt, c)
                        if g > 0 and two:
                            weigh(j, g - 1)
                        if not causal and g == 0 and there(n, 3):
                            weigh(i - 3, 3)
                        early = causal and g == 0
                        if one and early:
                            first_pass(i, 2 * g)
                        if two:
                            for m, (kt, c) in mine[half:]:
                                second_scores(j, m, kt, c)
                        if one and not early:
                            first_pass(i, 2 * g)
                        if one:
                            first_pass(i, 2 * g + 1)
                        if g == 1 and there(n, 1):
                            h = i - 1
                            split.wait(pe, h.times(1))
                            m_read.wait(pe, h.times(1, -1))
                            if not causal:
                                o_read.wait(pe, h.times(1, -2))
                            nc.tensor.transpose(ps[MP:MP + SHIFT * KTS, max_bank(h), 0:P // 2].bitcast(BF16),
                                                shift[:, h.slot(2), :], S.ident_b[:]).then_inc(m_mm.sem, 1)

                run(pe, step)

            @block.scalar
            def _(act):
                for s in (exped, m_read):
                    s.open(act)
                if not causal:
                    o_read.open(act)

                def read_output(h, n):
                    pv_mm.wait(act, h.times(NT, NT - 1))
                    if n is None or n - 3 >= 2:
                        act.wait_ge(stored[h.slot(2)], h.rounds(2) * 16)
                    nc.scalar.activation(o_out[:, h.slot(2), :], ps[:, OB + h.slot(2), :],
                                         ACT.Copy).then_inc(o_read.sem, 1)

                def step(i, n):
                    j = i - 2
                    for g in range(4):
                        at = sum(len(x) for x in groups[:g])
                        for m, (kt, c) in enumerate(groups[g], at):
                            if there(n, 2):
                                s2_mm.wait(act, j.times(NT, m))
                                pv_mm.wait(act, j.times(NT, m - RING))
                                o = offset(kt, c)
                                nc.scalar.activation(prob[:, m % RING, o:GROUP], ps[:, S2 + m % 2, o:GROUP],
                                                     ACT.Exp).then_inc(exped.sem, 1)
                        if g == 0 and not causal and there(n, 3):
                            read_output(i - 3, n)
                        if g == 1 and there(n, 1):
                            h = i - 1
                            m_mm.wait(act, h.times(1))
                            if n is None or n - 3 >= 0:
                                act.wait_ge(shifted[h.slot(2)], h.rounds(2) * 16)
                            nc.scalar.activation(shift_rows[MP:MP + SHIFT * KTS, h.slot(2), :],
                                                 ps[MP:MP + SHIFT * KTS, max_bank(h), 0:P // 2].bitcast(BF16),
                                                 ACT.Copy).then_inc(m_read.sem, 1)

                nc.scalar.activation(S.act_warm[:], S.eps[:], ACT.Exp)
                run(act, step)

            @block.vector
            def _(dve):
                maxed.open(dve)
                if causal:
                    o_read.open(dve)
                for n in range(4):
                    nc.vector.memset(qs[n][:], 0.0)
                    nc.vector.memset(ks[n][:], 1.0)
                    if VW > vd + 1:
                        nc.vector.memset(vs[n][:, vd + 1:VW, :], 0.0)
                    nc.vector.memset(vs[n][:, vd:vd + 1, :], 1.0).then_inc(cleared, 1)

                def step(i, n):
                    if causal and there(n, 3):
                        h = i - 3
                        pv_mm.wait(dve, h.times(NT, NT - 1))
                        if n is None or n - 3 >= 2:
                            dve.wait_ge(stored[h.slot(2)], h.rounds(2) * 16)
                        nc.vector.tensor_copy(o_out[0:OROWS, h.slot(2), :].rearrange("p (c n) -> p c n", c=CH),
                                              ps[0:OROWS, OB:OB + 2, :]).then_inc(o_read.sem, 1)
                    for m, qt in enumerate(order):
                        if there(n, 0):
                            if m == 0:
                                split.wait(dve, i.times(1, -2))
                            s1_mm.wait(dve, i.times(KTS, m))
                            bank = S1 + 2 * (m % 2)
                            keys = (qt + 1) * P if causal else SEQ
                            nc.vector.tensor_reduce(neg_max[:, i.slot(2), qt:qt + 1],
                                                    ps[:, bank:bank + 2, :].rearrange("p b n -> p (b n)")[:, 0:keys],
                                                    AX.X, ALU.max, negate=True).then_inc(maxed.sem, 1)

                run(dve, step)

            @block.gpsimd
            def _(pool):
                split.open(pool)

                def heads(i):
                    maxed.wait(pool, i.times(KTS, KTS - 1))
                    m_mm.wait(pool, i.times(1, -2))
                    hi = shift[:, i.slot(2), 0:KTS]
                    nc.gpsimd.tensor_tensor(hi, neg_max[:, i.slot(2), :], S.zeros[:, 0:KTS],
                                            ALU.add).then_inc(chain, 1)
                    pool.wait_ge(chain, i.times(1, 1))
                    nc.gpsimd.tensor_tensor(shift[:, i.slot(2), KTS:2 * KTS], neg_max[:, i.slot(2), :], hi,
                                            ALU.subtract).then_inc(split.sem, 1)

                with pool.Fori(0, HEADS // 4) as turn:
                    for c in range(4):
                        heads(Head(turn, c))

            @block.sync
            def _(sp):
                def load(i, n):
                    if n is not None and n < 4:
                        sp.wait_ge(cleared, n + 1)
                    if n is None or n >= 4:
                        pv_mm.wait(sp, i.times(NT, -3 * NT - 1))
                    at, slot = i.times(1), i.slot(4)
                    load_stacks(sp, S, i, qs[slot], ks[slot], loaded[slot])
                    sp.dma_start(vs[slot][:, 0:vd, :],
                                 S.v_heads[bass.ds(at, 1), :, 0:vd * KTS].rearrange("a p (d t) -> (a p) d t", t=KTS)
                                 ).then_inc(loaded[slot], 16)

                def step(i, n):
                    if n is None or n + 1 < HEADS:
                        load(i - (-1), None if n is None else n + 1)
                    if there(n, 3):
                        h = i - 3
                        o_read.wait(sp, h.times(1))
                        at = h.times(1)
                        if causal:
                            sp.dma_start(S.o_wide[bass.ds(at, 1), :, :].rearrange("a r n -> (a r) n"),
                                         o_out[0:OROWS, h.slot(2), :]).then_inc(stored[h.slot(2)], 16)
                        else:
                            sp.dma_start(S.o_quads[bass.ds(at, 1), :, :].rearrange("a r n -> (a r) n"),
                                         o_out[:, h.slot(2), :]).then_inc(stored[h.slot(2)], 16)
                    if there(n, 1):
                        h = i - 1
                        m_read.wait(sp, h.times(1))
                        sp.dma_start(qs[h.slot(4)][STACK:STACK + SHIFT, :].rearrange("r (q t) -> r q t", t=P),
                                     shift_rows[MP:MP + SHIFT * KTS, h.slot(2), :]).then_inc(shifted[h.slot(2)], 16)

                load(Head(0, 0), 0)
                run(sp, step)
                for s in stored:
                    sp.wait_ge(s, 16 * HEADS // 2)


def reciprocal_sums(nc, S, rows, out, split=False):
    ctx, sb, sem, steps = scope(nc)
    with ctx:
        part = sb("sums", [P, len(rows), GROUP])
        thirds = sb("thirds", [P, PARTS, GROUP], BF16)
        loaded, chain, stored = sem("loaded"), sem("chain"), sem("stored")
        links = (len(rows) == 2) + 1 + (2 * PARTS - 1 if split else 0)
        with nc.Block() as block:
            @block.sync
            def _(sp):
                n = 0
                for k, some in enumerate(rows):
                    for at, src in some:
                        sp.dma_start(part[at, k, :], src).then_inc(loaded, 16)
                        n += 1
                sp.wait_ge(chain, links)
                sp.dma_start(out, thirds[:] if split else part[:, 0, :]).then_inc(stored, 16)
                sp.wait_ge(stored, 16)

            @block.vector
            def _(dve):
                dve.wait_ge(loaded, 16 * sum(len(x) for x in rows))
                c = Chain(dve, chain)
                if len(rows) == 2:
                    c.run(nc.vector.tensor_tensor(part[:, 0, :], part[:, 0, :], part[:, 1, :], ALU.add))
                c.run(nc.vector.reciprocal(part[:, 0, :], part[:, 0, :]))
                if split:
                    for n in range(PARTS):
                        c.run(nc.vector.tensor_copy(thirds[:, n, :], part[:, 0, :]))
                        if n < PARTS - 1:
                            c.run(nc.vector.tensor_tensor(part[:, 0, :], part[:, 0, :], thirds[:, n, :], ALU.subtract))


def attention_output(nc, S, wo, bo):
    quads = S.o_quads[:, :, :].rearrange("a (c q r) n -> a c q r n", c=2, q=2)
    reciprocal_sums(nc, S, [[(slice(0, P), quads[:, :, q, HD, :].rearrange("a c n -> (a c) n"))] for q in (0, 1)],
                    S.r_sums[:, :, :].rearrange("a c n -> (a c) n"))
    ctx, sb, sem, steps = scope(nc)
    ps = S.ps
    with ctx:
        num = sb("num", [P, 2, 2, GROUP])
        r = sb("r", [P, 2, GROUP])
        oT = sb("oT", [P, 2, GROUP])
        loaded = [sem("loaded0"), sem("loaded1")]
        added, x_biased, o_ready, y_mm, x_ready = [steps(n) for n in "added x_biased o_ready y_mm x_ready".split()]
        with nc.Block() as block:
            @block.sync
            def _(sp):
                with sp.Fori(0, BATCH) as b:
                    for c in (0, 1):
                        o_ready.wait(sp, b * 2 + c - 2)
                        for q in (0, 1):
                            src = quads[bass.ds(b * H, H), c, q, 0:HD, :]
                            sp.dma_start(num[:, c, q, :], src.rearrange("h r n -> h r n")).then_inc(loaded[c], 16)
                        sp.dma_start(r[:, c, :],
                                     S.r_sums[bass.ds(b * H, H), c:c + 1, :].broadcast_to([H, HD, GROUP])
                                     ).then_inc(loaded[c], 16)

            @block.gpsimd
            def _(pool):
                added.open(pool)
                x_biased.open(pool)
                with pool.Fori(0, BATCH) as b:
                    for c in (0, 1):
                        x = S.x[:, cols((b * 2 + c) * GROUP, GROUP)]
                        nc.gpsimd.tensor_tensor(x, x, bo[:], ALU.add).then_inc(x_biased.sem, 1)
                        pool.wait_ge(loaded[c], b * 48 + 48)
                        nc.gpsimd.tensor_tensor(num[:, c, 0, :], num[:, c, 0, :], num[:, c, 1, :],
                                                ALU.add).then_inc(added.sem, 1)

            @block.vector
            def _(dve):
                o_ready.open(dve)
                x_ready.open(dve)
                with dve.Fori(0, BATCH) as b:
                    for c in (0, 1):
                        g = b * 2 + c
                        added.wait(dve, g)
                        dve.wait_ge(loaded[c], b * 48 + 48)
                        y_mm.wait(dve, g - 2)
                        nc.vector.tensor_tensor(oT[:, c, :], num[:, c, 0, :], r[:, c, :], ALU.mult).then_inc(o_ready.sem, 1)
                    for c in (0, 1):
                        g = b * 2 + c
                        y_mm.wait(dve, g)
                        x_biased.wait(dve, g)
                        x = S.x[:, cols(g * GROUP, GROUP)]
                        nc.vector.tensor_tensor(x, x, ps[:, c, :], ALU.add).then_inc(x_ready.sem, 1)
                        x_ready.wait(dve, g)
                        group_stats(nc, S, g)

            @block.tensor
            def _(pe):
                y_mm.open(pe)
                with pe.Fori(0, BATCH) as b:
                    for c in (0, 1):
                        g = b * 2 + c
                        o_ready.wait(pe, g)
                        x_ready.wait(pe, g - 2)
                        for k in range(GT):
                            op = nc.tensor.matmul(ps[:, c, k * P:(k + 1) * P], oT[:, c, k * P:(k + 1) * P], wo[:],
                                                  start=True, stop=True)
                        op.then_inc(y_mm.sem, 1)


def wide_attention_output(nc, S, wo, bo):
    VD = LATENT
    FC = H * VD // P
    reciprocal_sums(nc, S, [[(slice(c * HEADS, (c + 1) * HEADS), S.o_wide[:, VD, c * GROUP:(c + 1) * GROUP])
                             for c in (0, 1)]], S.r_wide[:, :, :, :].rearrange("c a r n -> (c a) r n"), split=True)
    ctx, sb, sem, steps = scope(nc)
    ps = S.ps
    Y = 6
    RB = 6
    with ctx:
        num = sb("num", [P, 2, FC, GROUP])
        r = sb("r", [P, 2, GROUP], BF16)
        oT = sb("oT", [P, 2, FC, GROUP])
        pick = sb("pick", [P, FC * P], BF16)
        made = sem("made")
        loaded = [sem("loaded0"), sem("loaded1")]
        r_mm, o_ready, x_biased, y_mm, x_ready = [steps(n) for n in "r_mm o_ready x_biased y_mm x_ready".split()]
        LOADS = 16 * (2 + PARTS)
        with nc.Block() as block:
            @block.sync
            def _(sp):
                sp.wait_ge(made, 1)
                with sp.Fori(0, BATCH) as b:
                    for c in (0, 1):
                        o_ready.wait(sp, (b * 2 + c) * FC - FC - 1)
                        for n in range(PARTS):
                            sp.dma_start(r[n * H:(n + 1) * H, c, :], S.r_wide[c, bass.ds(b * H, H), n, :]
                                         ).then_inc(loaded[c], 16)
                        for h in (0, 1):
                            src = S.o_wide[bass.ds(b * H, H), 0:VD, c * GROUP:(c + 1) * GROUP]
                            src = src.rearrange("(f h) l n -> h l f n", h=2)[h]
                            sp.dma_start(num[h * VD:(h + 1) * VD, c, :, :], src).then_inc(loaded[c], 16)

            @block.gpsimd
            def _(pool):
                x_biased.open(pool)
                nc.gpsimd.memset(r[:], 0.0).then_inc(made, 1)
                v = pick[:].rearrange("p (f h l) -> p f h l", f=FC, h=2)
                nc.gpsimd.memset(pick[:], 0.0).then_inc(made, 1)
                for n in range(PARTS):
                    pool.wait_ge(made, 2 + n)
                    nc.gpsimd.affine_select(out=v, in_=v, compare_op=ALU.not_equal, fill=1.0, base=-n * H,
                                            pattern=[[-2, FC], [-1, 2], [0, VD]], channel_multiplier=1
                                            ).then_inc(made, 1)
                with pool.Fori(0, GROUPS) as g:
                    x = S.x[:, cols(g * GROUP, GROUP)]
                    nc.gpsimd.tensor_tensor(x, x, bo[:], ALU.add).then_inc(x_biased.sem, 1)

            @block.vector
            def _(dve):
                o_ready.open(dve)
                x_ready.open(dve)

                def scale(g, c, half):
                    for f in range(half * FC // 2, (half + 1) * FC // 2):
                        r_mm.wait(dve, g * FC + f)
                        dve.wait_ge(loaded[c], g // 2 * LOADS + LOADS)
                        nc.vector.tensor_tensor(oT[:, c, f, :], num[:, c, f, :], ps[:, (g * FC + f) % RB, :],
                                                ALU.mult).then_inc(o_ready.sem, 1)

                for g in range(GROUPS + 1):
                    if g < GROUPS:
                        y_mm.wait(dve, g - 2)
                        scale(g, g % 2, 0)
                        scale(g, g % 2, 1)
                    if g > 0:
                        y_mm.wait(dve, g - 1)
                        x_biased.wait(dve, g - 1)
                        x = S.x[:, (g - 1) * GROUP:g * GROUP]
                        nc.vector.tensor_tensor(x, x, ps[:, Y + (g - 1) % 2, :], ALU.add).then_inc(x_ready.sem, 1)
                        x_ready.wait(dve, g - 1)
                        group_stats(nc, S, g - 1)

            @block.tensor
            def _(pe):
                r_mm.open(pe)
                y_mm.open(pe)
                pe.wait_ge(made, 2 + PARTS)

                def factors(g, half):
                    c = g % 2
                    if half == 0:
                        pe.wait_ge(loaded[c], g // 2 * LOADS + LOADS)
                    for f in range(half * FC // 2, (half + 1) * FC // 2):
                        o_ready.wait(pe, g * FC + f - RB)
                        nc.tensor.matmul(ps[:, (g * FC + f) % RB, :], pick[:, f * P:(f + 1) * P], r[:, c, :],
                                         start=True, stop=True).then_inc(r_mm.sem, 1)

                def products(g, half):
                    c = g % 2
                    if half == 0:
                        o_ready.wait(pe, g * FC + FC - 1)
                        x_ready.wait(pe, g - 2)
                    for k in range(half * GT // 2, (half + 1) * GT // 2):
                        for f in range(FC):
                            op = nc.tensor.matmul(ps[:, Y + c, k * P:(k + 1) * P], oT[:, c, f, k * P:(k + 1) * P],
                                                  wo[:, f, :], start=(f == 0), stop=(f == FC - 1))
                    if half == 1:
                        op.then_inc(y_mm.sem, 1)

                for g in range(GROUPS + 1):
                    for half in (0, 1):
                        if g < GROUPS:
                            factors(g, half)
                        if g > 0:
                            products(g - 1, half)


LATENT = 64


def full_attention(nc, S):
    project_qkv(nc, S, S.b0_wq, S.b0_bq, HD ** -0.5, S.b0_wk, S.b0_bk, S.b0_wv, S.b0_bv, HD)
    attend(nc, S, False, HD)
    attention_output(nc, S, S.b0_wo, S.b0_bo)


def fold_latent_key(nc, S):
    ctx, sb, sem, steps = scope(nc)
    ps = S.ps
    L = LATENT
    with ctx:
        outer = sb("outer", [L, H * HD])
        ones = sb("ones", [L, 1])
        wkl = sb("wkl", [L, H * D])
        loaded, made, folded = sem("loaded"), sem("made"), sem("folded")
        with nc.Block() as block:
            @block.sync
            def _(sp):
                sp.dma_start(wkl[:], S.a1_wkl).then_inc(loaded, 16)

            @block.vector
            def _(dve):
                nc.vector.memset(ones[:], 1.0)
                nc.vector.tensor_tensor(outer[:].rearrange("p (h d) -> p h d", h=H),
                                        S.a1_bkl[:].rearrange("p (h o) -> p h o", o=1).broadcast_to([L, H, HD]),
                                        S.a1_wc[:].rearrange("p (o d) -> p o d", o=1).broadcast_to([L, H, HD]),
                                        ALU.mult).then_inc(made, 1)
                dve.wait_ge(folded, 1)
                nc.vector.tensor_copy(S.a1_wk2[:], ps[:, 0, 0:P])
                nc.vector.tensor_copy(S.a1_bk2[:], ps[:, 1, 0:1])

            @block.tensor
            def _(pe):
                pe.wait_ge(loaded, 16)
                for h in range(H):
                    nc.tensor.matmul(ps[:, 0, h * HD:(h + 1) * HD], wkl[:, h * P:(h + 1) * P], S.a1_wc[:],
                                     start=True, stop=True)
                pe.wait_ge(made, 1)
                nc.tensor.matmul(ps[:, 1, 0:1], outer[:], ones[:], start=True, stop=True).then_inc(folded, 1)


def causal_attention(nc, S):
    fold_latent_key(nc, S)
    project_qkv(nc, S, S.a1_wq, S.a1_bq, LATENT ** -0.5, S.a1_wk2, S.a1_bk2, S.a1_wv, S.a1_bv, LATENT)
    attend(nc, S, True, LATENT)
    wide_attention_output(nc, S, S.a1_wo, S.a1_bo)


def row_attention(nc, S):
    ctx, sb, sem, steps = scope(nc)
    with ctx:
        S.v_tok = sb("v_tok", [P, TOK])
        S.weight = sb("weight", [P, TILES * H])
        project_qkv(nc, S, S.b1_wq, S.b1_bq, HD ** -0.5, S.b1_wk, S.b1_bk, S.b1_wv, S.b1_bv, HD, keep_v=True)
        attention_row_sums(nc, S)
        weighted_values_output(nc, S, S.b1_wo, S.b1_bo)


def attention_row_sums(nc, S):
    ctx, sb, sem, steps = scope(nc)
    ps = S.ps
    KTS = SEQ // P
    LOADS = 16 * 2 * PARTS
    with ctx:
        qs = [sb(f"q_stack{n}", [P, SEQ], BF16) for n in range(4)]
        ks = [sb(f"k_stack{n}", [P, SEQ], BF16) for n in range(4)]
        neg_max = sb("neg_max", [P, 2, KTS])
        sums = sb("sums", [P, HEADS * KTS])
        inverse = sb("inverse", [P, HEADS * KTS])
        s_mm, maxed, summed = [steps(n) for n in "s_mm maxed summed".split()]
        chain = sem("chain")
        loaded = [sem(f"loaded{n}") for n in range(4)]
        cleared = sem("cleared")

        def heads(eng, step):
            with eng.Fori(0, HEADS // 4) as turn:
                for c in range(4):
                    step(Head(turn, c))

        with nc.Block() as block:
            @block.tensor
            def _(pe):
                s_mm.open(pe)

                def step(i):
                    pe.wait_ge(loaded[i.slot(4)], (i.rounds(4) + 1) * LOADS)
                    for qt in range(KTS):
                        summed.wait(pe, i.times(KTS, qt - 4))
                        for c in (0, 1):
                            op = nc.tensor.matmul(ps[:, 2 * (qt % 4) + c, :], qs[i.slot(4)][:, qt * P:(qt + 1) * P],
                                                  ks[i.slot(4)][:, c * GROUP:(c + 1) * GROUP], start=True, stop=True)
                        op.then_inc(s_mm.sem, 1)

                heads(pe, step)

            @block.vector
            def _(dve):
                maxed.open(dve)
                for n in range(4):
                    nc.vector.memset(qs[n][:], 0.0)
                    nc.vector.memset(ks[n][:], 0.0).then_inc(cleared, 1)

                def step(i):
                    summed.wait(dve, i.times(KTS, -KTS - 1))
                    for qt in range(KTS):
                        s_mm.wait(dve, i.times(KTS, qt))
                        nc.vector.tensor_reduce(neg_max[:, i.slot(2), qt:qt + 1],
                                                ps[:, 2 * (qt % 4):2 * (qt % 4) + 2, :], AX.XY, ALU.max,
                                                negate=True).then_inc(maxed.sem, 1)

                heads(dve, step)
                summed.wait(dve, HEADS * KTS - 1)
                c = Chain(dve, chain)
                c.run(nc.vector.reciprocal(inverse[:], sums[:]))
                for b in range(BATCH):
                    mine = slice(b * H * KTS, (b + 1) * H * KTS)
                    nc.vector.tensor_tensor(S.weight[:, mine].rearrange("p (t h) -> p h t", h=H),
                                            sums[:, mine].rearrange("p (h t) -> p h t", h=H),
                                            inverse[:, mine].rearrange("p (h t) -> p h t", h=H), ALU.mult)

            @block.scalar
            def _(act):
                summed.open(act)
                nc.scalar.activation(S.act_warm[:], S.eps[:], ACT.Exp)

                def step(i):
                    for qt in range(KTS):
                        maxed.wait(act, i.times(KTS, qt))
                        s = ps[:, 2 * (qt % 4):2 * (qt % 4) + 2, :]
                        nc.scalar.activation(s, s, ACT.Exp, bias=neg_max[:, i.slot(2), qt:qt + 1],
                                             accum_out=sums[:, cols(i.times(KTS, qt), 1)]).then_inc(summed.sem, 1)

                heads(act, step)

            @block.sync
            def _(sp):

                def step(i):
                    s_mm.wait(sp, i.times(KTS, -3 * KTS - 1))
                    load_stacks(sp, S, i, qs[i.slot(4)], ks[i.slot(4)], loaded[i.slot(4)])

                for c in range(4):
                    sp.wait_ge(cleared, c + 1)
                    load_stacks(sp, S, Head(0, c), qs[c], ks[c], loaded[c])
                with sp.Fori(1, HEADS // 4) as turn:
                    for c in range(4):
                        step(Head(turn, c))


def weighted_values_output(nc, S, wo, bo):
    ctx, sb, sem, steps = scope(nc)
    ps = S.ps
    with ctx:
        y = sb("y", [P, 2, GROUP])
        yT = sb("yT", [P, 2, GROUP])
        y_ready, transposed, yT_ready, o_mm, x_biased, x_ready = [steps(n) for n in (
            "y_ready transposed yT_ready o_mm x_biased x_ready").split()]
        with nc.Block() as block:
            @block.tensor
            def _(pe):
                transposed.open(pe)
                o_mm.open(pe)
                with pe.Fori(0, BATCH) as b:
                    for s in (0, 1):
                        g = b * 2 + s
                        y_ready.wait(pe, g)
                        yT_ready.wait(pe, g - 2)
                        for k in range(GT):
                            op = nc.tensor.transpose(ps[:, s, k * P:(k + 1) * P], y[:, s, k * P:(k + 1) * P], S.ident[:])
                        op.then_inc(transposed.sem, 1)
                    for s in (0, 1):
                        g = b * 2 + s
                        yT_ready.wait(pe, g)
                        x_ready.wait(pe, g - 2)
                        for k in range(GT):
                            op = nc.tensor.matmul(ps[:, 2 + s, k * P:(k + 1) * P], yT[:, s, k * P:(k + 1) * P], wo[:],
                                                  start=True, stop=True)
                        op.then_inc(o_mm.sem, 1)

            @block.scalar
            def _(act):
                yT_ready.open(act)
                with act.Fori(0, BATCH) as b:
                    for s in (0, 1):
                        g = b * 2 + s
                        transposed.wait(act, g)
                        o_mm.wait(act, g - 2)
                        nc.scalar.activation(yT[:, s, :], ps[:, s, :], ACT.Copy).then_inc(yT_ready.sem, 1)

            @block.gpsimd
            def _(pool):
                x_biased.open(pool)
                with pool.Fori(0, GROUPS) as g:
                    x = S.x[:, cols(g * GROUP, GROUP)]
                    nc.gpsimd.tensor_tensor(x, x, bo[:], ALU.add).then_inc(x_biased.sem, 1)

            @block.vector
            def _(dve):
                y_ready.open(dve)
                x_ready.open(dve)
                with dve.Fori(0, BATCH) as b:
                    for s in (0, 1):
                        g = b * 2 + s
                        transposed.wait(dve, g - 2)
                        w = S.weight[:, cols(g * GT * H, GT * H)]
                        nc.vector.tensor_tensor(y[:, s, :].rearrange("p (h d) -> p h d", d=HD),
                                                S.v_tok[:, cols(g * GROUP, GROUP)].rearrange("p (h d) -> p h d", d=HD),
                                                bcast(w, HD), ALU.mult).then_inc(y_ready.sem, 1)
                    for s in (0, 1):
                        g = b * 2 + s
                        o_mm.wait(dve, g)
                        x_biased.wait(dve, g)
                        x = S.x[:, cols(g * GROUP, GROUP)]
                        nc.vector.tensor_tensor(x, x, ps[:, 2 + s, :], ALU.add).then_inc(x_ready.sem, 1)
                x_ready.wait(dve, GROUPS - 1)
                for g in range(GROUPS):
                    group_stats(nc, S, g)


def route_best(nc, S):
    ctx, sb, sem, steps = scope(nc)
    ps = S.ps
    T, L, C = (0, 1), 2, 3
    W = TILES * E
    with ctx:
        xn = sb("xn", [P, 2, GROUP])
        xT = sb("xT", [P, 2, GROUP])
        st = sb("bn", [P, TILES * 6])
        tmp = sb("bn_tmp", [P, 4, TILES])
        mx, total = sb("mx", [P, TILES]), sb("total", [P, TILES])
        logits, exped, gates, work = sb("logits", [P, W]), sb("exped", [P, W]), sb("gates", [P, W]), sb("work", [P, W])
        best, mask = sb("best", [P, W]), sb("mask", [P, W], BF16)
        totals, summed, cum = sb("totals", [P, W]), sb("summed", [P, W]), sb("cum", [P, W])
        rank = sb("rank", [P, TILES])
        filled = sb("filled", [P, E, TILES])
        tiles_of, base = sb("tiles_of", [P, E]), sb("base", [P, E])
        ones = sb("ones", [P, E])
        slot_f, expert_f = sb("slot_f", [P, TILES]), sb("expert_f", [P, SLOT_TILES])
        reached = sb("reached", [P, SLOT_TILES, E - 1])
        chain, bn, shifted, exp_done, masked, counted, var_ready, std_ready = [sem(n) for n in (
            "chain bn shifted exp_done masked counted var_ready std_ready").split()]
        normed, transposed, copied, xT_ready, l_mm = [steps(n) for n in (
            "normed transposed copied xT_ready l_mm").split()]
        with nc.Block() as block:
            @block.tensor
            def _(pe):
                transposed.open(pe)
                l_mm.open(pe)
                with pe.Fori(0, PAIRS) as b:
                    for s in (0, 1):
                        g = b * 2 + s
                        normed.wait(pe, g)
                        xT_ready.wait(pe, g - 2)
                        for k in range(GT):
                            op = nc.tensor.transpose(ps[:, T[s], k * P:(k + 1) * P], xn[:, s, k * P:(k + 1) * P],
                                                     S.ident[:])
                        op.then_inc(transposed.sem, 1)
                    for s in (0, 1):
                        g = b * 2 + s
                        xT_ready.wait(pe, g)
                        for k in range(GT):
                            op = nc.tensor.matmul(ps[:, L, cols((g * GT + k) * E, E)], xT[:, s, k * P:(k + 1) * P],
                                                  S.f1_wr[:], start=True, stop=True)
                        op.then_inc(l_mm.sem, 1)
                pe.wait_ge(masked, 1)
                count_matmuls(nc, S, ps[:, C, :], mask[:]).then_inc(counted, 1)

            @block.scalar
            def _(act):
                copied.open(act)
                xT_ready.open(act)
                with act.Fori(0, PAIRS) as b:
                    for s in (0, 1):
                        g = b * 2 + s
                        normed.wait(act, g)
                        nc.scalar.activation(S.normed[:, cols(g * GROUP, GROUP)], xn[:, s, :],
                                             ACT.Copy).then_inc(copied.sem, 1)
                        transposed.wait(act, g)
                        l_mm.wait(act, g - 2)
                        nc.scalar.activation(xT[:, s, :], ps[:, T[s], :], ACT.Copy).then_inc(xT_ready.sem, 1)
                act.wait_ge(var_ready, 1)
                nc.scalar.activation(tmp[:, 1], tmp[:, 2], ACT.Sqrt, bias=S.eps[:], scale=1.0 / D).then_inc(std_ready, 1)
                nc.scalar.activation(S.act_warm[:], S.eps[:], ACT.Exp)
                act.wait_ge(shifted, 1)
                nc.scalar.activation(exped[:], exped[:], ACT.Exp).then_inc(exp_done, 1)

            @block.vector
            def _(dve):
                normed.open(dve)
                with dve.Fori(0, PAIRS) as b:
                    for s in (0, 1):
                        g = b * 2 + s
                        transposed.wait(dve, g - 2)
                        copied.wait(dve, g - 2)
                        for k in range(GT):
                            op = normalize_tile(nc, S, xn[:, s, k * P:(k + 1) * P], g * GT + k)
                        op.then_inc(normed.sem, 1)
                    for s in (0, 1):
                        g = b * 2 + s
                        normed.wait(dve, g)
                        for k in range(GT):
                            op = nc.vector.bn_stats(st[:, cols((g * GT + k) * 6, 6)], xn[:, s, k * P:(k + 1) * P])
                        op.then_inc(bn, 1)
                        dve.wait_ge(bn, g + 1)
                c = Chain(dve, chain)
                stats_tail(nc, dve, c, st, tmp, S.mean2, S.rstd2, var_ready, std_ready)
                l_mm.wait(dve, GROUPS - 1)
                nc.vector.memset(ones[:], 1.0)
                c.run(nc.vector.tensor_tensor(by_tile(logits[:]), by_tile(ps[:, L, 0:W]), per_expert(S.f1_br[:]),
                                              ALU.add))
                softmax_start(nc, dve, c, by_tile(logits[:]), mx[:], exped[:]).then_inc(shifted, 1)
                dve.wait_ge(exp_done, 1)
                softmax_end(nc, c, exped[:], total[:], gates[:])
                pick_largest(nc, S, c, gates[:], mx[:], work[:], best[:], S.gate[:])
                nc.vector.tensor_copy(mask[:], best[:]).then_inc(masked, 1)
                dve.wait_ge(counted, 1)
                running_counts(nc, S, c, ps[:, C, :], totals[:], summed[:], cum[:])
                count = summed[:].rearrange("p (e t) -> p e t", e=E)[:, :, TILES - 1]
                c.run(nc.vector.tensor_tensor(work[:], cum[:], best[:], ALU.mult))
                nc.vector.tensor_reduce(rank[:], by_tile(work[:]), AX.X, ALU.add)
                c.run(nc.vector.tensor_tensor(filled[:], bcast(count, TILES),
                                              S.tile_start[:, 0:TILES].rearrange("p (o k) -> p o k", o=1)
                                              .broadcast_to([P, E, TILES]), ALU.is_gt))
                c.run(nc.vector.tensor_reduce(tiles_of[:], filled[:], AX.X, ALU.add))
                c.run(nc.vector.tensor_tensor_scan(base[:], ones[:], tiles_of[:], 0.0, ALU.mult, ALU.add))
                c.run(nc.vector.tensor_tensor(base[:], base[:], tiles_of[:], ALU.subtract))
                c.run(nc.vector.tensor_scalar(base[:], base[:], float(P), None, ALU.mult))
                c.run(nc.vector.tensor_tensor(by_tile(work[:]), by_tile(best[:]), per_expert(base[:]), ALU.mult))
                c.run(nc.vector.tensor_reduce(slot_f[:], by_tile(work[:]), AX.X, ALU.add))
                c.run(nc.vector.scalar_tensor_tensor(slot_f[:], slot_f[:], -1.0, rank[:], ALU.add, ALU.add))
                nc.vector.tensor_copy(S.slot[:], slot_f[:])
                c.run(nc.vector.tensor_tensor(reached[:], bcast(S.tile_start[:], E - 1),
                                              base[:, 1:E].rearrange("p (o e) -> p o e", o=1)
                                              .broadcast_to([P, SLOT_TILES, E - 1]), ALU.is_ge))
                c.run(nc.vector.tensor_reduce(expert_f[:], reached[:], AX.X, ALU.add))
                nc.vector.tensor_copy(S.tile_expert[:], expert_f[:])


def expert_tiles(nc, S):
    ctx, sb, sem, steps = scope(nc)
    ps = S.ps
    F = 4 * P
    FC = F // P
    TURNS = SLOT_TILES // 4
    XB, HB, TB, YB = (0, 1), (2, 3), (4, 5), (6, 7)
    with ctx:
        xs = sb("xs", [P, 4, P])
        xsT = sb("xsT", [P, 2, P])
        h = sb("h", [P, 2, F])
        hT = sb("hT", [P, 2, F])
        y = sb("y", [P, 2, P])
        back = sb("back", [P, TOK])
        normed_twice, scattered, x_ready = sem("normed_twice"), sem("scattered"), sem("x_ready")
        gathered = [sem(f"gathered{g}") for g in range(GROUPS)]
        loaded = [sem(f"loaded{n}") for n in range(4)]
        stored = [sem("stored0"), sem("stored1")]
        x_mm, xT_ready, h_mm, h_ready, hT_mm, hT_ready, y_mm, y_ready = [steps(n) for n in (
            "x_mm xT_ready h_mm h_ready hT_mm hT_ready y_mm y_ready").split()]
        with nc.Block() as block:
            @block.gpsimd
            def _(pool):
                for t in range(TILES):
                    pool.wait_ge(normed_twice, t + 1)
                    nc.gpsimd.indirect_dma_start(
                        S.x_slots[:, :], bass.IndirectOffsetOnAxis(ap=S.slot[:, t:t + 1], axis=0),
                        S.normed[:, t * P:(t + 1) * P], None).then_inc(scattered, 16)
                pool.wait_ge(scattered, 16 * TILES)

            @block.sync
            def _(sp):
                sp.wait_ge(scattered, 16 * TILES)

                def load(j, n):
                    for s in (0, 1):
                        sp.dma_start(xs[:, 2 * n + s, :], S.x_slots[bass.ds((j * 4 + (2 * n + s)) * P, P), :]
                                     ).then_inc(loaded[2 * n + s], 16)

                def store(j, n):
                    for s in (0, 1):
                        t = j * 4 + (2 * n + s)
                        y_ready.wait(sp, t)
                        sp.dma_start(S.y_slots[bass.ds(t * P, P), :], y[:, s, :]).then_inc(stored[s], 16)

                load(0, 0)
                load(0, 1)
                with sp.Fori(0, TURNS - 1) as j:
                    for n in (0, 1):
                        x_mm.wait(sp, j * 4 + (2 * n + 1))
                        load(j + 1, n)
                        store(j, n)
                for n in (0, 1):
                    store(TURNS - 1, n)
                for s in (0, 1):
                    sp.wait_ge(stored[s], 16 * SLOT_TILES // 2)

            def pairs(eng, step):
                step((0, 0), None)
                step((0, 1), (0, 0))
                with eng.Fori(1, TURNS) as j:
                    step((j, 0), (j - 1, 1))
                    step((j, 1), (j, 0))
                step(None, (TURNS - 1, 1))

            def tiles(pair):
                j, n = pair
                return [(j * 4 + (2 * n + s), s) for s in (0, 1)]

            def experts(eng, pair):
                return [eng.value_load(S.tile_expert[0:1, bass.ds(t, 1)], min_val=0, max_val=E - 1)
                        for t, s in tiles(pair)]

            @block.tensor
            def _(pe):
                for s in (x_mm, h_mm, hT_mm, y_mm):
                    s.open(pe)

                def step(front, back):
                    if front:
                        j, n = front
                        e = experts(pe, front)
                        for t, s in tiles(front):
                            pe.wait_ge(loaded[2 * n + s], j * 16 + 16)
                            xT_ready.wait(pe, t - 2)
                            nc.tensor.transpose(ps[:, XB[s], 0:P], xs[:, 2 * n + s, :], S.ident[:]).then_inc(x_mm.sem, 1)
                    if back:
                        for t, s in tiles(back):
                            h_ready.wait(pe, t)
                            hT_ready.wait(pe, t - 2)
                            for f in range(FC):
                                op = nc.tensor.transpose(ps[:, TB[s], f * P:(f + 1) * P], h[:, s, f * P:(f + 1) * P],
                                                         S.ident[:])
                            op.then_inc(hT_mm.sem, 1)
                    if front:
                        for t, s in tiles(front):
                            xT_ready.wait(pe, t)
                            h_ready.wait(pe, t - 2)
                            nc.tensor.matmul(ps[:, HB[s], :], xsT[:, s, :], S.f1_w1[:, cols(e[s] * F, F)], start=True,
                                             stop=True).then_inc(h_mm.sem, 1)
                    if back:
                        e = experts(pe, back)
                        for t, s in tiles(back):
                            hT_ready.wait(pe, t)
                            y_ready.wait(pe, t - 2)
                            for f in range(FC):
                                op = nc.tensor.matmul(ps[:, YB[s], 0:P], hT[:, s, f * P:(f + 1) * P],
                                                      S.f1_w2[:, cols(e[s] * F + f * P, P)], start=(f == 0),
                                                      stop=(f == FC - 1))
                            op.then_inc(y_mm.sem, 1)

                pairs(pe, step)

            @block.scalar
            def _(act):
                xT_ready.open(act)
                hT_ready.open(act)

                def step(front, back):
                    if front:
                        for t, s in tiles(front):
                            x_mm.wait(act, t)
                            h_mm.wait(act, t - 2)
                            nc.scalar.activation(xsT[:, s, :], ps[:, XB[s], 0:P], ACT.Identity, bias=S.f1_lnb[:],
                                                 scale=S.f1_lng[:]).then_inc(xT_ready.sem, 1)
                    if back:
                        for t, s in tiles(back):
                            hT_mm.wait(act, t)
                            y_mm.wait(act, t - 2)
                            nc.scalar.activation(hT[:, s, :], ps[:, TB[s], :], ACT.Relu).then_inc(hT_ready.sem, 1)

                pairs(act, step)

            @block.vector
            def _(dve):
                h_ready.open(dve)
                y_ready.open(dve)
                for t in range(TILES):
                    v = S.normed[:, t * P:(t + 1) * P]
                    nc.vector.tensor_scalar(v, v, S.mean2[:, t:t + 1], S.rstd2[:, t:t + 1], ALU.subtract,
                                            ALU.mult).then_inc(normed_twice, 1)

                def step(front, back):
                    if front:
                        e = experts(dve, front)
                        for t, s in tiles(front):
                            h_mm.wait(dve, t)
                            hT_mm.wait(dve, t - 2)
                            nc.vector.tensor_tensor(h[:, s, :], ps[:, HB[s], :], S.f1_b1[:, cols(e[s] * F, F)],
                                                    ALU.add).then_inc(h_ready.sem, 1)
                    if back:
                        j, n = back
                        e = experts(dve, back)
                        for t, s in tiles(back):
                            y_mm.wait(dve, t)
                            if not (isinstance(j, int) and j + n == 0):
                                dve.wait_ge(stored[s], (j * 2 + n) * 16)
                            nc.vector.tensor_tensor(y[:, s, :], ps[:, YB[s], 0:P], S.f1_b2[:, cols(e[s] * P, P)],
                                                    ALU.add).then_inc(y_ready.sem, 1)

                pairs(dve, step)
        with nc.Block() as block:
            @block.gpsimd
            def _(pool):
                for t in range(TILES):
                    nc.gpsimd.indirect_dma_start(
                        back[:, t * P:(t + 1) * P], None, S.y_slots[:, :],
                        bass.IndirectOffsetOnAxis(ap=S.slot[:, t:t + 1], axis=0)).then_inc(gathered[t // GT], 16)

            @block.vector
            def _(dve):
                for g in range(GROUPS):
                    dve.wait_ge(gathered[g], 16 * GT)
                    for t in range(g * GT, (g + 1) * GT):
                        x = S.x[:, t * P:(t + 1) * P]
                        op = nc.vector.scalar_tensor_tensor(x, back[:, t * P:(t + 1) * P], S.gate[:, t:t + 1], x,
                                                            ALU.mult, ALU.add)
                    op.then_inc(x_ready, 1)
                    dve.wait_ge(x_ready, g + 1)
                    group_stats(nc, S, g)


def best_expert_ffn(nc, S):
    ctx, sb, sem, steps = scope(nc)
    with ctx:
        S.normed = sb("normed", [P, TOK])
        S.mean2, S.rstd2 = sb("mean2", [P, TILES]), sb("rstd2", [P, TILES])
        S.gate = sb("gate", [P, TILES])
        S.slot = sb("slot", [P, TILES], I32)
        S.tile_expert = sb("tile_expert", [P, SLOT_TILES], I32)
        route_best(nc, S)
        expert_tiles(nc, S)


def program(nc, a, out):
    S = Shared()
    with ExitStack() as ctx:
        loads = []

        def sb(name, shape, dt=F32):
            return ctx.enter_context(nc.sbuf_tensor(name, shape, dt))

        def weight(name, shape, src=None):
            t = sb("w_" + name, shape)
            loads.append((t[:], a[name] if src is None else src))
            return t

        def column(name):
            return weight(name + "_col", [P, 1], a[name].rearrange("(p o) -> p o", o=1))

        def row(name, times=1):
            n = a[name].shape[0]
            t = sb("w_" + name + "_row", [P, times * n])
            for i in range(times):
                loads.append((t[:, i * n:(i + 1) * n], a[name].partition_broadcast(P)))
            return t

        S.ps = ctx.enter_context(nc.psum_tensor("ps", [P, 8, 512], F32))
        S.x = sb("x_res", [P, TOK])
        loads.append((S.x[:].rearrange("p (t d) -> p t d", d=D), a["x"].rearrange("(t p) d -> p t d", p=P)))
        S.st = sb("tile_stats", [P, TILES * 6])
        S.mean, S.rstd = sb("mean", [P, TILES]), sb("rstd", [P, TILES])
        S.eps, S.act_warm = sb("eps", [P, 1]), sb("act_warm", [P, 1])
        S.ident, S.ident_b = sb("ident", [P, P]), sb("ident_b", [P, P], BF16)
        S.head_mask = sb("head_mask", [P, P])
        S.prefix, S.ones_b = sb("prefix", [P, P], BF16), sb("ones_b", [P, P], BF16)
        S.mask_qk, S.mask_kq = sb("mask_qk", [P, P], BF16), sb("mask_kq", [P, P], BF16)
        S.first_rank, S.carry_on = sb("first_rank", [P, E]), sb("carry_on", [P, E * TILES])
        S.tile_start = sb("tile_start", [P, SLOT_TILES])

        S.a0_wq, S.a0_wkv, S.a0_wc = weight("a0_wqT", [P, D]), weight("a0_wkvT", [P, 2 * D]), weight("a0_wcT", [P, D])
        S.a0_bq, S.a0_bkv, S.a0_bc = column("a0_bq"), row("a0_bkv", 2), row("a0_bc", GT)
        S.a0_bq1 = sb("a0_bq1", [P, 1])
        first_loads = len(loads)

        S.f0_wr, S.f0_wg = weight("f0_wrT", [P, E]), weight("f0_wgT", [P, 2 * P])
        S.f0_wd = sb("f0_wd", [P, 2, E * D])
        loads.append((S.f0_wd[:], a["f0_wdT"].rearrange("(f p) n -> p f n", p=P)))

        S.b0_wq, S.b0_wk, S.b0_wv = weight("b0_wqT", [P, D]), weight("b0_wkT", [P, D]), weight("b0_wvT", [P, D])
        S.b0_bq, S.b0_bk, S.b0_bv = column("b0_bq"), column("b0_bk"), row("b0_bv", GT)
        S.b0_wo, S.b0_bo = weight("b0_woT", [P, D]), row("b0_bo", GT)

        S.a1_wq, S.a1_bq, S.a1_wkl = weight("a1_wq", [P, D]), column("a1_bq"), a["a1_wkl"]
        S.a1_bkl, S.a1_wc = weight("a1_bkl", [LATENT, H]), weight("a1_wcT", [LATENT, HD])
        S.a1_wk2, S.a1_bk2 = sb("a1_wk2", [P, P]), sb("a1_bk2", [P, 1])
        S.a1_wv, S.a1_bv = weight("a1_wv", [P, H * LATENT]), row("a1_bv")
        S.a1_wo = sb("a1_wo", [P, H * LATENT // P, D])
        loads.append((S.a1_wo[:], a["a1_wo"].rearrange("(f p) n -> p f n", p=P)))
        S.a1_bo = row("a1_bo", GT)
        S.b1_wq, S.b1_wk, S.b1_wv = weight("b1_wqT", [P, D]), weight("b1_wkT", [P, D]), weight("b1_wvT", [P, D])
        S.b1_bq, S.b1_bk, S.b1_bv = column("b1_bq"), column("b1_bk"), row("b1_bv", GT)
        S.b1_wo, S.b1_bo = weight("b1_woT", [P, D]), row("b1_bo", GT)
        S.f1_wr, S.f1_br = weight("f1_wr", [P, E]), row("f1_br")
        S.f1_lng, S.f1_lnb = column("f1_lng"), column("f1_lnb")
        S.f1_w1, S.f1_b1 = weight("f1_w1", [P, E * 4 * P]), row("f1_b1")
        S.f1_w2, S.f1_b2 = weight("f1_w2", [P, E * 4 * P]), row("f1_b2")
        S.zeros = sb("zeros", [P, D])

        S.x_slots = nc.dram_tensor("x_slots", [SLOT_TILES * P, D], F32)
        S.y_slots = nc.dram_tensor("y_slots", [SLOT_TILES * P, D], F32)
        S.q_parts = nc.dram_tensor("q_parts", [BATCH, PARTS, H, HD, SEQ], BF16)
        S.k_parts = nc.dram_tensor("k_parts", [BATCH, PARTS, H, HD, SEQ], BF16)
        S.v_heads = nc.dram_tensor("v_heads", [HEADS, P, LATENT * SEQ // P], F32)
        S.o_quads = nc.dram_tensor("o_quads", [HEADS, P, GROUP], F32)
        S.o_wide = nc.dram_tensor("o_wide", [HEADS, LATENT + 1, SEQ], F32)
        S.r_wide = nc.dram_tensor("r_wide", [2, HEADS, PARTS, GROUP], BF16)
        S.r_sums = nc.dram_tensor("r_sums", [HEADS, 2, GROUP], F32)

        S.late_loads = loads[first_loads:]
        load_phase(nc, S, loads[:first_loads])
        with nc.Block() as block:
            @block.vector
            def _(dve):
                nc.vector.tensor_scalar(S.a0_bq1[:], S.a0_bq[:], 1.0, None, ALU.add)
                nc.vector.memset(S.eps[:], EPS)
                for t in range(TILES):
                    tile_stats(nc, S, t)
        layers = (linear_attention, routed_pair_ffn, full_attention, routed_pair_ffn,
                  causal_attention, best_expert_ffn, row_attention, best_expert_ffn)
        for layer in layers:
            norm_stats(nc, S)
            layer(nc, S)
        store_phase(nc, S, out)


SLOT_TILES = 40


def arrays_of(i):
    import numpy as np

    def T(w):
        return np.ascontiguousarray(w.T)

    g = {k: np.asarray(v) for k, v in i.items()}
    w_in = g["L1_attn_b_w_in"].reshape(H, PARTS, HD, D)
    b_in = g["L1_attn_b_b_in"].reshape(H, PARTS, HD)
    return {
        **{f"b1_w{c}T": T(w_in[:, n].reshape(D, D)) for n, c in enumerate("qkv")},
        **{f"b1_b{c}": b_in[:, n].reshape(D) for n, c in enumerate("qkv")},
        "b1_woT": T(g["L1_attn_b_w_out"]),
        "b1_bo": g["L1_attn_b_b_out"],
        "a1_wq": g["L1_attn_a_Wq"],
        "a1_bq": g["L1_attn_a_bq"],
        "a1_wkl": g["L1_attn_a_Wk"].reshape(D, H, LATENT).transpose(2, 1, 0).reshape(LATENT, H * D),
        "a1_bkl": T(g["L1_attn_a_bk"].reshape(H, LATENT)),
        "a1_wcT": T(g["L1_attn_a_Wc"]),
        "a1_wv": g["L1_attn_a_Wv"],
        "a1_bv": g["L1_attn_a_bv"],
        "a1_wo": g["L1_attn_a_Wo"],
        "a1_bo": g["L1_attn_a_bo"],
        "f1_wr": g["L1_ffn_Wr"],
        "f1_br": g["L1_ffn_br"],
        "f1_lng": g["L1_ffn_ln_g"],
        "f1_lnb": g["L1_ffn_ln_b"],
        "f1_w1": g["L1_ffn_W1"].transpose(1, 0, 2).reshape(D, E * 4 * P),
        "f1_b1": g["L1_ffn_b1"].reshape(E * 4 * P),
        "f1_w2": g["L1_ffn_W2"].reshape(E, 4, P, D).transpose(2, 0, 1, 3).reshape(P, E * 4 * D),
        "f1_b2": g["L1_ffn_b2"].reshape(E * D),
        "x": g["L0_attn_a_x"].reshape(TOK, D),
        "a0_wqT": T(g["L0_attn_a_Wq"]),
        "a0_wkvT": np.concatenate([T(g["L0_attn_a_Wk"]), T(g["L0_attn_a_Wv"])], axis=1),
        "a0_bkv": np.concatenate([g["L0_attn_a_bk"], g["L0_attn_a_bv"]]),
        "a0_bq": g["L0_attn_a_bq"],
        "a0_wcT": T(g["L0_attn_a_Wc"]),
        "a0_bc": g["L0_attn_a_bc"],
        **{f"b0_w{c}T": T(g[f"L0_attn_b_W{c}"]) for c in "qkvo"},
        **{f"b0_b{c}": g[f"L0_attn_b_b{c}"] for c in "qkvo"},
        "f0_wrT": T(g["L0_ffn_w_router"]),
        "f0_wgT": T(g["L0_ffn_w_gate"]),
        "f0_wdT": np.ascontiguousarray(g["L0_ffn_w_down"].transpose(2, 0, 1)).reshape(2 * P, E * D),
    }


def kernel(**inputs):
    import numpy as np
    import concourse.bacc as bacc
    from concourse.bass_utils import run_bass_kernel_spmd

    nc = bacc.Bacc("TRN2", target_bir_lowering=False, num_devices=1)
    arrays = {f"in_{k}": v for k, v in arrays_of(inputs).items()}
    a = {k[3:]: nc.dram_tensor(k, v.shape, mybir.dt.from_np(v.dtype), kind="ExternalInput").ap()
         for k, v in arrays.items()}
    out = nc.dram_tensor("out", (BATCH, SEQ, D), F32, kind="ExternalOutput").ap()
    program(nc, a, out)
    r = run_bass_kernel_spmd(nc, [arrays], core_ids=[0])
    return r.results[0]["out"]
```
